# Optimizing a Trainium2 kernel written in Bass

```python
import numpy as np
import jax
import jax.numpy as jnp

def _softmax(x, axis=-1):
    return jax.nn.softmax(x, axis=axis)

def _gelu(x):
    return jax.nn.gelu(x, approximate=True)

def _silu(x):
    return jax.nn.silu(x)

def _sigmoid(x):
    return jax.nn.sigmoid(x)

def _layernorm(x, axis=-1, eps=1e-05):
    m = jnp.mean(x, axis=axis, keepdims=True)
    v = jnp.var(x, axis=axis, keepdims=True)
    return (x - m) / jnp.sqrt(v + eps)

def _scatter_add(tgt, idx, src, axis=0):
    return tgt.at[idx].add(src)

def _segment_sum(src, seg, n):
    return jax.ops.segment_sum(src, seg, n)
kernel_name = 'mk_metaformer_d4_conv_nchw256_r4_7619d2'

def setup_inputs(seed: int=0):
    np.random.seed(seed)
    _w = jnp.asarray

    def _rec_inputs():
        import jax
        import jax.numpy as jnp
        _gk = jax.random.key(seed)
        x = -9.26e-05 + 0.9999 * jax.random.normal(jax.random.fold_in(_gk, 1), (16, 64, 24, 24), jnp.float32)
        return x
    x = _rec_inputs()

    def _L0_conv_setup():
        import jax, jax.numpy as jnp
        import numpy as np
        ITERN = 5

        def _covpool(x):
            B, C, h, w = x.shape
            M = h * w
            xr = x.reshape(B, C, M)
            xc = xr - jnp.mean(xr, axis=-1, keepdims=True)
            return jnp.einsum('bcm,bdm->bcd', xc, xr) / M

        def _sqrtm_ns(cov, iterN):
            B, C, _ = cov.shape
            I3 = 3.0 * jnp.eye(C, dtype=cov.dtype)
            normA = jnp.trace(cov, axis1=1, axis2=2)[:, None, None]
            A = cov / normA
            ZY = 0.5 * (I3 - A)
            Y = jnp.einsum('bij,bjk->bik', A, ZY)
            Z = ZY
            for _ in range(1, iterN - 1):
                ZY = 0.5 * (I3 - jnp.einsum('bij,bjk->bik', Z, Y))
                Y = jnp.einsum('bij,bjk->bik', Y, ZY)
                Z = jnp.einsum('bij,bjk->bik', ZY, Z)
            ZY = 0.5 * jnp.einsum('bij,bjk->bik', Y, I3 - jnp.einsum('bij,bjk->bik', Z, Y))
            return ZY * jnp.sqrt(normA)
        key = jax.random.key(seed)
        k1, k2, k3 = jax.random.split(key, 3)
        B, C, H, W = (16, 64, 24, 24)
        r = 8
        x = jax.random.normal(k1, (B, C, H, W), dtype=jnp.float32)
        w1 = jax.random.normal(k2, (C // r, C), dtype=jnp.float32) * (1.0 / np.sqrt(C))
        b1 = jnp.zeros((C // r,), dtype=jnp.float32)
        w2 = jax.random.normal(k3, (C, C // r), dtype=jnp.float32) * (1.0 / np.sqrt(C // r))
        b2 = jnp.zeros((C,), dtype=jnp.float32)
        return {'x': x, 'w1': w1, 'b1': b1, 'w2': w2, 'b2': b2}
    _L0_conv_all = _L0_conv_setup()
    _L0_conv_in = {k: v for k, v in _L0_conv_all.items() if k in ('w1', 'b1', 'w2', 'b2')}
    del _L0_conv_all

    def _L0_ffn_setup():
        import jax, jax.numpy as jnp
        import numpy as np
        B, T, D, H, E = (16, 1024, 64, 128, 8)
        key = jax.random.key(seed)
        ks = jax.random.split(key, 5)
        x = jax.random.normal(ks[0], (B, T, D), dtype=jnp.float32)
        gate_w = jax.random.normal(ks[1], (D, E), dtype=jnp.float32) * 0.02
        gate_b = jnp.zeros((E,), dtype=jnp.float32)
        W1 = jax.random.normal(ks[2], (E, D, H), dtype=jnp.float32) * 0.02
        b1 = jnp.zeros((E, H), dtype=jnp.float32)
        W2 = jax.random.normal(ks[3], (E, H, D), dtype=jnp.float32) * 0.02
        b2 = jnp.zeros((E, D), dtype=jnp.float32)
        return {'x': x, 'gate_w': gate_w, 'gate_b': gate_b, 'W1': W1, 'b1': b1, 'W2': W2, 'b2': b2}
    _L0_ffn_all = _L0_ffn_setup()
    _L0_ffn_in = {k: v for k, v in _L0_ffn_all.items() if k in ('gate_w', 'gate_b', 'W1', 'b1', 'W2', 'b2')}
    del _L0_ffn_all

    def _L1_conv_setup():
        import jax, jax.numpy as jnp
        import numpy as np
        K = 2
        LAMBDA_ALPHA = 1.0
        LAMBDA_BETA = 0.5
        key = jax.random.key(seed)
        k1, k2, k3, k4, k5 = jax.random.split(key, 5)
        bs, C, H, W = (32, 64, 16, 16)
        R = 8
        hid = C // R
        x = jax.random.normal(k1, (bs, C, H, W), dtype=jnp.float32)
        w1 = jax.random.normal(k2, (hid, C), dtype=jnp.float32) * 0.05
        b1 = jnp.zeros((hid,), dtype=jnp.float32)
        w2 = jax.random.normal(k3, (K, 2 * C, hid), dtype=jnp.float32) * 0.05
        b2 = jax.random.normal(k4, (K, 2 * C), dtype=jnp.float32) * 0.05
        return {'x': x, 'w1': w1, 'b1': b1, 'w2': w2, 'b2': b2}
    _L1_conv_all = _L1_conv_setup()
    _L1_conv_in = {k: v for k, v in _L1_conv_all.items() if k in ('w1', 'b1', 'w2', 'b2')}
    del _L1_conv_all

    def _L1_ffn_setup():
        import jax, jax.numpy as jnp
        import numpy as np
        TOP_K = 2
        LN_EPS = 1e-05
        key = jax.random.key(seed)
        ks = jax.random.split(key, 8)
        B, S, D, E, H = (16, 256, 64, 8, 256)
        x = jax.random.normal(ks[0], (B, S, D), dtype=jnp.float32)
        Wr = jax.random.normal(ks[1], (D, E), dtype=jnp.float32) * 0.1
        br = jnp.zeros((E,), dtype=jnp.float32)
        ln_g = jnp.ones((E, D), dtype=jnp.float32)
        ln_b = jnp.zeros((E, D), dtype=jnp.float32)
        W1 = jax.random.normal(ks[2], (E, D, H), dtype=jnp.float32) * (1.0 / np.sqrt(D))
        b1 = jnp.zeros((E, H), dtype=jnp.float32)
        W2 = jax.random.normal(ks[3], (E, H, D), dtype=jnp.float32) * (1.0 / np.sqrt(H))
        b2 = jnp.zeros((E, D), dtype=jnp.float32)
        return {'x': x, 'Wr': Wr, 'br': br, 'ln_g': ln_g, 'ln_b': ln_b, 'W1': W1, 'b1': b1, 'W2': W2, 'b2': b2}
    _L1_ffn_all = _L1_ffn_setup()
    _L1_ffn_in = {k: v for k, v in _L1_ffn_all.items() if k in ('Wr', 'br', 'ln_g', 'ln_b', 'W1', 'b1', 'W2', 'b2')}
    del _L1_ffn_all

    def _L2_conv_setup():
        import jax, jax.numpy as jnp
        import numpy as np
        IN_PLANES = 64
        B, C, H, W = (16, 64, 56, 56)
        key = jax.random.key(seed)
        k_x, k1, k2, k3, k4 = jax.random.split(key, 5)
        x = jax.random.normal(k_x, (B, C, H, W), dtype=jnp.float32)
        w1 = jax.random.normal(k1, (C // 2, C), dtype=jnp.float32) * (1.0 / np.sqrt(C))
        w2 = jax.random.normal(k2, (C, C // 2), dtype=jnp.float32) * (1.0 / np.sqrt(C // 2))
        w_enc = jax.random.normal(k3, (1, C), dtype=jnp.float32) * (1.0 / np.sqrt(C))
        b_enc = jax.random.normal(k4, (1,), dtype=jnp.float32) * 0.01
        return {'x': x, 'w1': w1, 'w2': w2, 'w_enc': w_enc, 'b_enc': b_enc}
    _L2_conv_all = _L2_conv_setup()
    _L2_conv_in = {k: v for k, v in _L2_conv_all.items() if k in ('w1', 'w2', 'w_enc', 'b_enc')}
    del _L2_conv_all

    def _L2_ffn_setup():
        import jax, jax.numpy as jnp
        import numpy as np
        N_EXPERTS = 8
        TOP_K = 2
        key = jax.random.key(seed)
        ks = jax.random.split(key, 5)
        B, T, C, E, H = (8, 512, 64, 8, 682)
        scale = 1.0 / np.sqrt(C)
        return {'x': jax.random.normal(ks[0], (B, T, C), dtype=jnp.float32), 'router_w': jax.random.normal(ks[1], (E, C), dtype=jnp.float32) * scale, 'w1': jax.random.normal(ks[2], (E, H, C), dtype=jnp.float32) * scale, 'w2': jax.random.normal(ks[3], (E, C, H), dtype=jnp.float32) * (1.0 / np.sqrt(H)), 'w3': jax.random.normal(ks[4], (E, H, C), dtype=jnp.float32) * scale}
    _L2_ffn_all = _L2_ffn_setup()
    _L2_ffn_in = {k: v for k, v in _L2_ffn_all.items() if k in ('router_w', 'w1', 'w2', 'w3')}
    del _L2_ffn_all

    def _L3_conv_setup():
        import jax, jax.numpy as jnp
        import numpy as np
        from jax import lax
        key = jax.random.key(seed)
        k1, k2, k3 = jax.random.split(key, 3)
        N, C, H, W = (16, 64, 32, 32)
        KH = KW = 3
        x = jax.random.normal(k1, (N, C, H, W), dtype=jnp.float32)
        weight = jax.random.normal(k2, (C, 1, KH, KW), dtype=jnp.float32) * (1.0 / 3.0)
        bias = jax.random.normal(k3, (C,), dtype=jnp.float32) * 0.01
        return {'x': x, 'weight': weight, 'bias': bias}
    _L3_conv_all = _L3_conv_setup()
    _L3_conv_in = {k: v for k, v in _L3_conv_all.items() if k in ('weight', 'bias')}
    del _L3_conv_all

    def _L3_ffn_setup():
        import jax, jax.numpy as jnp
        import numpy as np
        N_EXPERTS = 8
        TOP_K = 2
        key = jax.random.key(seed)
        ks = jax.random.split(key, 5)
        B, T, C, E, H = (8, 512, 64, 8, 682)
        scale = 1.0 / np.sqrt(C)
        return {'x': jax.random.normal(ks[0], (B, T, C), dtype=jnp.float32), 'router_w': jax.random.normal(ks[1], (E, C), dtype=jnp.float32) * scale, 'w1': jax.random.normal(ks[2], (E, H, C), dtype=jnp.float32) * scale, 'w2': jax.random.normal(ks[3], (E, C, H), dtype=jnp.float32) * (1.0 / np.sqrt(H)), 'w3': jax.random.normal(ks[4], (E, H, C), dtype=jnp.float32) * scale}
    _L3_ffn_all = _L3_ffn_setup()
    _L3_ffn_in = {k: v for k, v in _L3_ffn_all.items() if k in ('router_w', 'w1', 'w2', 'w3')}
    del _L3_ffn_all
    return {'x': x, 'L0_conv_w1': _L0_conv_in['w1'], 'L0_conv_b1': _L0_conv_in['b1'], 'L0_conv_w2': _L0_conv_in['w2'], 'L0_conv_b2': _L0_conv_in['b2'], 'L0_ffn_gate_w': _L0_ffn_in['gate_w'], 'L0_ffn_gate_b': _L0_ffn_in['gate_b'], 'L0_ffn_W1': _L0_ffn_in['W1'], 'L0_ffn_b1': _L0_ffn_in['b1'], 'L0_ffn_W2': _L0_ffn_in['W2'], 'L0_ffn_b2': _L0_ffn_in['b2'], 'L1_conv_w1': _L1_conv_in['w1'], 'L1_conv_b1': _L1_conv_in['b1'], 'L1_conv_w2': _L1_conv_in['w2'], 'L1_conv_b2': _L1_conv_in['b2'], 'L1_ffn_Wr': _L1_ffn_in['Wr'], 'L1_ffn_br': _L1_ffn_in['br'], 'L1_ffn_ln_g': _L1_ffn_in['ln_g'], 'L1_ffn_ln_b': _L1_ffn_in['ln_b'], 'L1_ffn_W1': _L1_ffn_in['W1'], 'L1_ffn_b1': _L1_ffn_in['b1'], 'L1_ffn_W2': _L1_ffn_in['W2'], 'L1_ffn_b2': _L1_ffn_in['b2'], 'L2_conv_w1': _L2_conv_in['w1'], 'L2_conv_w2': _L2_conv_in['w2'], 'L2_conv_w_enc': _L2_conv_in['w_enc'], 'L2_conv_b_enc': _L2_conv_in['b_enc'], 'L2_ffn_router_w': _L2_ffn_in['router_w'], 'L2_ffn_w1': _L2_ffn_in['w1'], 'L2_ffn_w2': _L2_ffn_in['w2'], 'L2_ffn_w3': _L2_ffn_in['w3'], 'L3_conv_weight': _L3_conv_in['weight'], 'L3_conv_bias': _L3_conv_in['bias'], 'L3_ffn_router_w': _L3_ffn_in['router_w'], 'L3_ffn_w1': _L3_ffn_in['w1'], 'L3_ffn_w2': _L3_ffn_in['w2'], 'L3_ffn_w3': _L3_ffn_in['w3']}

def reference(x, L0_conv_w1, L0_conv_b1, L0_conv_w2, L0_conv_b2, L0_ffn_gate_w, L0_ffn_gate_b, L0_ffn_W1, L0_ffn_b1, L0_ffn_W2, L0_ffn_b2, L1_conv_w1, L1_conv_b1, L1_conv_w2, L1_conv_b2, L1_ffn_Wr, L1_ffn_br, L1_ffn_ln_g, L1_ffn_ln_b, L1_ffn_W1, L1_ffn_b1, L1_ffn_W2, L1_ffn_b2, L2_conv_w1, L2_conv_w2, L2_conv_w_enc, L2_conv_b_enc, L2_ffn_router_w, L2_ffn_w1, L2_ffn_w2, L2_ffn_w3, L3_conv_weight, L3_conv_bias, L3_ffn_router_w, L3_ffn_w1, L3_ffn_w2, L3_ffn_w3):
    import jax
    import jax.numpy as jnp

    def _L0_conv_ref(x, w1, b1, w2, b2):
        import jax, jax.numpy as jnp
        import numpy as np
        ITERN = 5

        def _covpool(x):
            B, C, h, w = x.shape
            M = h * w
            xr = x.reshape(B, C, M)
            xc = xr - jnp.mean(xr, axis=-1, keepdims=True)
            return jnp.einsum('bcm,bdm->bcd', xc, xr) / M

        def _sqrtm_ns(cov, iterN):
            B, C, _ = cov.shape
            I3 = 3.0 * jnp.eye(C, dtype=cov.dtype)
            normA = jnp.trace(cov, axis1=1, axis2=2)[:, None, None]
            A = cov / normA
            ZY = 0.5 * (I3 - A)
            Y = jnp.einsum('bij,bjk->bik', A, ZY)
            Z = ZY
            for _ in range(1, iterN - 1):
                ZY = 0.5 * (I3 - jnp.einsum('bij,bjk->bik', Z, Y))
                Y = jnp.einsum('bij,bjk->bik', Y, ZY)
                Z = jnp.einsum('bij,bjk->bik', ZY, Z)
            ZY = 0.5 * jnp.einsum('bij,bjk->bik', Y, I3 - jnp.einsum('bij,bjk->bik', Z, Y))
            return ZY * jnp.sqrt(normA)
        cov = _covpool(x)
        cov_sqrt = _sqrtm_ns(cov, ITERN)
        cov_sum = jnp.mean(cov_sqrt, axis=1)
        h1 = jax.nn.relu(cov_sum @ w1.T + b1)
        gate = jax.nn.sigmoid(h1 @ w2.T + b2)
        return gate[:, :, None, None] * x

    def _L0_ffn_ref(x, gate_w, gate_b, W1, b1, W2, b2):
        import jax, jax.numpy as jnp
        import numpy as np
        B, T, D, H, E = (16, 1024, 64, 128, 8)
        Bb, Tt, Dd = x.shape
        Ee = gate_w.shape[1]
        xf = x.reshape(-1, Dd)
        N = xf.shape[0]
        logits = xf @ gate_w + gate_b
        probs = jax.nn.softmax(logits, axis=-1)
        top2_vals, top2_idx = jax.lax.top_k(probs, 2)
        cw = jnp.zeros((N, Ee), dtype=xf.dtype).at[jnp.arange(N)[:, None], top2_idx].add(top2_vals)

        def step(acc, params):
            w1, bb1, w2, bb2, we = params
            h = jax.nn.gelu(xf @ w1 + bb1, approximate=False)
            y = h @ w2 + bb2
            return (acc + we[:, None] * y, None)
        out, _ = jax.lax.scan(step, jnp.zeros_like(xf), (W1, b1, W2, b2, cw.T))
        return out.reshape(Bb, Tt, Dd)

    def _L1_conv_ref(x, w1, b1, w2, b2):
        import jax, jax.numpy as jnp
        import numpy as np
        K = 2
        LAMBDA_ALPHA = 1.0
        LAMBDA_BETA = 0.5
        pooled = x.mean(axis=(2, 3))
        h = jax.nn.relu(pooled @ w1.T + b1)
        delta = 2.0 * jax.nn.sigmoid(jnp.einsum('koh,bh->bko', w2, h) + b2[None]) - 1.0
        alpha = delta[..., 0::2]
        beta = delta[..., 1::2]
        init_alpha = jnp.array([1.0, 0.0], dtype=x.dtype)
        init_beta = jnp.array([1.0, 0.0], dtype=x.dtype)
        a = init_alpha[None, :, None] + LAMBDA_ALPHA * alpha
        b = init_beta[None, :, None] + LAMBDA_BETA * beta
        y = x[:, None] * a[..., None, None] + b[..., None, None]
        return jnp.max(y, axis=1)

    def _L1_ffn_ref(x, Wr, br, ln_g, ln_b, W1, b1, W2, b2):
        import jax, jax.numpy as jnp
        import numpy as np
        TOP_K = 2
        LN_EPS = 1e-05
        B, S, D = x.shape
        N = B * S
        xt = x.reshape(N, D)
        logits = xt @ Wr + br
        probs = jax.nn.softmax(logits, axis=-1)
        top_p, top_idx = jax.lax.top_k(probs, TOP_K)
        weights = top_p / top_p.sum(axis=-1, keepdims=True)
        mu = xt.mean(axis=-1, keepdims=True)
        var = ((xt - mu) ** 2).mean(axis=-1, keepdims=True)
        xn = (xt - mu) * jax.lax.rsqrt(var + LN_EPS)
        xe = xn[None, :, :] * ln_g[:, None, :] + ln_b[:, None, :]
        h = jax.nn.gelu(jnp.einsum('end,edh->enh', xe, W1) + b1[:, None, :], approximate=False)
        y = jnp.einsum('enh,ehd->end', h, W2) + b2[:, None, :]
        y_tok = jnp.transpose(y, (1, 0, 2))
        sel = jnp.take_along_axis(y_tok, top_idx[:, :, None], axis=1)
        out = (weights[:, :, None] * sel).sum(axis=1)
        return out.reshape(B, S, D)

    def _L2_conv_ref(x, w1, w2, w_enc, b_enc):
        import jax, jax.numpy as jnp
        import numpy as np
        IN_PLANES = 64
        B, C, H, W = (16, 64, 56, 56)
        x01 = x[:, :, 0::2, :] * 0.5
        x02 = x[:, :, 1::2, :] * 0.5
        x1 = x01[:, :, :, 0::2]
        x2 = x02[:, :, :, 0::2]
        x3 = x01[:, :, :, 1::2]
        x4 = x02[:, :, :, 1::2]
        x_LL = x1 + x2 + x3 + x4
        x_HL = -x1 - x2 + x3 + x4
        x_LH = -x1 + x2 - x3 + x4
        x_HH = x1 - x2 - x3 + x4
        bands = jnp.stack([x_LL, x_HL, x_LH, x_HH], axis=1)
        ori_y = bands.mean(axis=(3, 4))
        a1 = jax.nn.sigmoid(jnp.einsum('bkc,oc->bko', ori_y, w_enc) + b_enc)
        top_idx = jnp.argmax(a1[..., 0], axis=1)
        Q = jnp.take_along_axis(ori_y, top_idx[:, None, None], axis=1)
        y = jnp.maximum(ori_y - Q, 0.0).sum(axis=1)
        h = jnp.maximum(y @ w1.T, 0.0)
        s = jax.nn.sigmoid(h @ w2.T)
        return x * s[:, :, None, None]

    def _L2_ffn_ref(x, router_w, w1, w2, w3):
        import jax, jax.numpy as jnp
        import numpy as np
        N_EXPERTS = 8
        TOP_K = 2
        B, T, C = x.shape
        flat = x.reshape(-1, C)
        logits = flat @ router_w.T
        probs = jax.nn.softmax(logits, axis=-1)
        topk_probs, topk_idx = jax.lax.top_k(probs, TOP_K)
        topk_probs = topk_probs / (jnp.sum(topk_probs, axis=-1, keepdims=True) + 1e-09)
        onehot = jax.nn.one_hot(topk_idx, N_EXPERTS, dtype=flat.dtype)
        gates = jnp.einsum('nk,nke->ne', topk_probs, onehot)
        h1 = jnp.einsum('nc,ehc->neh', flat, w1)
        h3 = jnp.einsum('nc,ehc->neh', flat, w3)
        h = jax.nn.silu(h1) * h3
        y = jnp.einsum('neh,ech->nec', h, w2)
        out = jnp.einsum('ne,nec->nc', gates, y)
        return out.reshape(B, T, C)

    def _L3_conv_ref(x, weight, bias):
        import jax, jax.numpy as jnp
        import numpy as np
        from jax import lax
        C = x.shape[1]
        y = lax.conv_general_dilated(x, weight, window_strides=(1, 1), padding=((1, 1), (1, 1)), dimension_numbers=('NCHW', 'OIHW', 'NCHW'), feature_group_count=C)
        y = y + bias[None, :, None, None]
        return y.astype(jnp.float32)

    def _L3_ffn_ref(x, router_w, w1, w2, w3):
        import jax, jax.numpy as jnp
        import numpy as np
        N_EXPERTS = 8
        TOP_K = 2
        B, T, C = x.shape
        flat = x.reshape(-1, C)
        logits = flat @ router_w.T
        probs = jax.nn.softmax(logits, axis=-1)
        topk_probs, topk_idx = jax.lax.top_k(probs, TOP_K)
        topk_probs = topk_probs / (jnp.sum(topk_probs, axis=-1, keepdims=True) + 1e-09)
        onehot = jax.nn.one_hot(topk_idx, N_EXPERTS, dtype=flat.dtype)
        gates = jnp.einsum('nk,nke->ne', topk_probs, onehot)
        h1 = jnp.einsum('nc,ehc->neh', flat, w1)
        h3 = jnp.einsum('nc,ehc->neh', flat, w3)
        h = jax.nn.silu(h1) * h3
        y = jnp.einsum('neh,ech->nec', h, w2)
        out = jnp.einsum('ne,nec->nc', gates, y)
        return out.reshape(B, T, C)

    def _gn(v, G=32, eps=1e-05):
        B_, C_, H_, W_ = v.shape
        g = v.reshape(B_, G, C_ // G, H_, W_)
        m = jnp.mean(g, axis=(2, 3, 4), keepdims=True)
        s = jnp.var(g, axis=(2, 3, 4), keepdims=True)
        return ((g - m) / jnp.sqrt(s + eps)).reshape(v.shape)

    def _ln_c(v, eps=1e-06):
        m = jnp.mean(v, axis=1, keepdims=True)
        s = jnp.var(v, axis=1, keepdims=True)
        return (v - m) / jnp.sqrt(s + eps)

    def _ln_t(v, eps=1e-05):
        m = jnp.mean(v, axis=-1, keepdims=True)
        s = jnp.var(v, axis=-1, keepdims=True)
        return (v - m) / jnp.sqrt(s + eps)

    def _to_tokens(v):
        B_, C_, H_, W_ = v.shape
        return v.reshape(B_, C_, H_ * W_).transpose(0, 2, 1)

    def _from_tokens(t, like):
        B_, C_, H_, W_ = like.shape
        return t.transpose(0, 2, 1).reshape(B_, C_, H_, W_)
    x = x + _L0_conv_ref(_ln_c(x), L0_conv_w1, L0_conv_b1, L0_conv_w2, L0_conv_b2)
    t = _to_tokens(x)
    t = t + _L0_ffn_ref(_ln_t(t), L0_ffn_gate_w, L0_ffn_gate_b, L0_ffn_W1, L0_ffn_b1, L0_ffn_W2, L0_ffn_b2)
    x = _from_tokens(t, x)
    x = x + _L1_conv_ref(_ln_c(x), L1_conv_w1, L1_conv_b1, L1_conv_w2, L1_conv_b2)
    t = _to_tokens(x)
    t = t + _L1_ffn_ref(_ln_t(t), L1_ffn_Wr, L1_ffn_br, L1_ffn_ln_g, L1_ffn_ln_b, L1_ffn_W1, L1_ffn_b1, L1_ffn_W2, L1_ffn_b2)
    x = _from_tokens(t, x)
    x = x + _L2_conv_ref(_ln_c(x), L2_conv_w1, L2_conv_w2, L2_conv_w_enc, L2_conv_b_enc)
    t = _to_tokens(x)
    t = t + _L2_ffn_ref(_ln_t(t), L2_ffn_router_w, L2_ffn_w1, L2_ffn_w2, L2_ffn_w3)
    x = _from_tokens(t, x)
    x = x + _L3_conv_ref(_ln_c(x), L3_conv_weight, L3_conv_bias)
    t = _to_tokens(x)
    t = t + _L3_ffn_ref(_ln_t(t), L3_ffn_router_w, L3_ffn_w1, L3_ffn_w2, L3_ffn_w3)
    x = _from_tokens(t, x)
    return x

_drawn_inputs = setup_inputs


def setup_inputs(seed=0):
    import zlib

    import numpy as np

    out = dict(_drawn_inputs(seed))
    spreads = {'L0_conv_b1': (0.0, 0.613),
     'L0_conv_b2': (0.0, 0.1),
     'L0_ffn_gate_b': (0.0, 0.1),
     'L0_ffn_b1': (0.0, 0.8),
     'L0_ffn_b2': (0.0, 0.1),
     'L1_conv_b1': (0.0, 0.706),
     'L1_ffn_br': (0.0, 0.1),
     'L1_ffn_ln_g': (1.0, 0.2),
     'L1_ffn_ln_b': (0.0, 0.1),
     'L1_ffn_b1': (0.0, 0.1),
     'L1_ffn_b2': (0.0, 0.1)}
    factors = {'L0_conv_w1': 8.0,
     'L0_conv_w2': 5.041,
     'L0_ffn_W1': 5.299,
     'L0_ffn_W2': 4.575,
     'L1_conv_w1': 8.0,
     'L1_conv_w2': 5.755,
     'L2_conv_w1': 2.936,
     'L2_conv_w2': 2.685,
     'L2_conv_w_enc': 3.401,
     'L3_conv_bias': 8.0}
    for name, (base, spread) in spreads.items():
        noise = np.random.default_rng([zlib.crc32(name.encode()), seed]).standard_normal(out[name].shape)
        drawn = base * np.exp(spread * noise) if base else spread * noise
        out[name] = jnp.asarray(drawn.astype(out[name].dtype))
    for name, factor in factors.items():
        out[name] = (out[name] * factor).astype(out[name].dtype)
    return out
```

```python
import numpy as np
import concourse.bass as bass
from concourse import mybir
from contextlib import ExitStack

FP32 = mybir.dt.float32
FP16 = mybir.dt.float16
I32 = mybir.dt.int32
ALU = mybir.AluOpType
ACT = mybir.ActivationFunctionType
AX = mybir.AxisListType
ds = bass.ds

B, C, HW = 16, 64, 24
PIX = HW * HW
P = 128
HALVES = 2
HB = B // HALVES
QS = HB // 2
NTOK = HB * PIX
NT = NTOK // P
QT = NT // 2
E, TOPK = 8, 2
ROWS = 256
SUB = ROWS // P
UNROLL = 4
TILES = -(-((TOPK * NTOK + E * (ROWS - 1)) // ROWS) // UNROLL) * UNROLL
MAXE = -(-NTOK // ROWS)
WSCALE = 16.0
RW = 2 * C + 2
H0, H1, H2 = 128, 256, 682
CH = 114
NCH = 6
CH_AT = [c * CH for c in range(NCH - 1)] + [H2 - CH]
OVERLAP = NCH * CH - H2
TBANK = 4
TB = [(b * TBANK, min(QT, (b + 1) * TBANK)) for b in range(-(-QT // TBANK))]
EPS_C, EPS_T = 1e-6, 1e-5
BIG = 1e30

_K = {}
_at = 0
for _n, _w in (("ident", P), ("tri", P), ("blk", P), ("i2", C), ("haar", QT * QS * 4), ("ind", QT * QS),
               ("mask", 2), ("e8", E), ("k4", 4), ("tile", TILES), ("thr", MAXE)):
    _K[_n] = (_at, _w)
    _at += _w
KCOLS = _at


def constants():
    k = np.zeros((P, KCOLS), np.float32)
    p = np.arange(P)

    def put(name, a):
        k[:, _K[name][0]:_K[name][0] + _K[name][1]] = np.asarray(a, np.float32).reshape(-1, _K[name][1])
    put("ident", np.eye(P))
    put("tri", p[:, None] < p[None, :])
    put("blk", (p[:, None] // C) == (p[None, :] // C))
    put("i2", (p[:, None] % C) == np.arange(C)[None, :])
    tok = np.arange(QT)[None, :] * P + p[:, None]
    s, pix = tok // PIX, tok % PIX
    r, c = (pix // HW) % 2, pix % 2
    sr, sc = 2 * r - 1, 2 * c - 1
    sign = np.stack([np.ones_like(r), sc, sr, sr * sc], -1)
    own = s[:, :, None] == np.arange(QS)
    put("haar", own[:, :, :, None] * sign[:, :, None, :])
    put("ind", own)
    put("mask", np.stack([p < P // 2, p >= P // 2], -1))
    put("e8", (E - np.arange(E))[None])
    put("k4", (4 - np.arange(4))[None])
    put("tile", np.arange(TILES)[None])
    put("thr", (np.arange(MAXE) * ROWS)[None])
    return k


_S = {}
_at = 0
for _n, _w in (("c0w1", 16), ("c0w2", P), ("c0b1", 1), ("c0b2", 1), ("c1w1", 16), ("c1w2", 4 * P), ("c1b1", 1),
               ("c1b2", 4), ("c2w1", C), ("c2w2", P), ("c2we", 1), ("c2be", 1), ("c3w", 9), ("c3b", 1),
               ("r0", 16), ("r1", 16), ("r2", 16), ("r3", 16), ("rb0", E), ("rb1", E)):
    _S[_n] = (_at, _w)
    _at += _w
SCOLS = _at


class Turn:

    def __init__(self):
        self.n = {}

    def __call__(self, sem, by=1):
        self.n[id(sem)] = self.n.get(id(sem), 0) + by
        return self.n[id(sem)]


def program(nc, I, konst, out):
    ctx = ExitStack()
    with ctx:
        def sb(name, shape, dt=FP32):
            return ctx.enter_context(nc.sbuf_tensor(name, shape, dt))

        def sem(name):
            return ctx.enter_context(nc.semaphore(name))

        rows_d = [nc.dram_tensor(f"rows_{h}", [TILES * ROWS, RW // 2], I32).ap() for h in range(HALVES)]
        y_d = [nc.dram_tensor(f"y_{h}", [TILES * ROWS, C], FP32).ap() for h in range(HALVES)]

        K = sb("K", [P, KCOLS])
        S = sb("S", [P, SCOLS])
        x = [sb(f"x{h}", [P, NT, C]) for h in range(HALVES)]
        xn = sb("xn", [P, NT, C])
        tmp = sb("tmp", [P, NT, C])
        rowsb = [sb(f"rowsb{h}", [P, NT, RW], FP16) for h in range(HALVES)]
        w01 = sb("w01", [P, 2 * E * (H0 + H1)], FP16)
        wA = {0: w01[:, 0:E * H0], 1: w01[:, 2 * E * H0:2 * E * H0 + E * H1]}
        wB = {0: w01[:, E * H0:2 * E * H0], 1: w01[:, 2 * E * H0 + E * H1:]}
        wD = {0: sb("w0d", [P, E * C]), 1: sb("w1d", [P, E * 2 * C])}
        b1T = {0: sb("b1T0", [P, E]), 1: sb("b1T1", [P, 2 * E])}
        b2R = {0: sb("b2R0", [P, E * C]), 1: sb("b2R1", [P, E * C])}
        gA, gB = sb("gA", [P, E * NCH * CH], FP16), sb("gB", [P, E * NCH * CH], FP16)
        uA, uB = sb("uA", [P, E * NCH * CH], FP16), sb("uB", [P, E * NCH * CH], FP16)
        dT = sb("dT", [CH, E * NCH * C])
        STW = E * NCH * C
        stage = [sb(f"stage{i}", [P, STW]) for i in range(2)]
        lnT = sb("lnT", [P, 2 * E])
        id16, tri16, one16 = (sb(n, [P, P], FP16) for n in ("id16", "tri16", "one16"))
        onef = sb("onef", [P, 2])
        i15 = sb("i15", [P, C])
        wencb = sb("wencb", [P, P])
        st = sb("st", [P, 8, NT])
        lg, eq, k1, k2 = (sb(n, [P, NT, E]) for n in ("lg", "eq", "k1", "k2"))
        ex = sb("ex", [P, NT * E + NT])
        mt = sb("mt", [P, E * NT], FP16)
        incl = sb("incl", [P, E, NT])
        r8 = sb("r8", [P, 6, E])
        cmp_ = sb("cmp", [P, E * MAXE])
        eidf = sb("eidf", [1, TILES * E])
        eidr = sb("eidr", [1, TILES])
        eid = [sb(f"eid{h}", [1, TILES], I32) for h in range(HALVES)]
        pos = [sb(f"pos{h}", [P, TOPK, NT], I32) for h in range(HALVES)]
        gts = [sb(f"gts{h}", [P, TOPK, NT]) for h in range(HALVES)]
        mx = sb("mx", [P, 2, 4, C])
        srow = sb("srow", [1, 2, HB * C])
        nsA, nsY, nsZ, nsW = (sb(n, [P, QS, C]) for n in ("nsA", "nsY", "nsZ", "nsW"))
        sm = sb("sm", [P, 64])
        hid = sb("hid", [P, QS])
        gate = sb("gate", [P, QS])
        par = sb("par", [P, 4, QS])
        gx = sb("gx", [P, 4 * QS * C])
        xs = [sb(f"xs{i}", [P, SUB * RW], FP16) for i in range(UNROLL)]
        xT = [sb(f"xT{i}", [P, ROWS], FP16) for i in range(UNROLL)]
        gt = [sb(f"gt{i}", [P, SUB]) for i in range(UNROLL)]
        act = [sb(f"act{i}", [P, 2 * ROWS]) for i in range(2)]
        hb = [sb(f"hb{i}", [P, 2 * ROWS]) for i in range(2)]
        yb = [sb(f"yb{i}", [P, SUB * C]) for i in range(UNROLL)]
        ysb = [sb(f"ysb{i}", [P, SUB * C]) for i in range(UNROLL)]
        PW = HW + 2
        pad = w01[:, 0:2 * QS * PW * PW].bitcast(FP32).rearrange("p (s a b) -> p s a b", s=QS, a=PW)
        PB = [ctx.enter_context(nc.psum_tensor(f"bank{i}", [P, 512], FP32)) for i in range(8)]

        def kc(name, rows=P):
            return K[0:rows, _K[name][0]:_K[name][0] + _K[name][1]]

        def sc(name, p0=0, p1=P):
            return S[p0:p1, _S[name][0]:_S[name][0] + _S[name][1]]

        ident = kc("ident")

        names = ("const_ld small_ld zeroed rows_zero x_ld dve_chain act_chain consts_done xin_ps xin_done centred squared "
                 "var_ready std_ready xn_ready mixed_ready sums_ps rows_ready cov_ps diag_ready tr_ps normv_ready "
                 "norm_root ns_ready ns_ps col_ps v_ready hid_ps hid_ready gate_ps gate_ready gain_ps applied "
                 "pool_ps pooled out4_ps out4_ready gate_wide par_ready band_ps band_ready z_ps z_ready t_ps t_done "
                 "split_hi logits_ps logit_shift exp_ready onehot_ready rank_ps route_ready first_sent second_gate second_sent "
                 "first_added second_added xT_ps xT_done h_ps s_ready hp_ready y_grp y_done "
                 "stage_ld0 stage_ld1 stage_used wt_ps w_hi w_lo conv_done res_ps out_ps out_ready stored "
                 "b_ld b_ps b_done l1b_ps w01_done pad_zero up_done").split()
        s = {n: sem(n) for n in names}
        xs_ld = [sem(f"xs_ld{i}") for i in range(UNROLL)]
        y_st = [sem(f"y_st{i}") for i in range(UNROLL)]

        block = ctx.enter_context(nc.Block())

        NL = 4
        G = [1, 1, 3, 3]
        order = [(l, h) for l in range(NL) for h in range(HALVES)]

        def n_of(l, h):
            return l * HALVES + h

        def group_base(l, h):
            return sum(G[a] * TILES for a, b in order[:n_of(l, h)])

        def tile_base(l, h):
            return n_of(l, h) * TILES

        LOOPS = TILES // UNROLL

        def pieces(q, s4):
            m = s4 // 2
            if s4 % 2 == 0:
                return [xn[:, 2 * (9 * m + t) + q, :] for t in range(4)] + [mx[:, 0, 2 * m + q, :]]
            return [mx[:, 1, 2 * m + q, :]] + [xn[:, 2 * (9 * m + 5 + t) + q, :] for t in range(4)]

        def pair(t, j):
            return t[:, 2 * j:2 * j + 2, :].rearrange("p q c -> p (q c)")

        def words(h):
            return rowsb[h][:, :, :].rearrange("p t c -> p (t c)").bitcast(I32)

        def gain_view(v):
            m, k = divmod(v, 3)
            t0 = 9 * m + (0, 4, 5)[k]
            return t0, t0 + (4, 1, 4)[k]

        NV = 6

        @block.sync
        def _(sp):
            turn = Turn()
            sp.dma_start(K[:, :], konst).then_inc(s["const_ld"], 16)
            for h in range(HALVES):
                for q in range(2):
                    b0 = h * HB + q * QS
                    dst = (xn, tmp)[h][q * C:(q + 1) * C, :, :].rearrange("p t c -> p (t c)").rearrange(
                        "p (s n) -> p s n", s=QS)
                    sp.dma_start(dst, I["x"][b0:b0 + QS].rearrange("s c a b -> c s (a b)")).then_inc(s["x_ld"], 16)
            for l in (0, 1):
                sp.dma_start(wD[l][:, :].rearrange("p (e k c) -> p e k c", e=E, c=C),
                             I[f"L{l}_ffn_W2"].rearrange("e (k p) c -> p e k c", p=P)).then_inc(s["b_ld"], 16)
                sp.dma_start(b2R[l][:, :], I[f"L{l}_ffn_b2"].rearrange("e c -> (e c)").partition_broadcast(P)
                             ).then_inc(s["b_ld"], 16)
            sp.dma_start(act[0][0:E, 0:P], I["L0_ffn_b1"]).then_inc(s["b_ld"], 16)
            sp.dma_start(act[1][0:2 * E, 0:P], I["L1_ffn_b1"].rearrange("e (k p) -> (e k) p", p=P)).then_inc(s["b_ld"], 16)
            for d in range(2):
                sp.dma_start(act[0][0:E, P + d * C:P + (d + 1) * C], I["L1_ffn_ln_g"]).then_inc(s["b_ld"], 16)
                sp.dma_start(act[1][0:E, P + d * C:P + (d + 1) * C], I["L1_ffn_ln_b"]).then_inc(s["b_ld"], 16)
            for l, w in ((0, H0), (1, H1)):
                for d in range(2):
                    sp.dma_start(stage[l][d * C:(d + 1) * C, 0:E * w].rearrange("p (e n) -> p e n", e=E),
                                 I[f"L{l}_ffn_W1"].rearrange("e d n -> d e n")).then_inc(s[f"stage_ld{l}"], 16)
            used = 0

            def load_stage(l):
                nonlocal used
                for k in range(4):
                    used += 1
                    sp.wait_ge(s["stage_used"], used)
                    if k < 2:
                        w = I[f"L{l}_ffn_{('w1', 'w3')[k]}"]
                        v = stage[k % 2][0:CH, :].rearrange("p (k e c) -> p k e c", k=NCH, e=E)
                        for c in range(NCH):
                            sp.dma_start(v[:, c], w[:, CH_AT[c]:CH_AT[c] + CH, :].rearrange("e p c -> p e c")
                                         ).then_inc(s[f"stage_ld{k % 2}"], 16)
                    else:
                        w = I[f"L{l}_ffn_w2"][4 * (k - 2):4 * (k - 1)]
                        sp.dma_start(stage[k % 2][0:C, 0:4 * H2].rearrange("p (e n) -> p e n", e=4),
                                     w.rearrange("e c n -> c e n")).then_inc(s[f"stage_ld{k % 2}"], 16)
            load_stage(2)

            def moe(l, h):
                n, tb = n_of(l, h), tile_base(l, h)

                def load(t, i, k):
                    if tb + k + t >= UNROLL or not isinstance(i, int):
                        sp.wait_ge(s["xT_done"], i * UNROLL + (tb + k + t - UNROLL + 1))
                    sp.dma_start(xs[k][:, :].bitcast(I32), rows_d[h][ds((i * UNROLL + (k + t)) * ROWS, ROWS), :].rearrange(
                        "(p s) c -> p (s c)", s=SUB)).then_inc(xs_ld[k], 16)

                def store(i, k):
                    sp.wait_ge(s["y_done"], i * UNROLL + (tb + k + 1))
                    sp.dma_start(y_d[h][ds((i * UNROLL + k) * ROWS, ROWS), :].rearrange(
                        "(p s) c -> p (s c)", s=SUB), ysb[k][:, :]).then_inc(y_st[k], 16)
                sp.wait_ge(s["first_sent"], 16 * NT * (n + 1))
                sp.wait_ge(s["second_sent"], 16 * NT * (n + 1))
                for k in range(UNROLL):
                    load(0, 0, k)
                with sp.Fori(0, LOOPS - 1) as i:
                    for k in range(UNROLL):
                        load(UNROLL, i, k)
                        store(i, k)
                for k in range(UNROLL):
                    store(LOOPS - 1, k)

            for l in range(NL):
                if l == 3:
                    load_stage(3)
                for h in range(HALVES):
                    moe(l, h)
            for h in range(HALVES):
                for q in range(2):
                    b0 = h * HB + q * QS
                    sp.wait_ge(s["out_ready"], h + 1)
                    src = (xn, tmp)[h][q * C:(q + 1) * C, :, :].rearrange("p t c -> p (t c)").rearrange(
                        "p (s n) -> p s n", s=QS)
                    sp.dma_start(out[b0:b0 + QS].rearrange("s c a b -> c s (a b)"), src).then_inc(s["stored"], 16)
            sp.wait_ge(s["stored"], 16 * 2 * HALVES)

        @block.gpsimd
        def _(pool):
            pool.memset(S[:, :], 0.0).then_inc(s["zeroed"], 1)
            pool.memset(rowsb[0][:, :, :], 0.0).then_inc(s["rows_zero"], 1)
            pool.wait_ge(s["rows_zero"], 1)
            for h in range(HALVES):
                flat = rows_d[h].rearrange("(p r) c -> p (r c)", p=P)
                per = TILES * ROWS // P * (RW // 2)
                for a in range(0, per, NT * RW // 2):
                    w = min(NT * RW // 2, per - a)
                    pool.dma_start(flat[:, a:a + w], words(0)[:, 0:w]).then_inc(s["up_done"], 16)
            nz = HALVES * -(-(TILES * ROWS // P * RW) // (NT * RW))
            pool.wait_ge(s["up_done"], 16 * nz)
            pool.memset(onef[:, :], 1.0).then_inc(s["rows_zero"], 1)

            def scatter(l, h):
                n = n_of(l, h)
                pool.wait_ge(s["route_ready"], n + 1)
                for j in range(NT):
                    pool.indirect_dma_start(rows_d[h], bass.IndirectOffsetOnAxis(pos[h][:, 0, j:j + 1], 0),
                                            words(h)[:, j * RW // 2:(j + 1) * RW // 2], None).then_inc(s["first_sent"], 16)
                pool.wait_ge(s["second_gate"], n + 1)
                for j in range(NT):
                    pool.indirect_dma_start(rows_d[h], bass.IndirectOffsetOnAxis(pos[h][:, 1, j:j + 1], 0),
                                            words(h)[:, j * RW // 2:(j + 1) * RW // 2], None).then_inc(s["second_sent"], 16)

            def gather(l, h):
                n = n_of(l, h)
                for k in range(UNROLL):
                    pool.wait_ge(y_st[k], 16 * LOOPS * (n + 1))
                for j in range(NT):
                    pool.indirect_dma_start(x[h][:, j, :], None, y_d[h], bass.IndirectOffsetOnAxis(pos[h][:, 0, j:j + 1], 0),
                                            compute_op=ALU.add).then_inc(s["first_added"], 16)
                pool.wait_ge(s["first_added"], 16 * NT * (n + 1))
                for j in range(NT):
                    pool.indirect_dma_start(x[h][:, j, :], None, y_d[h], bass.IndirectOffsetOnAxis(pos[h][:, 1, j:j + 1], 0),
                                            compute_op=ALU.add).then_inc(s["second_added"], 16)
            for l in range(NL):
                for h in range(HALVES):
                    scatter(l, h)
                for h in range(HALVES):
                    gather(l, h)

        @block.scalar
        def _(a):
            turn = Turn()

            def ln():
                a.wait_ge(s["centred"], turn(s["centred"]))
                a.activation(tmp[:, :, :], xn[:, :, :], ACT.Square).then_inc(s["squared"], 1)
                a.wait_ge(s["var_ready"], turn(s["var_ready"]))
                a.activation(st[:, 3, :], st[:, 2, :], ACT.Sqrt).then_inc(s["std_ready"], 1)

            def gate_tail(hr, b1, b2, w):
                a.wait_ge(s["hid_ps"], turn(s["hid_ps"]))
                if b1 is None:
                    a.activation(hid[0:hr, :], PB[4][0:hr, 0:QS], ACT.Relu).then_inc(s["hid_ready"], 1)
                else:
                    a.activation(hid[0:hr, :], PB[4][0:hr, 0:QS], ACT.Relu, bias=b1[0:hr, :]).then_inc(s["hid_ready"], 1)
                a.wait_ge(s["gate_ps"], turn(s["gate_ps"]))
                if b2 is None:
                    a.activation(gate[:, :], PB[5][:, 0:QS], ACT.Sigmoid).then_inc(s["gate_ready"], 1)
                else:
                    a.activation(gate[:, :], PB[5][:, 0:QS], ACT.Sigmoid, bias=b2).then_inc(s["gate_ready"], 1)

            def conv(l):
                if l == 0:
                    a.wait_ge(s["normv_ready"], turn(s["normv_ready"]))
                    a.activation(sm[:, 12:16], sm[:, 8:12], ACT.Sqrt).then_inc(s["norm_root"], 1)
                    gate_tail(16, sc("c0b1"), sc("c0b2"), None)
                elif l == 1:
                    a.wait_ge(s["hid_ps"], turn(s["hid_ps"]))
                    a.activation(hid[0:16, :], PB[4][0:16, 0:QS], ACT.Relu, bias=sc("c1b1")[0:16, :]).then_inc(s["hid_ready"], 1)
                    a.wait_ge(s["out4_ps"], turn(s["out4_ps"]))
                    for k in range(4):
                        ins = a.activation(par[:, k, :], PB[5][:, k * QS:(k + 1) * QS], ACT.Sigmoid,
                                           bias=sc("c1b2")[:, k:k + 1])
                    ins.then_inc(s["out4_ready"], 1)
                elif l == 2:
                    a.wait_ge(s["z_ps"], turn(s["z_ps"]))
                    a.activation(sm[:, 16:32], PB[1][:, 0:16], ACT.Sigmoid, bias=sc("c2be")).then_inc(s["z_ready"], 1)
                    gate_tail(C, None, None, None)

            def prep(l, h):
                ln()
                conv(l)
                ln()
                a.wait_ge(s["xn_ready"], 2 * (n_of(l, h) + 1))
                a.activation(rowsb[h][:, :, 0:C], xn[:, :, :], ACT.Copy).then_inc(s["split_hi"], 1)
                a.wait_ge(s["logit_shift"], turn(s["logit_shift"]))
                a.activation(ex[:, :], ex[:, :], ACT.Exp).then_inc(s["exp_ready"], 1)

            def wprep():
                for k in range(2):
                    for b in range(12):
                        a.wait_ge(s["wt_ps"], turn(s["wt_ps"]))
                        dst = (gA, uA)[k][:, b * 4 * CH:(b + 1) * 4 * CH]
                        a.activation(dst, PB[b % 4][:, 0:4 * CH], ACT.Copy, scale=WSCALE).then_inc(s["w_hi"], 1)
                turn(s["wt_ps"], 6)

            def moe(l, h):
                n, tb, gb = n_of(l, h), tile_base(l, h), group_base(l, h)
                with a.Fori(0, LOOPS) as i:
                    for k in range(UNROLL):
                        if l < 2:
                            e = a.value_load(eid[h][0:1, ds(i * UNROLL + k, 1)], min_val=0, max_val=E - 1)
                        for g in range(G[l]):
                            q = k * G[l] + g
                            v = i * (UNROLL * G[l]) + (gb + q)
                            a.wait_ge(s["h_ps"], v + 1)
                            if l < 2:
                                if gb or q >= 2:
                                    a.wait_ge(s["y_grp"], v - 1)
                                else:
                                    a.wait_ge(s["y_grp"], i * (UNROLL * G[l]))
                                for c in range(l + 1):
                                    ins = a.activation(hb[q % 2][:, c * ROWS:(c + 1) * ROWS], PB[q % 2][:, c * ROWS:(c + 1) * ROWS],
                                                       ACT.Gelu, scale=1.0 / WSCALE, bias=b1T[l][:, ds(e * (l + 1) + c, 1)])
                                ins.then_inc(s["hp_ready"], 1)
                            else:
                                a.wait_ge(s["hp_ready"], v - 1)
                                a.activation(act[q % 2][0:CH, :], PB[q % 2][0:CH, :], ACT.Silu, scale=1.0 / WSCALE
                                             ).then_inc(s["s_ready"], 1)

            a.wait_ge(s["zeroed"], 1)
            small = []
            for q in range(2):
                cq, hq = slice(q * C, (q + 1) * C), slice(q * 8, (q + 1) * 8)
                small += [
                    (sc("c0w1")[cq, hq], I["L0_conv_w1"].rearrange("o c -> c o")),
                    (sc("c0w2")[hq, cq], I["L0_conv_w2"].rearrange("c o -> o c")),
                    (sc("c0b1")[hq, :], I["L0_conv_b1"].rearrange("(c o) -> c o", o=1)),
                    (sc("c0b2")[cq, :], I["L0_conv_b2"].rearrange("(c o) -> c o", o=1)),
                    (sc("c1w1")[cq, hq], I["L1_conv_w1"].rearrange("o c -> c o")),
                    (sc("c1b1")[hq, :], I["L1_conv_b1"].rearrange("(c o) -> c o", o=1)),
                    (sc("c1b2")[cq, :].rearrange("p (k t) -> p k t", k=2), I["L1_conv_b2"].rearrange("k (c t) -> c k t", t=2)),
                    (sc("c2w1")[cq, q * 32:(q + 1) * 32], I["L2_conv_w1"].rearrange("o c -> c o")),
                    (sc("c2w2")[q * 32:(q + 1) * 32, cq], I["L2_conv_w2"].rearrange("c o -> o c")),
                    (sc("c2we")[cq, :], I["L2_conv_w_enc"].rearrange("o c -> c o")),
                    (sc("c3w")[cq, :], I["L3_conv_weight"].rearrange("c o a b -> c (o a b)")),
                    (sc("c3b")[cq, :], I["L3_conv_bias"].rearrange("(c o) -> c o", o=1)),
                    (sc("r0")[cq, hq], I["L0_ffn_gate_w"]),
                    (sc("r1")[cq, hq], I["L1_ffn_Wr"]),
                    (sc("r2")[cq, hq], I["L2_ffn_router_w"].rearrange("e c -> c e")),
                    (sc("r3")[cq, hq], I["L3_ffn_router_w"].rearrange("e c -> c e")),
                ]
                for k in range(2):
                    for t in range(2):
                        v = sc("c1w2")[hq, (2 * k + t) * P + q * C:(2 * k + t) * P + (q + 1) * C]
                        small.append((v, I["L1_conv_w2"][k].rearrange("(c t) h -> t h c", t=2)[t]))
            small.append((sc("c2be"), I["L2_conv_b_enc"].partition_broadcast(P)))
            small.append((sc("rb0"), I["L0_ffn_gate_b"].partition_broadcast(P)))
            small.append((sc("rb1"), I["L1_ffn_br"].partition_broadcast(P)))
            for dst, src in small:
                a.dma_start(dst, src, allow_slow_non_contiguous=True).then_inc(s["small_ld"], 16)
            for l, w in ((0, H0), (1, H1)):
                a.wait_ge(s["w01_done"], 1 + l)
                a.activation(wA[l][:, :], stage[l][:, 0:E * w], ACT.Copy, scale=WSCALE).then_inc(s["w_hi"], 1)
            for l in range(NL):
                for h in range(HALVES):
                    prep(l, h)
                if l in (0, 3):
                    wprep()
                for h in range(HALVES):
                    moe(l, h)

        @block.vector
        def _(v):
            turn = Turn()

            def link(ins):
                ins.then_inc(s["dve_chain"], 1)
                v.wait_ge(s["dve_chain"], turn(s["dve_chain"]))

            def bc(ap, m):
                return ap.unsqueeze(2).broadcast_to([ap.shape[0], ap.shape[1], m])

            def bt(ap, m):
                return ap.unsqueeze(1).broadcast_to([ap.shape[0], m, ap.shape[1]])

            def ln(xh, eps):
                link(v.tensor_reduce(st[:, 0, :], xh[:, :, :], AX.X, ALU.add))
                link(v.tensor_scalar(st[:, 1, :], st[:, 0, :], 1.0 / C, None, ALU.mult))
                v.tensor_tensor(xn[:, :, :], xh[:, :, :], bc(st[:, 1, :], C), ALU.subtract).then_inc(s["centred"], 1)
                v.wait_ge(s["squared"], turn(s["squared"]))
                link(v.tensor_reduce(st[:, 0, :], tmp[:, :, :], AX.X, ALU.add))
                v.tensor_scalar(st[:, 2, :], st[:, 0, :], 1.0 / C, eps, ALU.mult, ALU.add).then_inc(s["var_ready"], 1)
                v.wait_ge(s["std_ready"], turn(s["std_ready"]))
                link(v.reciprocal(st[:, 4, :], st[:, 3, :]))
                link(v.tensor_tensor(st[:, 5, :], st[:, 4, :], st[:, 4, :], ALU.mult))
                link(v.tensor_tensor(st[:, 5, :], st[:, 5, :], st[:, 2, :], ALU.mult))
                link(v.tensor_scalar(st[:, 5, :], st[:, 5, :], -0.5, 1.5, ALU.mult, ALU.add))
                link(v.tensor_tensor(st[:, 4, :], st[:, 4, :], st[:, 5, :], ALU.mult))
                v.tensor_tensor(xn[:, :, :], xn[:, :, :], bc(st[:, 4, :], C), ALU.mult).then_inc(s["xn_ready"], 1)
                v.wait_ge(s["xn_ready"], turn(s["xn_ready"]))

            def gained(dst, src, banks, kind, op):
                for k in range(NV):
                    t0, t1 = gain_view(k)
                    i = kind * NV + k
                    g = PB[banks[i // 4]][:, (i % 4) * P:(i % 4 + 1) * P]
                    g = g.unsqueeze(1).broadcast_to([P, t1 - t0, P])
                    d = dst[:, 2 * t0:2 * t1, :].rearrange("p (t q) c -> p t (q c)", q=2)
                    r = src[:, 2 * t0:2 * t1, :].rearrange("p (t q) c -> p t (q c)", q=2)
                    ins = v.tensor_tensor(d, r, g, op)
                link(ins)

            def apply_gate(xh):
                v.wait_ge(s["gate_ready"], turn(s["gate_ready"]))
                v.tensor_copy(gx[:, 0:QS * C].rearrange("p (k c) -> p k c", c=C), bc(gate[:, :], C)).then_inc(s["gate_wide"], 1)
                v.wait_ge(s["gain_ps"], turn(s["gain_ps"]))
                gained(tmp, xn, (6, 7), 0, ALU.mult)
                v.tensor_tensor(xh[:, :, :], xh[:, :, :], tmp[:, :, :], ALU.add).then_inc(s["applied"], 1)
                v.wait_ge(s["applied"], turn(s["applied"]))

            def conv0(xh, h):
                shared = xn[:, :, :].rearrange("p (m t) c -> p m t c", m=2)[:, :, 8:10, :]
                for m in range(2):
                    ins = v.tensor_scalar(mx[:, m, :, :].rearrange("p (m t) c -> p m t c", m=2), shared,
                                          kc("mask")[:, m:m + 1], None, ALU.mult)
                ins.then_inc(s["mixed_ready"], 1)
                v.wait_ge(s["sums_ps"], turn(s["sums_ps"]))
                link(v.tensor_copy(srow[:, 0, :], PB[0][0:1, 0:HB * C]))
                v.tensor_scalar(srow[:, 1, :], srow[:, 0, :], -1.0 / PIX, None, ALU.mult).then_inc(s["rows_ready"], 1)
                v.wait_ge(s["cov_ps"], turn(s["cov_ps"]))
                cov = PB[1][:, 0:QS * C].rearrange("p (s c) -> p s c", s=QS)
                link(v.tensor_tensor(nsW[:, :, :], cov, bt(kc("i2"), QS), ALU.mult))
                v.tensor_reduce(sm[:, 0:4], nsW[:, :, :], AX.X, ALU.add).then_inc(s["diag_ready"], 1)
                v.wait_ge(s["tr_ps"], turn(s["tr_ps"]))
                link(v.tensor_copy(sm[:, 0:4], PB[2][:, 0:QS]))
                link(v.reciprocal(sm[:, 4:8], sm[:, 0:4]))
                v.tensor_scalar(sm[:, 8:12], sm[:, 0:4], 1.0 / PIX, None, ALU.mult).then_inc(s["normv_ready"], 1)
                link(v.tensor_tensor(nsA[:, :, :], cov, bc(sm[:, 4:8], C), ALU.mult))
                v.scalar_tensor_tensor(nsZ[:, :, :], nsA[:, :, :], -0.5, bt(i15[:, :], QS), ALU.mult, ALU.add
                                       ).then_inc(s["ns_ready"], 1)
                yp, wp, zp = (PB[b][:, 0:QS * C].rearrange("p (s c) -> p s c", s=QS) for b in (3, 4, 5))
                v.wait_ge(s["ns_ps"], turn(s["ns_ps"]))
                v.tensor_copy(nsY[:, :, :], yp).then_inc(s["ns_ready"], 1)
                for it in range(4):
                    v.wait_ge(s["ns_ps"], turn(s["ns_ps"]))
                    v.scalar_tensor_tensor(nsW[:, :, :], wp, -0.5, bt(i15[:, :], QS), ALU.mult, ALU.add
                                           ).then_inc(s["ns_ready"], 1)
                    v.wait_ge(s["ns_ps"], turn(s["ns_ps"]))
                    if it < 3:
                        v.tensor_copy(nsZ[:, :, :], zp)
                    v.tensor_copy(nsY[:, :, :], yp).then_inc(s["ns_ready"], 1)
                v.wait_ge(s["norm_root"], turn(s["norm_root"]))
                link(v.reciprocal(sm[:, 16:20], sm[:, 12:16]))
                link(v.tensor_tensor(sm[:, 16:20], sm[:, 16:20], sm[:, 8:12], ALU.mult))
                link(v.tensor_tensor(sm[:, 16:20], sm[:, 16:20], sm[:, 12:16], ALU.add))
                v.wait_ge(s["col_ps"], turn(s["col_ps"]))
                v.scalar_tensor_tensor(sm[:, 20:24], PB[2][:, 0:QS], 0.5 / C, sm[:, 16:20], ALU.mult, ALU.mult
                                       ).then_inc(s["v_ready"], 1)
                apply_gate(xh)

            def conv1(xh, h):
                v.wait_ge(s["pool_ps"], turn(s["pool_ps"]))
                v.tensor_scalar(sm[:, 20:24], PB[0][:, 0:QS], 1.0 / PIX, None, ALU.mult).then_inc(s["v_ready"], 1)
                v.wait_ge(s["out4_ready"], turn(s["out4_ready"]))
                link(v.tensor_scalar(par[:, :, :], par[:, :, :], 2.0, -1.0, ALU.mult, ALU.add))
                link(v.tensor_scalar(par[:, 1:4:2, :], par[:, 1:4:2, :], 0.5, None, ALU.mult))
                link(v.tensor_scalar(par[:, 0:2, :], par[:, 0:2, :], 1.0, None, ALU.add))
                v.tensor_copy(gx[:, :].rearrange("p (k c) -> p k c", c=C),
                              bc(par[:, :, :].rearrange("p k s -> p (k s)"), C)).then_inc(s["par_ready"], 1)
                v.wait_ge(s["gain_ps"], turn(s["gain_ps"]))
                banks = (0, 1, 2, 3, 6, 7)
                gained(tmp, xn, banks, 0, ALU.mult)
                gained(tmp, tmp, banks, 1, ALU.add)
                gained(xn, xn, banks, 2, ALU.mult)
                gained(xn, xn, banks, 3, ALU.add)
                link(v.tensor_tensor(tmp[:, :, :], tmp[:, :, :], xn[:, :, :], ALU.max))
                v.tensor_tensor(xh[:, :, :], xh[:, :, :], tmp[:, :, :], ALU.add).then_inc(s["applied"], 1)
                v.wait_ge(s["applied"], turn(s["applied"]))

            def conv2(xh, h):
                v.wait_ge(s["band_ps"], turn(s["band_ps"]))
                ori = sm[:, 0:16]
                v.tensor_scalar(ori, PB[0][:, 0:16], 2.0 / PIX, None, ALU.mult).then_inc(s["band_ready"], 1)
                v.wait_ge(s["z_ready"], turn(s["z_ready"]))

                def sk(c):
                    return sm[:, c:c + 16].rearrange("p (s k) -> p s k", k=4)
                link(v.tensor_reduce(sm[:, 32:36], sk(16), AX.X, ALU.max))
                link(v.tensor_tensor(sk(36), sk(16), bc(sm[:, 32:36], 4), ALU.is_equal))
                link(v.tensor_tensor(sk(36), sk(36), bt(kc("k4"), QS), ALU.mult))
                link(v.tensor_reduce(sm[:, 32:36], sk(36), AX.X, ALU.max))
                link(v.tensor_tensor(sk(36), sk(36), bc(sm[:, 32:36], 4), ALU.is_equal))
                link(v.tensor_tensor(sk(36), sk(36), sk(0), ALU.mult))
                link(v.tensor_reduce(sm[:, 32:36], sk(36), AX.X, ALU.add))
                link(v.tensor_tensor(sk(36), sk(0), bc(sm[:, 32:36], 4), ALU.subtract))
                link(v.tensor_scalar(sm[:, 36:52], sm[:, 36:52], 0.0, None, ALU.max))
                v.tensor_reduce(sm[:, 20:24], sk(36), AX.X, ALU.add).then_inc(s["v_ready"], 1)
                apply_gate(xh)

            t_seen = [0]

            def t_count(k):
                t_seen[0] += k
                return t_seen[0]

            def tr_out(dst_flat):
                for b, (j0, j1) in enumerate(TB):
                    v.wait_ge(s["t_ps"], turn(s["t_ps"]))
                    v.tensor_copy(dst_flat[:, j0 * P:j1 * P], PB[b][:, 0:(j1 - j0) * P]).then_inc(s["t_done"], 1)

            def conv3(xh, h):
                flat = tmp[:, :, :].rearrange("p t c -> p (t c)")
                if h == 0:
                    link(v.memset(pad, 0.0))
                tr_out(flat)
                v.wait_ge(s["t_done"], t_count(len(TB)))
                link(v.tensor_copy(pad[:, :, 1:1 + HW, 1:1 + HW].rearrange("p s a b -> p s a b"),
                                   flat.rearrange("p (s a b) -> p s a b", s=QS, a=HW)))
                img = flat.rearrange("p (s a b) -> p s a b", s=QS, a=HW)
                for smp in range(QS):
                    for tap in range(9):
                        dy, dx = divmod(tap, 3)
                        win = pad[:, smp, dy:dy + HW, dx:dx + HW]
                        w = sc("c3w")[:, tap:tap + 1]
                        if tap == 0:
                            ins = v.tensor_scalar(img[:, smp], win, w, sc("c3b"), ALU.mult, ALU.add)
                        else:
                            ins = v.scalar_tensor_tensor(img[:, smp], win, w, img[:, smp], ALU.mult, ALU.add)
                        if smp < QS - 1 or tap < 8:
                            link(ins)
                ins.then_inc(s["conv_done"], 1)
                for b, (j0, j1) in enumerate(TB):
                    v.wait_ge(s["res_ps"], turn(s["res_ps"]))
                    xv = xh[:, 2 * j0:2 * j1, :].rearrange("p t c -> p (t c)")
                    pv = PB[b][:, 0:(j1 - j0) * P]
                    ins = v.tensor_tensor(xv, xv, pv, ALU.add)
                ins.then_inc(s["applied"], 1)
                v.wait_ge(s["applied"], turn(s["applied"]))

            def top(src, mask, m):
                link(v.tensor_tensor(eq[:, :, :], src, bc(m, E), ALU.is_equal))
                link(v.tensor_tensor(eq[:, :, :], eq[:, :, :], bt(kc("e8"), NT), ALU.mult))
                link(v.tensor_reduce(st[:, 7, :], eq[:, :, :], AX.X, ALU.max))
                link(v.tensor_tensor(mask[:, :, :], eq[:, :, :], bc(st[:, 7, :], E), ALU.is_equal))

            def route(l, h):
                flat = tmp[:, :, :].rearrange("p t c -> p (t c)")
                tr_out(flat)
                t_count(len(TB))
                v.wait_ge(s["split_hi"], turn(s["split_hi"]))
                v.tensor_tensor(rowsb[h][:, :, C:2 * C], xn[:, :, :], rowsb[h][:, :, 0:C], ALU.subtract)
                v.wait_ge(s["logits_ps"], turn(s["logits_ps"]))
                src = PB[5][:, 0:QT * 16].rearrange("p (t e) -> p t e", e=E)
                if l < 2:
                    link(v.tensor_tensor(lg[:, :, :], src, bt(sc(f"rb{l}"), NT), ALU.add))
                else:
                    link(v.tensor_copy(lg[:, :, :], src))
                m1, m2 = st[:, 0, :], st[:, 1, :]
                link(v.tensor_reduce(m1, lg[:, :, :], AX.X, ALU.max))
                top(lg[:, :, :], k1, m1)
                exv = ex[:, 0:NT * E].rearrange("p (t e) -> p t e", e=E)
                link(v.tensor_tensor(exv, lg[:, :, :], bc(m1, E), ALU.subtract))
                link(v.scalar_tensor_tensor(lg[:, :, :], k1[:, :, :], -BIG, lg[:, :, :], ALU.mult, ALU.add))
                link(v.tensor_reduce(m2, lg[:, :, :], AX.X, ALU.max))
                v.tensor_tensor(ex[:, NT * E:], m2, m1, ALU.subtract).then_inc(s["logit_shift"], 1)
                top(lg[:, :, :], k2, m2)
                v.tensor_tensor(mt[:, :].rearrange("p (e t) -> p t e", e=E), k1[:, :, :], k2[:, :, :], ALU.add
                                ).then_inc(s["onehot_ready"], 1)
                v.wait_ge(s["exp_ready"], turn(s["exp_ready"]))
                link(v.tensor_reduce(st[:, 2, :], exv, AX.X, ALU.add))
                link(v.reciprocal(gts[h][:, 0, :], st[:, 2, :]))
                link(v.tensor_tensor(gts[h][:, 1, :], gts[h][:, 0, :], ex[:, NT * E:], ALU.mult))
                if l > 0:
                    link(v.tensor_tensor(st[:, 2, :], gts[h][:, 0, :], gts[h][:, 1, :], ALU.add))
                    if l > 1:
                        link(v.tensor_scalar(st[:, 2, :], st[:, 2, :], 1e-9, None, ALU.add))
                    link(v.reciprocal(st[:, 3, :], st[:, 2, :]))
                    link(v.tensor_tensor(gts[h][:, :, :], gts[h][:, :, :], bt(st[:, 3, :], TOPK), ALU.mult))
                gcol = rowsb[h][:, :, :].rearrange("p t c -> p (t c)").bitcast(FP32).rearrange(
                    "p (t c) -> p t c", c=RW // 2)[:, :, RW // 2 - 1]
                link(v.tensor_copy(gcol, gts[h][:, 0, :]))
                v.wait_ge(s["rank_ps"], turn(s["rank_ps"]))
                rank = PB[6][:, 0:E * NT].rearrange("p (e t) -> p e t", e=E)
                cnt = PB[7][:, 0:E * NT].rearrange("p (e t) -> p e t", e=E)
                one = onef[:, 0:1]
                inf = incl[:, :, :].rearrange("p e t -> p (e t)")
                link(v.tensor_tensor_scan(inf, one.broadcast_to([P, E * NT]), PB[7][:, 0:E * NT], 0.0, ALU.mult, ALU.add))
                link(v.tensor_tensor(incl[:, :, :], incl[:, :, :], cnt, ALU.subtract))
                link(v.tensor_tensor(incl[:, :, :], incl[:, :, :], rank, ALU.add))
                link(v.tensor_reduce(r8[:, 0, :], cnt, AX.X, ALU.add))
                cv = cmp_[:, :].rearrange("p (e k) -> p e k", e=E)
                link(v.tensor_tensor(cv, bc(r8[:, 0, :], MAXE), bt(kc("thr"), E), ALU.is_gt))
                link(v.tensor_reduce(r8[:, 1, :], cv, AX.X, ALU.add))
                link(v.tensor_tensor_scan(r8[:, 2, :], one.broadcast_to([P, E]), r8[:, 1, :], 0.0, ALU.mult, ALU.add))
                link(v.tensor_tensor_scan(r8[:, 3, :], one.broadcast_to([P, E]), r8[:, 0, :], 0.0, ALU.mult, ALU.add))
                link(v.tensor_tensor(r8[:, 4, :], r8[:, 2, :], r8[:, 1, :], ALU.subtract))
                link(v.tensor_tensor(r8[:, 5, :], r8[:, 0, :], r8[:, 3, :], ALU.subtract))
                link(v.scalar_tensor_tensor(r8[:, 5, :], r8[:, 4, :], float(ROWS), r8[:, 5, :], ALU.mult, ALU.add))
                link(v.tensor_tensor(incl[:, :, :], incl[:, :, :], bc(r8[:, 5, :], NT), ALU.add))
                pv = incl[:, :, :].rearrange("p e t -> p t e")
                for k, m in enumerate((k1, k2)):
                    link(v.tensor_tensor(eq[:, :, :], m[:, :, :], pv, ALU.mult))
                    link(v.tensor_reduce(st[:, 2, :], eq[:, :, :], AX.X, ALU.add))
                    link(v.tensor_copy(pos[h][:, k, :], st[:, 2, :]))
                ev = eidf[:, :].rearrange("p (t e) -> p t e", e=E)
                link(v.tensor_tensor(ev, bt(r8[0:1, 2, :], TILES), bc(kc("tile", 1), E), ALU.is_le))
                link(v.tensor_reduce(eidr[:, :], ev, AX.X, ALU.add))
                link(v.tensor_scalar(eidr[:, :], eidr[:, :], float(E - 1), None, ALU.min))
                v.tensor_copy(eid[h][:, :], eidr[:, :]).then_inc(s["route_ready"], 1)
                v.wait_ge(s["first_sent"], 16 * NT * (n_of(l, h) + 1))
                v.tensor_copy(gcol, gts[h][:, 1, :]).then_inc(s["second_gate"], 1)

            def prep(l, h):
                if l > 0:
                    v.wait_ge(s["second_added"], 16 * NT * (n_of(l - 1, h) + 1))
                ln(x[h], EPS_C)
                (conv0, conv1, conv2, conv3)[l](x[h], h)
                ln(x[h], EPS_T)
                route(l, h)

            def wprep():
                for k in range(2):
                    for b in range(12):
                        v.wait_ge(s["w_hi"], turn(s["w_hi"]))
                        hi = (gA, uA)[k][:, b * 4 * CH:(b + 1) * 4 * CH]
                        lo = (gB, uB)[k][:, b * 4 * CH:(b + 1) * 4 * CH]
                        v.scalar_tensor_tensor(lo, PB[b % 4][:, 0:4 * CH], WSCALE, hi, ALU.mult, ALU.subtract
                                               ).then_inc(s["w_lo"], 1)
                for b in range(6):
                    v.wait_ge(s["wt_ps"], turn(s["wt_ps"], 24 + 1 if b == 0 else 1))
                    v.tensor_copy(dT[:, b * 512:(b + 1) * 512], PB[4 + b % 2][0:CH, :]).then_inc(s["w_lo"], 1)
                v.wait_ge(s["w_lo"], turn(s["w_lo"], 30))
                last = dT[0:OVERLAP, :].rearrange("p (e k c) -> p e k c", e=E, k=NCH)[:, :, NCH - 1, :]
                v.memset(last, 0.0).then_inc(s["w_lo"], 1)
                turn(s["w_lo"])

            def moe(l, h):
                n, tb, gb = n_of(l, h), tile_base(l, h), group_base(l, h)

                def evict(i, k, first=False):
                    t = i * UNROLL + (tb + k)
                    v.wait_ge(s["y_grp"], i * (UNROLL * G[l]) + (gb + (k + 1) * G[l]))
                    if n > 0:
                        v.wait_ge(y_st[k], i * 16 + 16 * LOOPS * n)
                    elif not isinstance(i, int):
                        v.wait_ge(y_st[k], i * 16)
                    elif i > 0:
                        v.wait_ge(y_st[k], i * 16)
                    src = PB[4 + k % 2]
                    if l < 2:
                        e = v.value_load(eid[h][0:1, ds(i * UNROLL + k, 1)], min_val=0, max_val=E - 1)
                        b2 = b2R[l][:, ds(e * C, C)]
                        for u in range(SUB):
                            ins = v.tensor_tensor(yb[k][:, u * C:(u + 1) * C], src[:, u * C:(u + 1) * C], b2, ALU.add)
                        ins.then_inc(s["b_done"], 1)
                        v.wait_ge(s["b_done"], i * UNROLL + (3 + tb + k + 1))
                        src, scale = yb[k], 1.0
                    else:
                        scale = 1.0 / WSCALE
                    for u in range(SUB):
                        ins = v.tensor_scalar(ysb[k][:, u * C:(u + 1) * C], src[:, u * C:(u + 1) * C], gt[k][:, u:u + 1],
                                              scale, ALU.mult, ALU.mult)
                    ins.then_inc(s["y_done"], 1)

                def take(i, k, t):
                    k2_ = (k + t) % UNROLL
                    w = i * UNROLL + (tb + k + t)
                    v.wait_ge(s["xT_ps"], w + 1)
                    gv = xs[k2_][:, :].bitcast(FP32).rearrange("p (s c) -> p s c", s=SUB)[:, :, RW // 2 - 1]
                    v.tensor_copy(gt[k2_][:, :], gv)
                    v.tensor_copy(xT[k2_][:, :], PB[6 + k2_ % 2][:, :].bitcast(FP16)[:, 0:ROWS]).then_inc(s["xT_done"], 1)

                def product(i, k, g):
                    if l < 2:
                        return
                    q = k * G[l] + g
                    w = i * (UNROLL * G[l]) + (gb + q)
                    v.wait_ge(s["s_ready"], i * (UNROLL * G[l]) + (gb + q + 1 - group_base(2, 0)))
                    v.wait_ge(s["y_grp"], w - 1)
                    v.tensor_tensor(hb[q % 2][0:CH, :], PB[2 + q % 2][0:CH, :], act[q % 2][0:CH, :], ALU.mult
                                    ).then_inc(s["hp_ready"], 1)

                def body(i, last=False, first=False):
                    for k in range(UNROLL):
                        product(i, k, 0)
                        if k > 0:
                            evict(i, k - 1)
                        elif not first:
                            evict(i - 1, UNROLL - 1)
                        if not (last and k + 2 >= UNROLL):
                            take(i, k, 2)
                        for g in range(1, G[l]):
                            product(i, k, g)
                take(0, 0, 0)
                take(0, 1, 0)
                body(0, first=True)
                with v.Fori(1, LOOPS - 1) as i:
                    body(i)
                body(LOOPS - 1, last=True)
                evict(LOOPS - 1, UNROLL - 1)

            v.wait_ge(s["const_ld"], 16)
            v.wait_ge(s["rows_zero"], 2)
            v.tensor_copy(id16[:, :], ident)
            v.tensor_copy(tri16[:, :], kc("tri"))
            v.memset(one16[:, :], 1.0)
            v.wait_ge(s["small_ld"], 16 * (2 * 20 + 3))
            v.tensor_scalar(wencb[:, :], kc("blk"), sc("c2we"), None, ALU.mult)
            v.tensor_scalar(i15[:, :], kc("i2"), 1.5, None, ALU.mult).then_inc(s["consts_done"], 1)
            for h in range(HALVES):
                for b, (j0, j1) in enumerate(TB):
                    v.wait_ge(s["xin_ps"], turn(s["xin_ps"]))
                    xv = x[h][:, 2 * j0:2 * j1, :].rearrange("p t c -> p (t c)")
                    v.tensor_copy(xv, PB[b][:, 0:(j1 - j0) * P]).then_inc(s["xin_done"], 1)
            v.wait_ge(s["xin_done"], turn(s["xin_done"], HALVES * len(TB)))
            v.wait_ge(s["b_ps"], 1)
            v.tensor_copy(b1T[0][:, :], PB[5][:, 0:E])
            link(v.tensor_copy(b1T[1][:, :], PB[5][:, 64:64 + 2 * E]))
            v.tensor_copy(lnT[:, :], PB[5][:, 128:128 + 2 * E]).then_inc(s["b_done"], 1)
            v.wait_ge(s["b_done"], 1)
            v.wait_ge(s["stage_ld0"], 32)
            v.tensor_scalar(lnT[:, 0:1], lnT[:, 0:1], 1.0, None, ALU.mult).then_inc(s["w01_done"], 1)
            v.wait_ge(s["w01_done"], 1)
            v.wait_ge(s["l1b_ps"], 1)
            v.tensor_tensor(b1T[1][:, :], b1T[1][:, :], PB[6][:, 0:2 * E], ALU.add).then_inc(s["b_done"], 1)
            for e in range(E):
                ins = v.tensor_scalar(stage[1][:, e * H1:(e + 1) * H1], stage[1][:, e * H1:(e + 1) * H1], lnT[:, e:e + 1],
                                      None, ALU.mult)
            ins.then_inc(s["w01_done"], 1)
            for l, w in ((0, H0), (1, H1)):
                v.wait_ge(s["w_hi"], turn(s["w_hi"]))
                v.scalar_tensor_tensor(wB[l][:, :], stage[l][:, 0:E * w], WSCALE, wA[l][:, :], ALU.mult, ALU.subtract
                                       ).then_inc(s["stage_used"], 1)
            v.wait_ge(s["b_ld"], 16 * 10)
            v.memset(yb[0][:, :], 0.0).then_inc(s["b_done"], 1)
            for l in range(NL):
                for h in range(HALVES):
                    prep(l, h)
                if l in (0, 3):
                    wprep()
                for h in range(HALVES):
                    moe(l, h)
            for h in range(HALVES):
                v.wait_ge(s["second_added"], 16 * NT * (n_of(NL - 1, h) + 1))
                flat = (xn, tmp)[h][:, :, :].rearrange("p t c -> p (t c)")
                tr_out(flat)
                v.wait_ge(s["t_done"], t_count(len(TB)))
                v.tensor_scalar(sm[:, 63:64], onef[:, 0:1], 1.0, None, ALU.mult).then_inc(s["out_ready"], 1)

        @block.tensor
        def _(pe):
            turn = Turn()

            def transposes(src, sem_ps, sem_done, wait_all):
                for b, (j0, j1) in enumerate(TB):
                    for j in range(j0, j1):
                        ins = pe.transpose(PB[b][:, (j - j0) * P:(j - j0 + 1) * P], src(j), ident)
                    ins.then_inc(sem_ps, 1)

            def conv0():
                pe.wait_ge(s["mixed_ready"], turn(s["mixed_ready"]))
                for smp in range(HB):
                    ops = pieces(*divmod(smp, QS))
                    for i, o in enumerate(ops):
                        ins = pe.matmul(PB[0][0:1, smp * C:(smp + 1) * C], onef[:, 0:1], o, start=(i == 0), stop=(i == 4))
                ins.then_inc(s["sums_ps"], 1)
                for smp in range(HB):
                    q, s4 = divmod(smp, QS)
                    ops = pieces(q, s4)
                    for i, o in enumerate(ops):
                        pe.matmul(PB[1][q * C:(q + 1) * C, s4 * C:(s4 + 1) * C], o, o, start=(i == 0 and s4 == 0),
                                  stop=False, skip_group_check=True)
                pe.wait_ge(s["rows_ready"], turn(s["rows_ready"]))
                for smp in range(HB):
                    q, s4 = divmod(smp, QS)
                    ins = pe.matmul(PB[1][q * C:(q + 1) * C, s4 * C:(s4 + 1) * C], srow[0:1, 1, smp * C:(smp + 1) * C],
                                    srow[0:1, 0, smp * C:(smp + 1) * C], start=False, stop=True, skip_group_check=True)
                ins.then_inc(s["cov_ps"], 1)
                pe.wait_ge(s["diag_ready"], turn(s["diag_ready"]))
                pe.matmul(PB[2][:, 0:QS], kc("blk"), sm[:, 0:4], start=True, stop=True).then_inc(s["tr_ps"], 1)

                def product(bank, a_, b_):
                    for s4 in range(QS):
                        for q in range(2):
                            r = slice(q * C, (q + 1) * C)
                            ins = pe.matmul(PB[bank][r, s4 * C:(s4 + 1) * C], a_[r, s4, :], b_[r, s4, :], start=True, stop=True)
                    return ins
                pe.wait_ge(s["ns_ready"], turn(s["ns_ready"]))
                product(3, nsA, nsZ).then_inc(s["ns_ps"], 1)
                for it in range(4):
                    pe.wait_ge(s["ns_ready"], turn(s["ns_ready"]))
                    product(4, nsZ, nsY).then_inc(s["ns_ps"], 1)
                    pe.wait_ge(s["ns_ready"], turn(s["ns_ready"]))
                    if it < 3:
                        product(5, nsW, nsZ)
                    product(3, nsY, nsW).then_inc(s["ns_ps"], 1)
                pe.wait_ge(s["ns_ready"], turn(s["ns_ready"]))
                for s4 in range(QS):
                    for q in range(2):
                        r = slice(q * C, (q + 1) * C)
                        ins = pe.matmul(PB[2][r, s4:s4 + 1], nsY[r, s4, :], onef[r, 0:1], start=True, stop=True)
                ins.then_inc(s["col_ps"], 1)
                gate_tail("c0", 16)

            def hidden(c, hr):
                pe.wait_ge(s["v_ready"], turn(s["v_ready"]))
                pe.matmul(PB[4][0:hr, 0:QS], sc(f"{c}w1"), sm[:, 20:24], start=True, stop=True).then_inc(s["hid_ps"], 1)
                pe.wait_ge(s["hid_ready"], turn(s["hid_ready"]))

            def spread(src, banks, kind):
                for k in range(NV):
                    m, part = divmod(k, 3)
                    if part == 1:
                        at = (kind * QS + 2 * m) * C
                        lhs = gx[:, at:at + P]
                    else:
                        c = 2 * m + part // 2
                        lhs = src[:, c:c + 1].broadcast_to([P, P])
                    i = kind * NV + k
                    ins = pe.matmul(PB[banks[i // 4]][:, (i % 4) * P:(i % 4 + 1) * P], lhs, ident, start=True, stop=True)
                return ins

            def gate_tail(c, hr):
                hidden(c, hr)
                pe.matmul(PB[5][:, 0:QS], sc(f"{c}w2", 0, hr), hid[0:hr, :], start=True, stop=True).then_inc(s["gate_ps"], 1)
                pe.wait_ge(s["gate_wide"], turn(s["gate_wide"]))
                spread(gate, (6, 7), 0).then_inc(s["gain_ps"], 1)

            def sums(cols, w):
                for j in range(QT):
                    ins = pe.matmul(PB[0][:, 0:w], pair(xn, j), kc(cols)[:, j * w:(j + 1) * w], start=(j == 0), stop=(j == QT - 1))
                return ins

            def conv1():
                sums("ind", QS).then_inc(s["pool_ps"], 1)
                hidden("c1", 16)
                for k in range(4):
                    ins = pe.matmul(PB[5][:, k * QS:(k + 1) * QS], sc("c1w2", 0, 16)[:, k * P:(k + 1) * P], hid[0:16, :],
                                    start=True, stop=True)
                ins.then_inc(s["out4_ps"], 1)
                pe.wait_ge(s["par_ready"], turn(s["par_ready"]))
                for k in range(4):
                    ins = spread(par[:, k, :], (0, 1, 2, 3, 6, 7), k)
                ins.then_inc(s["gain_ps"], 1)

            def conv2():
                sums("haar", QS * 4).then_inc(s["band_ps"], 1)
                pe.wait_ge(s["band_ready"], turn(s["band_ready"]))
                pe.matmul(PB[1][:, 0:16], wencb[:, :], sm[:, 0:16], start=True, stop=True).then_inc(s["z_ps"], 1)
                gate_tail("c2", C)

            def conv3():
                transposes(lambda j: pair(xn, j), s["t_ps"], None, None)
                pe.wait_ge(s["t_done"], turn(s["t_done"], len(TB)))
                pe.wait_ge(s["conv_done"], turn(s["conv_done"]))
                flat = tmp[:, :, :].rearrange("p t c -> p (t c)")
                transposes(lambda j: flat[:, j * P:(j + 1) * P], s["res_ps"], None, None)

            def route(l, h):
                pe.wait_ge(s["applied"], n_of(l, h) + 1)
                pe.wait_ge(s["xn_ready"], 2 * (n_of(l, h) + 1))
                transposes(lambda j: pair(xn, j), s["t_ps"], None, None)
                flat = tmp[:, :, :].rearrange("p t c -> p (t c)")
                for b, (j0, j1) in enumerate(TB):
                    pe.wait_ge(s["t_done"], turn(s["t_done"]))
                    for j in range(j0, j1):
                        ins = pe.matmul(PB[5][:, j * 16:(j + 1) * 16], flat[:, j * P:(j + 1) * P], sc(f"r{l}"),
                                        start=True, stop=True)
                ins.then_inc(s["logits_ps"], 1)
                pe.wait_ge(s["onehot_ready"], turn(s["onehot_ready"]))
                pe.matmul(PB[6][:, 0:E * NT], tri16[:, :], mt[:, :], start=True, stop=True)
                pe.matmul(PB[7][:, 0:E * NT], one16[:, :], mt[:, :], start=True, stop=True).then_inc(s["rank_ps"], 1)

            def prep(l, h):
                n = n_of(l, h)
                pe.wait_ge(s["xn_ready"], 2 * n + 1)
                if n > 0:
                    pe.wait_ge(s["route_ready"], n)
                (conv0, conv1, conv2, conv3)[l]()
                route(l, h)

            stage_n = [2, 2]

            def wprep(l):
                nonlocal_lo = turn(s["w_lo"], 0)
                for k in range(2):
                    stage_n[k] += NCH
                    pe.wait_ge(s[f"stage_ld{k}"], 16 * stage_n[k])
                    vv = stage[k][0:CH, :].rearrange("p (k e c) -> p e k c", k=NCH, e=E)
                    for b in range(12):
                        if k * 12 + b >= 4:
                            pe.wait_ge(s["w_lo"], nonlocal_lo + k * 12 + b - 3)
                        for i in range(4):
                            e, c = divmod(4 * b + i, NCH)
                            for q in range(2):
                                ins = pe.matmul(PB[b % 4][q * C:(q + 1) * C, i * CH:(i + 1) * CH], vv[:, e, c, :],
                                                ident[0:CH, 0:CH], start=True, stop=True)
                        ins.then_inc(s["wt_ps"], 1)
                    pe.wait_ge(s["wt_ps"], turn(s["wt_ps"], 12))
                    pe.matmul(PB[7][0:1, 0:1], onef[:, 0:1], onef[:, 0:1], start=True, stop=True).then_inc(s["stage_used"], 1)
                for k in range(2):
                    stage_n[k] += 1
                    pe.wait_ge(s[f"stage_ld{k}"], 16 * stage_n[k])
                    for b in range(3):
                        n = 3 * k + b
                        if n >= 2:
                            pe.wait_ge(s["w_lo"], nonlocal_lo + 24 + n - 1)
                        for i in range(8):
                            e, c = divmod(8 * b + i, NCH)
                            src = stage[k][0:C, e * H2 + CH_AT[c]:e * H2 + CH_AT[c] + CH]
                            ins = pe.transpose(PB[4 + n % 2][0:CH, i * C:(i + 1) * C], src, ident[0:C, 0:C])
                        ins.then_inc(s["wt_ps"], 1)
                    pe.wait_ge(s["wt_ps"], turn(s["wt_ps"], 3))
                    pe.matmul(PB[7][0:1, 0:1], onef[:, 0:1], onef[:, 0:1], start=True, stop=True).then_inc(s["stage_used"], 1)
                turn(s["w_lo"], 31)
                pe.wait_ge(s["w_lo"], nonlocal_lo + 31)

            def moe(l, h):
                n, tb, gb = n_of(l, h), tile_base(l, h), group_base(l, h)
                g_ = G[l]
                widths = {0: H0, 1: H1}

                def expert(i, k):
                    return pe.value_load(eid[h][0:1, ds(i * UNROLL + k, 1)], min_val=0, max_val=E - 1)

                def turn_rows(i, k, t):
                    r = (k + t) % UNROLL
                    ld = 16 * LOOPS * n + 16 * (1 + (k + t) // UNROLL)
                    pe.wait_ge(xs_ld[r], i * 16 + ld)
                    w = i * UNROLL + (tb + k + t)
                    if not (isinstance(i, int) and tb + i * UNROLL + k + t < 2):
                        pe.wait_ge(s["xT_done"], w - 1)
                    bank = PB[6 + r % 2][:, :].bitcast(FP16)
                    for u in range(SUB):
                        ins = pe.transpose(bank[:, u * P:(u + 1) * P], xs[r][:, u * RW:u * RW + P], id16[:, :])
                    ins.then_inc(s["xT_ps"], 1)

                def up(i, k, g, e):
                    q = k * g_ + g
                    w = i * (UNROLL * g_) + (gb + q)
                    if g == 0:
                        pe.wait_ge(s["xT_done"], i * UNROLL + (tb + k + 1))
                    if not (isinstance(i, int) and gb + i * UNROLL * g_ + q < 1):
                        pe.wait_ge(s["hp_ready"], w - 1)
                    rows = xT[k][:, :]
                    for c in range(l + 1 if l < 2 else 2):
                        o = slice(c * ROWS, (c + 1) * ROWS)
                        if l < 2:
                            at = ds(e * widths[l] + c * P, P)
                            pe.matmul(PB[q % 2][:, o], wA[l][:, at], rows, start=True, stop=False)
                            ins = pe.matmul(PB[q % 2][:, o], wB[l][:, at], rows, start=False, stop=True)
                        else:
                            at = ds(e * (NCH * CH) + (2 * g + c) * CH, CH)
                            pe.matmul(PB[q % 2][0:CH, o], gA[:, at], rows, start=True, stop=False)
                            pe.matmul(PB[q % 2][0:CH, o], gB[:, at], rows, start=False, stop=True)
                            pe.matmul(PB[2 + q % 2][0:CH, o], uA[:, at], rows, start=True, stop=False)
                            ins = pe.matmul(PB[2 + q % 2][0:CH, o], uB[:, at], rows, start=False, stop=True)
                    ins.then_inc(s["h_ps"], 1)

                def down(i, k, g, e):
                    q = k * g_ + g
                    w = i * (UNROLL * g_) + (gb + q)
                    pe.wait_ge(s["hp_ready"], w + 1)
                    if g == 0 and not (isinstance(i, int) and tb + i * UNROLL + k < 2):
                        pe.wait_ge(s["y_done"], i * UNROLL + (tb + k - 1))
                    cs = l + 1 if l < 2 else 2
                    kr = P if l < 2 else CH
                    for c in range(cs):
                        for u in range(SUB):
                            col = c * ROWS + u * P
                            if l < 2:
                                rhs = wD[l][:, ds(e * ((l + 1) * C) + c * C, C)]
                            else:
                                rhs = dT[0:CH, ds(e * (NCH * C) + (2 * g + c) * C, C)]
                            ins = pe.matmul(PB[4 + k % 2][:, u * C:(u + 1) * C], hb[q % 2][0:kr, col:col + P], rhs,
                                            start=(g == 0 and c == 0 and u == 0), stop=(g == g_ - 1 and c == cs - 1),
                                            skip_group_check=True)
                    ins.then_inc(s["y_grp"], 1)

                def body(i, e, last=False):
                    for k in range(UNROLL):
                        if not (last and k + 2 >= UNROLL):
                            turn_rows(i, k, 2)
                        for g in range(g_):
                            if g + 1 < g_:
                                up(i, k, g + 1, e)
                                down(i, k, g, e)
                            elif k + 1 < UNROLL:
                                en = expert(i, k + 1)
                                up(i, k + 1, 0, en)
                                down(i, k, g, e)
                                e = en
                            elif not last:
                                up(i + 1, 0, 0, expert(i + 1, 0))
                                down(i, k, g, e)
                            else:
                                down(i, k, g, e)

                pe.wait_ge(s["route_ready"], 2 * (l + 1))
                turn_rows(0, 0, 0)
                turn_rows(0, 1, 0)
                e0 = expert(0, 0)
                up(0, 0, 0, e0)
                body(0, e0)
                with pe.Fori(1, LOOPS - 1) as i:
                    body(i, expert(i, 0))
                body(LOOPS - 1, expert(LOOPS - 1, 0), last=True)

            pe.wait_ge(s["const_ld"], 16)
            for h in range(HALVES):
                pe.wait_ge(s["x_ld"], 32 * (h + 1))
                if h == 0:
                    pe.wait_ge(s["x_ld"], 64)
                src = (xn, tmp)[h][:, :, :].rearrange("p t c -> p (t c)")
                for b, (j0, j1) in enumerate(TB):
                    if h:
                        pe.wait_ge(s["xin_done"], b + 1)
                    for j in range(j0, j1):
                        ins = pe.transpose(PB[b][:, (j - j0) * P:(j - j0 + 1) * P], src[:, j * P:(j + 1) * P], ident)
                    ins.then_inc(s["xin_ps"], 1)
            pe.wait_ge(s["b_ld"], 16 * 10)
            pe.wait_ge(s["consts_done"], 1)
            pe.transpose(PB[5][:, 0:E], act[0][0:E, 0:P], ident[0:E, 0:E])
            pe.transpose(PB[5][:, 64:64 + 2 * E], act[1][0:2 * E, 0:P], ident[0:2 * E, 0:2 * E])
            pe.transpose(PB[5][:, 128:128 + E], act[0][0:E, P:2 * P], ident[0:E, 0:E])
            pe.transpose(PB[5][:, 128 + E:128 + 2 * E], act[1][0:E, P:2 * P], ident[0:E, 0:E]).then_inc(s["b_ps"], 1)
            pe.wait_ge(s["b_done"], 1)
            pe.wait_ge(s["stage_ld1"], 32)
            for e in range(E):
                for c in range(2):
                    at = e * H1 + c * P
                    ins = pe.matmul(PB[6][:, 2 * e + c:2 * e + c + 1], stage[1][0:C, at:at + P], lnT[0:C, E + e:E + e + 1],
                                    start=True, stop=True)
            ins.then_inc(s["l1b_ps"], 1)
            for l in range(NL):
                for h in range(HALVES):
                    prep(l, h)
                if l in (0, 3):
                    wprep(l)
                for h in range(HALVES):
                    moe(l, h)
            for h in range(HALVES):
                pe.wait_ge(s["second_added"], 16 * NT * (n_of(NL - 1, h) + 1))
                if h:
                    pe.wait_ge(s["t_done"], turn(s["t_done"], len(TB)))
                transposes(lambda j: pair(x[h], j), s["t_ps"], None, None)


_NAMES = ["x"] + [f"L0_conv_{n}" for n in ("w1", "b1", "w2", "b2")] + \
    [f"L0_ffn_{n}" for n in ("gate_w", "gate_b", "W1", "b1", "W2", "b2")] + \
    [f"L1_conv_{n}" for n in ("w1", "b1", "w2", "b2")] + \
    [f"L1_ffn_{n}" for n in ("Wr", "br", "ln_g", "ln_b", "W1", "b1", "W2", "b2")] + \
    [f"L2_conv_{n}" for n in ("w1", "w2", "w_enc", "b_enc")] + [f"L2_ffn_{n}" for n in ("router_w", "w1", "w2", "w3")] + \
    ["L3_conv_weight", "L3_conv_bias"] + [f"L3_ffn_{n}" for n in ("router_w", "w1", "w2", "w3")]


def kernel(**inputs):
    import concourse.bacc as bacc
    from concourse.bass_utils import run_bass_kernel_spmd

    nc = bacc.Bacc("TRN2", target_bir_lowering=False, num_devices=1)
    arrays, aps = {}, {}
    for name in _NAMES:
        arr = np.ascontiguousarray(inputs[name])
        arrays[f"in_{name}"] = arr
        aps[name] = nc.dram_tensor(f"in_{name}", arr.shape, mybir.dt.from_np(arr.dtype), kind="ExternalInput").ap()
    k = constants()
    arrays["konst"] = k
    konst = nc.dram_tensor("konst", k.shape, FP32, kind="ExternalInput").ap()
    out = nc.dram_tensor("out", (B, C, HW, HW), FP32, kind="ExternalOutput").ap()
    program(nc, aps, konst, out)
    r = run_bass_kernel_spmd(nc, [arrays], core_ids=[0])
    return r.results[0]["out"]
```

```python
import numpy as np
import concourse.bass as bass
from concourse import mybir
from contextlib import ExitStack

FP32 = mybir.dt.float32
FP16 = mybir.dt.float16
I32 = mybir.dt.int32
ALU = mybir.AluOpType
ACT = mybir.ActivationFunctionType
AX = mybir.AxisListType
ds = bass.ds

B, C, HW = 16, 64, 24
PIX = HW * HW
P = 128
HALVES = 2
HB = B // HALVES
QS = HB // 2
NTOK = HB * PIX
NT = NTOK // P
QT = NT // 2
E, TOPK = 8, 2
ROWS = 256
SUB = ROWS // P
UNROLL = 4
JOIN = 3
TILES = -(-((TOPK * NTOK + E * (ROWS - 1)) // ROWS) // UNROLL) * UNROLL
WORD = 7
MAXE = -(-NTOK // ROWS)
AHEAD = 3
WSCALE = 16.0
RW = 2 * C + 2
H0, H1, H2 = 128, 256, 682
CH = 114
NCH = 6
CH_AT = [c * CH for c in range(NCH - 1)] + [H2 - CH]
OVERLAP = NCH * CH - H2
SPLIT = 2
TBANK = 4
TB = [(b * TBANK, min(QT, (b + 1) * TBANK)) for b in range(-(-QT // TBANK))]
EPS_C, EPS_T = 1e-6, 1e-5
BIG = 1e30

_K = {}
_at = 0
for _n, _w in (("ident", P), ("tri", P), ("blk", P), ("i2", C), ("haar", QT * QS * 4), ("ind", QT * QS),
               ("mask", 2), ("e8", E), ("k4", 4), ("tile", TILES + WORD - UNROLL), ("thr", MAXE)):
    _K[_n] = (_at, _w)
    _at += _w
KCOLS = _at


def constants():
    k = np.zeros((P, KCOLS), np.float32)
    p = np.arange(P)

    def put(name, a):
        k[:, _K[name][0]:_K[name][0] + _K[name][1]] = np.asarray(a, np.float32).reshape(-1, _K[name][1])
    put("ident", np.eye(P))
    put("tri", p[:, None] < p[None, :])
    put("blk", (p[:, None] // C) == (p[None, :] // C))
    put("i2", (p[:, None] % C) == np.arange(C)[None, :])
    tok = np.arange(QT)[None, :] * P + p[:, None]
    s, pix = tok // PIX, tok % PIX
    r, c = (pix // HW) % 2, pix % 2
    sr, sc = 2 * r - 1, 2 * c - 1
    sign = np.stack([np.ones_like(r), sc, sr, sr * sc], -1)
    own = s[:, :, None] == np.arange(QS)
    put("haar", own[:, :, :, None] * sign[:, :, None, :])
    put("ind", own)
    put("mask", np.stack([p < P // 2, p >= P // 2], -1))
    put("e8", (E - np.arange(E))[None])
    put("k4", (4 - np.arange(4))[None])
    put("tile", np.arange(TILES + WORD - UNROLL)[None] - 1)
    put("thr", (np.arange(MAXE) * ROWS)[None])
    return k


_S = {}
_at = 0
for _n, _w in (("c0w1", 16), ("c0w2", P), ("c0b1", 1), ("c0b2", 1), ("c1w1", 16), ("c1w2", 4 * P), ("c1b1", 1),
               ("c1b2", 4), ("c2w1", C), ("c2w2", P), ("c2we", 1), ("c2be", 1), ("c3w", 9), ("c3b", 1),
               ("r0", 16), ("r1", 16), ("r2", 16), ("r3", 16), ("rb0", E), ("rb1", E)):
    _S[_n] = (_at, _w)
    _at += _w
SCOLS = _at


class Turn:

    def __init__(self):
        self.n = {}

    def __call__(self, sem, by=1):
        self.n[id(sem)] = self.n.get(id(sem), 0) + by
        return self.n[id(sem)]


def program(nc, I, konst, out):
    ctx = ExitStack()
    with ctx:
        def sb(name, shape, dt=FP32):
            return ctx.enter_context(nc.sbuf_tensor(name, shape, dt))

        def sem(name):
            return ctx.enter_context(nc.semaphore(name))

        rows_d = [nc.dram_tensor(f"rows_{h}", [TILES * ROWS, RW // 2], I32).ap() for h in range(HALVES)]
        y_d = [nc.dram_tensor(f"y_{h}", [TILES * ROWS, C], FP32).ap() for h in range(HALVES)]

        K = sb("K", [P, KCOLS])
        S = sb("S", [P, SCOLS])
        x = [sb(f"x{h}", [P, NT, C]) for h in range(HALVES)]
        xn = sb("xn", [P, NT, C])
        tmp = sb("tmp", [P, NT, C])
        rowsb = [sb(f"rowsb{h}", [P, NT, RW], FP16) for h in range(HALVES)]
        w01 = sb("w01", [P, 2 * E * (H0 + H1)], FP16)
        wA = {0: w01[:, 0:E * H0], 1: w01[:, 2 * E * H0:2 * E * H0 + E * H1]}
        wB = {0: w01[:, E * H0:2 * E * H0], 1: w01[:, 2 * E * H0 + E * H1:]}
        wD = {0: sb("w0d", [P, E * C]), 1: sb("w1d", [P, E * 2 * C])}
        b1T = {0: sb("b1T0", [P, E]), 1: sb("b1T1", [P, 2 * E])}
        b2R = {0: sb("b2R0", [P, E * C]), 1: sb("b2R1", [P, E * C])}
        gA, gB = sb("gA", [P, E * NCH * CH], FP16), sb("gB", [P, E * NCH * CH], FP16)
        uA, uB = sb("uA", [P, E * NCH * CH], FP16), sb("uB", [P, E * NCH * CH], FP16)
        NSP, NFU = 2 * SPLIT, NCH - 2 * SPLIT
        dW = sb("dW", [CH, E * NSP * 2 * C], FP16)
        dV = dW[:, :].rearrange("p (k s c) -> p k s c", s=2, c=C)
        dF = sb("dF", [CH, E * NFU * C])
        STW = E * NCH * C
        stage = [sb(f"stage{i}", [P, STW]) for i in range(2)]
        lnT = sb("lnT", [P, 2 * E])
        id16, tri16, one16 = (sb(n, [P, P], FP16) for n in ("id16", "tri16", "one16"))
        onef = sb("onef", [P, 2])
        i15 = sb("i15", [P, C])
        wencb = sb("wencb", [P, P])
        st = sb("st", [P, 8, NT])
        lg, eq, k1, k2 = (sb(n, [P, NT, E]) for n in ("lg", "eq", "k1", "k2"))
        ex = sb("ex", [P, NT * E + NT])
        mt = sb("mt", [P, E * NT], FP16)
        incl = sb("incl", [P, E, NT])
        r8 = sb("r8", [P, 6, E])
        spare = tmp[:, :, :].rearrange("p t c -> p (t c)")
        cmp_ = spare[:, 0:E * MAXE]
        NEID = TILES + WORD - UNROLL
        eidf = spare[0:1, E * MAXE:(MAXE + NEID) * E]
        eidr = spare[0:1, (MAXE + NEID) * E:(MAXE + NEID) * E + NEID]
        eidw = spare[0:1, (MAXE + NEID) * E + NEID:(MAXE + NEID) * E + NEID + TILES // UNROLL]
        eid = [sb(f"eid{h}", [1, TILES // UNROLL], I32) for h in range(HALVES)]
        pos = [sb(f"pos{h}", [P, TOPK, NT], I32) for h in range(HALVES)]
        gts = [sb(f"gts{h}", [P, TOPK, NT]) for h in range(HALVES)]
        mx = sb("mx", [P, 2, 4, C])
        srow = sb("srow", [1, 2, HB * C])
        nsW = sb("nsW", [P, QS, C])
        sm = sb("sm", [P, 64])
        hid = sb("hid", [P, QS])
        gate = sb("gate", [P, QS])
        par = sb("par", [P, 4, QS])
        gx = sb("gx", [P, 4 * QS * C])
        nsA, nsY, nsZ = (gx[:, k * QS * C:(k + 1) * QS * C].rearrange("p (s c) -> p s c", c=C) for k in (1, 2, 3))
        xs = [sb(f"xs{i}", [P, SUB * RW], FP16) for i in range(UNROLL)]
        xT = [sb(f"xT{i}", [P, ROWS], FP16) for i in range(UNROLL)]
        gt = [sb(f"gt{i}", [P, SUB]) for i in range(UNROLL)]
        act = [sb(f"act{i}", [P, 2 * ROWS]) for i in range(2)]
        hb = [sb(f"hb{i}", [P, 2 * ROWS]) for i in range(2)]
        hid4 = hb + act
        prod = act + hb
        hl = [sb(f"hl{i}", [P, 4 * ROWS], FP16) for i in range(SPLIT)]
        yb = [sb(f"yb{i}", [P, SUB * C]) for i in range(2)]
        ysb = [sb(f"ysb{i}", [P, SUB * C]) for i in range(UNROLL)]
        PW = HW + 2
        pad = w01[:, 0:2 * QS * PW * PW].bitcast(FP32).rearrange("p (s a b) -> p s a b", s=QS, a=PW)
        PB = [ctx.enter_context(nc.psum_tensor(f"bank{i}", [P, 512], FP32)) for i in range(8)]

        def kc(name, rows=P):
            return K[0:rows, _K[name][0]:_K[name][0] + _K[name][1]]

        def sc(name, p0=0, p1=P):
            return S[p0:p1, _S[name][0]:_S[name][0] + _S[name][1]]

        ident = kc("ident")

        names = ("const_ld small_ld zeroed rows_zero x_ld dve_chain act_chain consts_done xin_ps xin_done centred squared "
                 "var_ready std_ready xn_ready mixed_ready sums_ps rows_ready cov_ps diag_ready tr_ps normv_ready "
                 "norm_root ns_ready ns_ps col_ps v_ready hid_ps hid_ready gate_ps gate_ready gain_ps applied "
                 "pool_ps pooled out4_ps out4_ready gate_wide par_ready band_ps band_ready z_ps z_ready t_ps t_done "
                 "split_hi logits_ps logit_shift exp_ready onehot_ready rank_ps route_ready first_sent second_gate second_sent "
                 "first_added second_added xT_ps xT_done h_ps s_ready hp_ready y_grp y_done "
                 "stage_ld0 stage_ld1 stage_used wt_ps w_hi w_lo prod_ready hi_ready conv_done res_ps out_ps out_ready stored "
                 "b_ld b_ps b_done l1b_ps w01_done pad_zero up_done").split()
        s = {n: sem(n) for n in names}
        xs_ld = [sem(f"xs_ld{i}") for i in range(UNROLL)]
        y_st = [sem(f"y_st{i}") for i in range(UNROLL)]

        block = ctx.enter_context(nc.Block())

        NL = 4
        G = [1, 1, 3, 3]
        order = [(l, h) for l in range(NL) for h in range(HALVES)]

        def n_of(l, h):
            return l * HALVES + h

        def group_base(l, h):
            return sum(G[a] * TILES for a, b in order[:n_of(l, h)])

        def tile_base(l, h):
            return n_of(l, h) * TILES

        LOOPS = TILES // UNROLL
        assert (LOOPS - 2) % JOIN == 0

        def experts(eng, h, i, tiles=range(-1, WORD - 1)):
            w = eng.value_load(eid[h][0:1, ds(i, 1)], min_val=0, max_val=E ** WORD - 1)
            return {k: eng.snap((w >> (3 * (k + 1))) & (E - 1), min_val=0, max_val=E - 1) for k in tiles}

        def middle(eng, body):
            with eng.Fori(0, (LOOPS - 2) // JOIN) as i:
                for j in range(JOIN):
                    body(i * JOIN + (j + 1))

        def split_base(l, h):
            return (n_of(l, h) - n_of(2, 0)) * TILES * SPLIT

        def hold(k, g):
            return prod[g if g < SPLIT else SPLIT + k % 2]

        def wait_from(eng, semaphore, value, floor):
            if not isinstance(value, int) or value > floor:
                eng.wait_ge(semaphore, value)

        def pieces(q, s4):
            m = s4 // 2
            if s4 % 2 == 0:
                return [xn[:, 2 * (9 * m + t) + q, :] for t in range(4)] + [mx[:, 0, 2 * m + q, :]]
            return [mx[:, 1, 2 * m + q, :]] + [xn[:, 2 * (9 * m + 5 + t) + q, :] for t in range(4)]

        def pair(t, j):
            return t[:, 2 * j:2 * j + 2, :].rearrange("p q c -> p (q c)")

        def words(h):
            return rowsb[h][:, :, :].rearrange("p t c -> p (t c)").bitcast(I32)

        def gate_column(h):
            return words(h).bitcast(FP32).rearrange("p (t c) -> p t c", c=RW // 2)[:, :, RW // 2 - 1]

        def gain_view(v):
            m, k = divmod(v, 3)
            t0 = 9 * m + (0, 4, 5)[k]
            return t0, t0 + (4, 1, 4)[k]

        NV = 6

        @block.sync
        def _(sp):
            turn = Turn()
            sp.dma_start(K[:, :], konst).then_inc(s["const_ld"], 16)
            for h in range(HALVES):
                for q in range(2):
                    b0 = h * HB + q * QS
                    dst = (xn, tmp)[h][q * C:(q + 1) * C, :, :].rearrange("p t c -> p (t c)").rearrange(
                        "p (s n) -> p s n", s=QS)
                    sp.dma_start(dst, I["x"][b0:b0 + QS].rearrange("s c a b -> c s (a b)")).then_inc(s["x_ld"], 16)
            for l in (0, 1):
                sp.dma_start(wD[l][:, :].rearrange("p (e k c) -> p e k c", e=E, c=C),
                             I[f"L{l}_ffn_W2"].rearrange("e (k p) c -> p e k c", p=P)).then_inc(s["b_ld"], 16)
                sp.dma_start(b2R[l][:, :], I[f"L{l}_ffn_b2"].rearrange("e c -> (e c)").partition_broadcast(P)
                             ).then_inc(s["b_ld"], 16)
            sp.dma_start(act[0][0:E, 0:P], I["L0_ffn_b1"]).then_inc(s["b_ld"], 16)
            sp.dma_start(act[1][0:2 * E, 0:P], I["L1_ffn_b1"].rearrange("e (k p) -> (e k) p", p=P)).then_inc(s["b_ld"], 16)
            for d in range(2):
                sp.dma_start(act[0][0:E, P + d * C:P + (d + 1) * C], I["L1_ffn_ln_g"]).then_inc(s["b_ld"], 16)
                sp.dma_start(act[1][0:E, P + d * C:P + (d + 1) * C], I["L1_ffn_ln_b"]).then_inc(s["b_ld"], 16)
            for l, w in ((0, H0), (1, H1)):
                for d in range(2):
                    sp.dma_start(stage[l][d * C:(d + 1) * C, 0:E * w].rearrange("p (e n) -> p e n", e=E),
                                 I[f"L{l}_ffn_W1"].rearrange("e d n -> d e n")).then_inc(s[f"stage_ld{l}"], 16)
            used = 0

            def load_stage(l):
                nonlocal used
                for k in range(4):
                    used += 1
                    sp.wait_ge(s["stage_used"], used)
                    if k < 2:
                        w = I[f"L{l}_ffn_{('w1', 'w3')[k]}"]
                        v = stage[k % 2][0:CH, :].rearrange("p (k e c) -> p k e c", k=NCH, e=E)
                        for c in range(NCH):
                            sp.dma_start(v[:, c], w[:, CH_AT[c]:CH_AT[c] + CH, :].rearrange("e p c -> p e c")
                                         ).then_inc(s[f"stage_ld{k % 2}"], 16)
                    else:
                        w = I[f"L{l}_ffn_w2"][4 * (k - 2):4 * (k - 1)]
                        sp.dma_start(stage[k % 2][0:C, 0:4 * H2].rearrange("p (e n) -> p e n", e=4),
                                     w.rearrange("e c n -> c e n")).then_inc(s[f"stage_ld{k % 2}"], 16)
            load_stage(2)

            def moe(l, h):
                n, tb = n_of(l, h), tile_base(l, h)
                ahead = AHEAD if l < 2 else 2

                def load(t, i, k):
                    r = (k + t) % UNROLL
                    wait_from(sp, s["xT_done"], i * UNROLL + (tb + k + t - UNROLL + 1), 0)
                    sp.dma_start(xs[r][:, :].bitcast(I32), rows_d[h][ds((i * UNROLL + (k + t)) * ROWS, ROWS), :].rearrange(
                        "(p s) c -> p (s c)", s=SUB)).then_inc(xs_ld[r], 16)

                def store(i, k):
                    sp.wait_ge(s["y_done"], i * UNROLL + (tb + k + 1))
                    sp.dma_start(y_d[h][ds((i * UNROLL + k) * ROWS, ROWS), :].rearrange(
                        "(p s) c -> p (s c)", s=SUB), ysb[k][:, :]).then_inc(y_st[k], 16)
                sp.wait_ge(s["first_sent"], 16 * NT * (n + 1))
                sp.wait_ge(s["second_sent"], 16 * NT * (n + 1))
                for k in range(UNROLL):
                    load(0, 0, k)
                for k in range(ahead):
                    load(UNROLL, 0, k)

                def body(i, first=False, last=False):
                    for k in range(UNROLL):
                        if not (last and k + ahead >= UNROLL):
                            load(UNROLL + ahead, i, k)
                        if k > 0:
                            store(i, k - 1)
                        elif not first:
                            store(i - 1, UNROLL - 1)
                body(0, first=True)
                with sp.Fori(1, LOOPS - 2) as i:
                    body(i)
                body(LOOPS - 2, last=True)
                for k in range(UNROLL + 1):
                    store(*divmod((LOOPS - 1) * UNROLL - 1 + k, UNROLL))

            for l in range(NL):
                if l == 3:
                    load_stage(3)
                for h in range(HALVES):
                    moe(l, h)
            for h in range(HALVES):
                for q in range(2):
                    b0 = h * HB + q * QS
                    sp.wait_ge(s["out_ready"], h + 1)
                    src = (xn, tmp)[h][q * C:(q + 1) * C, :, :].rearrange("p t c -> p (t c)").rearrange(
                        "p (s n) -> p s n", s=QS)
                    sp.dma_start(out[b0:b0 + QS].rearrange("s c a b -> c s (a b)"), src).then_inc(s["stored"], 16)
            sp.wait_ge(s["stored"], 16 * 2 * HALVES)

        @block.gpsimd
        def _(pool):
            pool.memset(S[:, :], 0.0).then_inc(s["zeroed"], 1)
            pool.memset(rowsb[0][:, :, :], 0.0).then_inc(s["rows_zero"], 1)
            pool.wait_ge(s["rows_zero"], 1)
            for h in range(HALVES):
                flat = rows_d[h].rearrange("(p r) c -> p (r c)", p=P)
                per = TILES * ROWS // P * (RW // 2)
                for a in range(0, per, NT * RW // 2):
                    w = min(NT * RW // 2, per - a)
                    pool.dma_start(flat[:, a:a + w], words(0)[:, 0:w]).then_inc(s["up_done"], 16)
            nz = HALVES * -(-(TILES * ROWS // P * RW) // (NT * RW))
            pool.wait_ge(s["up_done"], 16 * nz)
            pool.memset(onef[:, :], 1.0).then_inc(s["rows_zero"], 1)

            def scatter(l, h):
                n = n_of(l, h)
                pool.wait_ge(s["route_ready"], n + 1)
                for j in range(NT):
                    pool.indirect_dma_start(rows_d[h], bass.IndirectOffsetOnAxis(pos[h][:, 0, j:j + 1], 0),
                                            words(h)[:, j * RW // 2:(j + 1) * RW // 2], None).then_inc(s["first_sent"], 16)
                pool.wait_ge(s["first_sent"], 16 * NT * (n + 1))
                pool.tensor_copy(gate_column(h), gts[h][:, 1, :]).then_inc(s["second_gate"], 1)
                pool.wait_ge(s["second_gate"], n + 1)
                for j in range(NT):
                    pool.indirect_dma_start(rows_d[h], bass.IndirectOffsetOnAxis(pos[h][:, 1, j:j + 1], 0),
                                            words(h)[:, j * RW // 2:(j + 1) * RW // 2], None).then_inc(s["second_sent"], 16)

            def gather(l, h):
                n = n_of(l, h)
                for k in range(UNROLL):
                    pool.wait_ge(y_st[k], 16 * LOOPS * (n + 1))
                for j in range(NT):
                    pool.indirect_dma_start(x[h][:, j, :], None, y_d[h], bass.IndirectOffsetOnAxis(pos[h][:, 0, j:j + 1], 0),
                                            compute_op=ALU.add).then_inc(s["first_added"], 16)
                pool.wait_ge(s["first_added"], 16 * NT * (n + 1))
                for j in range(NT):
                    pool.indirect_dma_start(x[h][:, j, :], None, y_d[h], bass.IndirectOffsetOnAxis(pos[h][:, 1, j:j + 1], 0),
                                            compute_op=ALU.add).then_inc(s["second_added"], 16)
            for l in range(NL):
                for h in range(HALVES):
                    scatter(l, h)
                for h in range(HALVES):
                    gather(l, h)

        @block.scalar
        def _(a):
            turn = Turn()

            def ln():
                a.wait_ge(s["centred"], turn(s["centred"]))
                a.activation(tmp[:, :, :], xn[:, :, :], ACT.Square).then_inc(s["squared"], 1)
                a.wait_ge(s["var_ready"], turn(s["var_ready"]))
                a.activation(st[:, 3, :], st[:, 2, :], ACT.Sqrt).then_inc(s["std_ready"], 1)

            def gate_tail(hr, b1, b2, w):
                a.wait_ge(s["hid_ps"], turn(s["hid_ps"]))
                if b1 is None:
                    a.activation(hid[0:hr, :], PB[4][0:hr, 0:QS], ACT.Relu).then_inc(s["hid_ready"], 1)
                else:
                    a.activation(hid[0:hr, :], PB[4][0:hr, 0:QS], ACT.Relu, bias=b1[0:hr, :]).then_inc(s["hid_ready"], 1)
                a.wait_ge(s["gate_ps"], turn(s["gate_ps"]))
                if b2 is None:
                    a.activation(gate[:, :], PB[5][:, 0:QS], ACT.Sigmoid).then_inc(s["gate_ready"], 1)
                else:
                    a.activation(gate[:, :], PB[5][:, 0:QS], ACT.Sigmoid, bias=b2).then_inc(s["gate_ready"], 1)

            def conv(l):
                if l == 0:
                    a.wait_ge(s["normv_ready"], turn(s["normv_ready"]))
                    a.activation(sm[:, 12:16], sm[:, 8:12], ACT.Sqrt).then_inc(s["norm_root"], 1)
                    gate_tail(16, sc("c0b1"), sc("c0b2"), None)
                elif l == 1:
                    a.wait_ge(s["hid_ps"], turn(s["hid_ps"]))
                    a.activation(hid[0:16, :], PB[4][0:16, 0:QS], ACT.Relu, bias=sc("c1b1")[0:16, :]).then_inc(s["hid_ready"], 1)
                    a.wait_ge(s["out4_ps"], turn(s["out4_ps"]))
                    for k in range(4):
                        ins = a.activation(par[:, k, :], PB[5][:, k * QS:(k + 1) * QS], ACT.Sigmoid,
                                           bias=sc("c1b2")[:, k:k + 1])
                    ins.then_inc(s["out4_ready"], 1)
                elif l == 2:
                    a.wait_ge(s["z_ps"], turn(s["z_ps"]))
                    a.activation(sm[:, 16:32], PB[1][:, 0:16], ACT.Sigmoid, bias=sc("c2be")).then_inc(s["z_ready"], 1)
                    gate_tail(C, None, None, None)

            def prep(l, h):
                ln()
                conv(l)
                ln()
                a.wait_ge(s["xn_ready"], 2 * (n_of(l, h) + 1))
                a.activation(rowsb[h][:, :, 0:C], xn[:, :, :], ACT.Copy).then_inc(s["split_hi"], 1)
                a.wait_ge(s["logit_shift"], turn(s["logit_shift"]))
                a.activation(ex[:, :], ex[:, :], ACT.Exp).then_inc(s["exp_ready"], 1)

            def wprep():
                for k in range(2):
                    for b in range(12):
                        a.wait_ge(s["wt_ps"], turn(s["wt_ps"]))
                        dst = (gA, uA)[k][:, b * 4 * CH:(b + 1) * 4 * CH]
                        a.activation(dst, PB[b % 4][:, 0:4 * CH], ACT.Copy, scale=WSCALE).then_inc(s["w_hi"], 1)
                for k in range(2):
                    for b in range(2):
                        a.wait_ge(s["wt_ps"], turn(s["wt_ps"]))
                        a.activation(dV[:, (2 * k + b) * 8:(2 * k + b + 1) * 8, 0, :], PB[4 + (3 * k + b) % 2][0:CH, :].rearrange(
                            "p (k c) -> p k c", c=C), ACT.Copy, scale=WSCALE).then_inc(s["w_hi"], 1)
                    turn(s["wt_ps"])

            def moe01(l, h):
                gb = group_base(l, h)
                nc_ = l + 1

                def body(i):
                    es = experts(a, h, i, range(UNROLL))
                    for k in range(UNROLL):
                        v = i * UNROLL + (gb + k)
                        a.wait_ge(s["h_ps"], v + 1)
                        wait_from(a, s["y_grp"], v - 3, 0)
                        for c in range(nc_):
                            o = slice(c * ROWS, (c + 1) * ROWS)
                            ins = a.activation(hid4[k][:, o], PB[k][:, o], ACT.Gelu, scale=1.0 / WSCALE,
                                               bias=b1T[l][:, ds(es[k] * nc_ + c, 1)])
                        ins.then_inc(s["hp_ready"], 1)
                body(0)
                middle(a, body)
                body(LOOPS - 1)

            def moe23(l, h):
                gb, tb = group_base(l, h), tile_base(l, h)
                g0, sb_ = group_base(2, 0), split_base(l, h)

                def silu(i, k, g):
                    q = k * G[l] + g
                    w = i * (UNROLL * G[l]) + (gb + q)
                    a.wait_ge(s["h_ps"], w + 1)
                    if g < SPLIT:
                        a.wait_ge(s["hp_ready"], i * (UNROLL * SPLIT) + (g0 + sb_ + (k - 1) * SPLIT + g + 1))
                    else:
                        a.wait_ge(s["y_grp"], w + 1 - 2 * G[l])
                    a.activation(hold(k, g)[0:CH, :], PB[q % 2][0:CH, :], ACT.Silu, scale=1.0 / WSCALE
                                 ).then_inc(s["s_ready"], 1)

                def high(i, k, g):
                    w = i * (UNROLL * G[l]) + (gb + k * G[l] + g)
                    a.wait_ge(s["prod_ready"], w + 1 - g0)
                    a.wait_ge(s["y_grp"], w + 1 - G[l])
                    a.activation(hl[g][0:CH, 0:2 * ROWS], hold(k, g)[0:CH, :], ACT.Copy).then_inc(s["hi_ready"], 1)

                def take(i, k, t):
                    r = (k + t) % UNROLL
                    a.wait_ge(s["xT_ps"], i * UNROLL + (tb + k + t + 1))
                    a.wait_ge(s["y_done"], i * UNROLL + (tb + k + t - UNROLL + 1))
                    gv = xs[r][:, :].bitcast(FP32).rearrange("p (s c) -> p s c", s=SUB)[:, :, RW // 2 - 1]
                    a.activation(gt[r][:, :], gv, ACT.Copy, scale=1.0 / WSCALE ** 2)
                    a.activation(xT[r][:, :], PB[6 + r % 2][:, :].bitcast(FP16)[:, 0:ROWS], ACT.Copy
                                 ).then_inc(s["xT_done"], 1)

                def body(i, last=False):
                    for k in range(UNROLL):
                        for g in range(G[l]):
                            silu(i, k, g)
                            if g > 0:
                                high(i, k, g - 1)
                            if g == 1 and not (last and k + 2 >= UNROLL):
                                take(i, k, 2)
                take(0, 0, 0)
                take(0, 1, 0)
                body(0)
                middle(a, body)
                body(LOOPS - 1, last=True)

            a.wait_ge(s["zeroed"], 1)
            small = []
            for q in range(2):
                cq, hq = slice(q * C, (q + 1) * C), slice(q * 8, (q + 1) * 8)
                small += [
                    (sc("c0w1")[cq, hq], I["L0_conv_w1"].rearrange("o c -> c o")),
                    (sc("c0w2")[hq, cq], I["L0_conv_w2"].rearrange("c o -> o c")),
                    (sc("c0b1")[hq, :], I["L0_conv_b1"].rearrange("(c o) -> c o", o=1)),
                    (sc("c0b2")[cq, :], I["L0_conv_b2"].rearrange("(c o) -> c o", o=1)),
                    (sc("c1w1")[cq, hq], I["L1_conv_w1"].rearrange("o c -> c o")),
                    (sc("c1b1")[hq, :], I["L1_conv_b1"].rearrange("(c o) -> c o", o=1)),
                    (sc("c1b2")[cq, :].rearrange("p (k t) -> p k t", k=2), I["L1_conv_b2"].rearrange("k (c t) -> c k t", t=2)),
                    (sc("c2w1")[cq, q * 32:(q + 1) * 32], I["L2_conv_w1"].rearrange("o c -> c o")),
                    (sc("c2w2")[q * 32:(q + 1) * 32, cq], I["L2_conv_w2"].rearrange("c o -> o c")),
                    (sc("c2we")[cq, :], I["L2_conv_w_enc"].rearrange("o c -> c o")),
                    (sc("c3w")[cq, :], I["L3_conv_weight"].rearrange("c o a b -> c (o a b)")),
                    (sc("c3b")[cq, :], I["L3_conv_bias"].rearrange("(c o) -> c o", o=1)),
                    (sc("r0")[cq, hq], I["L0_ffn_gate_w"]),
                    (sc("r1")[cq, hq], I["L1_ffn_Wr"]),
                    (sc("r2")[cq, hq], I["L2_ffn_router_w"].rearrange("e c -> c e")),
                    (sc("r3")[cq, hq], I["L3_ffn_router_w"].rearrange("e c -> c e")),
                ]
                for k in range(2):
                    for t in range(2):
                        v = sc("c1w2")[hq, (2 * k + t) * P + q * C:(2 * k + t) * P + (q + 1) * C]
                        small.append((v, I["L1_conv_w2"][k].rearrange("(c t) h -> t h c", t=2)[t]))
            small.append((sc("c2be"), I["L2_conv_b_enc"].partition_broadcast(P)))
            small.append((sc("rb0"), I["L0_ffn_gate_b"].partition_broadcast(P)))
            small.append((sc("rb1"), I["L1_ffn_br"].partition_broadcast(P)))
            for dst, src in small:
                a.dma_start(dst, src, allow_slow_non_contiguous=True).then_inc(s["small_ld"], 16)
            for l, w in ((0, H0), (1, H1)):
                a.wait_ge(s["w01_done"], 1 + l)
                a.activation(wA[l][:, :], stage[l][:, 0:E * w], ACT.Copy, scale=WSCALE).then_inc(s["w_hi"], 1)
            for l in range(NL):
                for h in range(HALVES):
                    prep(l, h)
                if l in (0, 3):
                    wprep()
                for h in range(HALVES):
                    (moe01 if l < 2 else moe23)(l, h)

        @block.vector
        def _(v):
            turn = Turn()

            def link(ins):
                ins.then_inc(s["dve_chain"], 1)
                v.wait_ge(s["dve_chain"], turn(s["dve_chain"]))

            def bc(ap, m):
                return ap.unsqueeze(2).broadcast_to([ap.shape[0], ap.shape[1], m])

            def bt(ap, m):
                return ap.unsqueeze(1).broadcast_to([ap.shape[0], m, ap.shape[1]])

            def ln(xh, eps):
                link(v.tensor_reduce(st[:, 0, :], xh[:, :, :], AX.X, ALU.add))
                link(v.tensor_scalar(st[:, 1, :], st[:, 0, :], 1.0 / C, None, ALU.mult))
                v.tensor_tensor(xn[:, :, :], xh[:, :, :], bc(st[:, 1, :], C), ALU.subtract).then_inc(s["centred"], 1)
                v.wait_ge(s["squared"], turn(s["squared"]))
                link(v.tensor_reduce(st[:, 0, :], tmp[:, :, :], AX.X, ALU.add))
                v.tensor_scalar(st[:, 2, :], st[:, 0, :], 1.0 / C, eps, ALU.mult, ALU.add).then_inc(s["var_ready"], 1)
                v.wait_ge(s["std_ready"], turn(s["std_ready"]))
                link(v.reciprocal(st[:, 4, :], st[:, 3, :]))
                link(v.tensor_tensor(st[:, 5, :], st[:, 4, :], st[:, 4, :], ALU.mult))
                link(v.tensor_tensor(st[:, 5, :], st[:, 5, :], st[:, 2, :], ALU.mult))
                link(v.tensor_scalar(st[:, 5, :], st[:, 5, :], -0.5, 1.5, ALU.mult, ALU.add))
                link(v.tensor_tensor(st[:, 4, :], st[:, 4, :], st[:, 5, :], ALU.mult))
                v.tensor_tensor(xn[:, :, :], xn[:, :, :], bc(st[:, 4, :], C), ALU.mult).then_inc(s["xn_ready"], 1)
                v.wait_ge(s["xn_ready"], turn(s["xn_ready"]))

            def gained(dst, src, banks, kind, op):
                for k in range(NV):
                    t0, t1 = gain_view(k)
                    i = kind * NV + k
                    g = PB[banks[i // 4]][:, (i % 4) * P:(i % 4 + 1) * P]
                    g = g.unsqueeze(1).broadcast_to([P, t1 - t0, P])
                    d = dst[:, 2 * t0:2 * t1, :].rearrange("p (t q) c -> p t (q c)", q=2)
                    r = src[:, 2 * t0:2 * t1, :].rearrange("p (t q) c -> p t (q c)", q=2)
                    ins = v.tensor_tensor(d, r, g, op)
                link(ins)

            def apply_gate(xh):
                v.wait_ge(s["gate_ready"], turn(s["gate_ready"]))
                v.tensor_copy(gx[:, 0:QS * C].rearrange("p (k c) -> p k c", c=C), bc(gate[:, :], C)).then_inc(s["gate_wide"], 1)
                v.wait_ge(s["gain_ps"], turn(s["gain_ps"]))
                gained(tmp, xn, (6, 7), 0, ALU.mult)
                v.tensor_tensor(xh[:, :, :], xh[:, :, :], tmp[:, :, :], ALU.add).then_inc(s["applied"], 1)
                v.wait_ge(s["applied"], turn(s["applied"]))

            def conv0(xh, h):
                shared = xn[:, :, :].rearrange("p (m t) c -> p m t c", m=2)[:, :, 8:10, :]
                for m in range(2):
                    ins = v.tensor_scalar(mx[:, m, :, :].rearrange("p (m t) c -> p m t c", m=2), shared,
                                          kc("mask")[:, m:m + 1], None, ALU.mult)
                ins.then_inc(s["mixed_ready"], 1)
                v.wait_ge(s["sums_ps"], turn(s["sums_ps"]))
                link(v.tensor_copy(srow[:, 0, :], PB[0][0:1, 0:HB * C]))
                v.tensor_scalar(srow[:, 1, :], srow[:, 0, :], -1.0 / PIX, None, ALU.mult).then_inc(s["rows_ready"], 1)
                v.wait_ge(s["cov_ps"], turn(s["cov_ps"]))
                cov = PB[1][:, 0:QS * C].rearrange("p (s c) -> p s c", s=QS)
                link(v.tensor_tensor(nsW[:, :, :], cov, bt(kc("i2"), QS), ALU.mult))
                v.tensor_reduce(sm[:, 0:4], nsW[:, :, :], AX.X, ALU.add).then_inc(s["diag_ready"], 1)
                v.wait_ge(s["tr_ps"], turn(s["tr_ps"]))
                link(v.tensor_copy(sm[:, 0:4], PB[2][:, 0:QS]))
                link(v.reciprocal(sm[:, 4:8], sm[:, 0:4]))
                v.tensor_scalar(sm[:, 8:12], sm[:, 0:4], 1.0 / PIX, None, ALU.mult).then_inc(s["normv_ready"], 1)
                link(v.tensor_tensor(nsA[:, :, :], cov, bc(sm[:, 4:8], C), ALU.mult))
                v.scalar_tensor_tensor(nsZ[:, :, :], nsA[:, :, :], -0.5, bt(i15[:, :], QS), ALU.mult, ALU.add
                                       ).then_inc(s["ns_ready"], 1)
                yp, wp, zp = (PB[b][:, 0:QS * C].rearrange("p (s c) -> p s c", s=QS) for b in (3, 4, 5))
                v.wait_ge(s["ns_ps"], turn(s["ns_ps"]))
                v.tensor_copy(nsY[:, :, :], yp).then_inc(s["ns_ready"], 1)
                for it in range(4):
                    v.wait_ge(s["ns_ps"], turn(s["ns_ps"]))
                    v.scalar_tensor_tensor(nsW[:, :, :], wp, -0.5, bt(i15[:, :], QS), ALU.mult, ALU.add
                                           ).then_inc(s["ns_ready"], 1)
                    v.wait_ge(s["ns_ps"], turn(s["ns_ps"]))
                    if it < 3:
                        v.tensor_copy(nsZ[:, :, :], zp)
                    v.tensor_copy(nsY[:, :, :], yp).then_inc(s["ns_ready"], 1)
                v.wait_ge(s["norm_root"], turn(s["norm_root"]))
                link(v.reciprocal(sm[:, 16:20], sm[:, 12:16]))
                link(v.tensor_tensor(sm[:, 16:20], sm[:, 16:20], sm[:, 8:12], ALU.mult))
                link(v.tensor_tensor(sm[:, 16:20], sm[:, 16:20], sm[:, 12:16], ALU.add))
                v.wait_ge(s["col_ps"], turn(s["col_ps"]))
                v.scalar_tensor_tensor(sm[:, 20:24], PB[2][:, 0:QS], 0.5 / C, sm[:, 16:20], ALU.mult, ALU.mult
                                       ).then_inc(s["v_ready"], 1)
                apply_gate(xh)

            def conv1(xh, h):
                v.wait_ge(s["pool_ps"], turn(s["pool_ps"]))
                v.tensor_scalar(sm[:, 20:24], PB[0][:, 0:QS], 1.0 / PIX, None, ALU.mult).then_inc(s["v_ready"], 1)
                v.wait_ge(s["out4_ready"], turn(s["out4_ready"]))
                link(v.tensor_scalar(par[:, :, :], par[:, :, :], 2.0, -1.0, ALU.mult, ALU.add))
                link(v.tensor_scalar(par[:, 1:4:2, :], par[:, 1:4:2, :], 0.5, None, ALU.mult))
                link(v.tensor_scalar(par[:, 0:2, :], par[:, 0:2, :], 1.0, None, ALU.add))
                v.tensor_copy(gx[:, :].rearrange("p (k c) -> p k c", c=C),
                              bc(par[:, :, :].rearrange("p k s -> p (k s)"), C)).then_inc(s["par_ready"], 1)
                v.wait_ge(s["gain_ps"], turn(s["gain_ps"]))
                banks = (0, 1, 2, 3, 6, 7)
                gained(tmp, xn, banks, 0, ALU.mult)
                gained(tmp, tmp, banks, 1, ALU.add)
                gained(xn, xn, banks, 2, ALU.mult)
                gained(xn, xn, banks, 3, ALU.add)
                link(v.tensor_tensor(tmp[:, :, :], tmp[:, :, :], xn[:, :, :], ALU.max))
                v.tensor_tensor(xh[:, :, :], xh[:, :, :], tmp[:, :, :], ALU.add).then_inc(s["applied"], 1)
                v.wait_ge(s["applied"], turn(s["applied"]))

            def conv2(xh, h):
                v.wait_ge(s["band_ps"], turn(s["band_ps"]))
                ori = sm[:, 0:16]
                v.tensor_scalar(ori, PB[0][:, 0:16], 2.0 / PIX, None, ALU.mult).then_inc(s["band_ready"], 1)
                v.wait_ge(s["z_ready"], turn(s["z_ready"]))

                def sk(c):
                    return sm[:, c:c + 16].rearrange("p (s k) -> p s k", k=4)
                link(v.tensor_reduce(sm[:, 32:36], sk(16), AX.X, ALU.max))
                link(v.tensor_tensor(sk(36), sk(16), bc(sm[:, 32:36], 4), ALU.is_equal))
                link(v.tensor_tensor(sk(36), sk(36), bt(kc("k4"), QS), ALU.mult))
                link(v.tensor_reduce(sm[:, 32:36], sk(36), AX.X, ALU.max))
                link(v.tensor_tensor(sk(36), sk(36), bc(sm[:, 32:36], 4), ALU.is_equal))
                link(v.tensor_tensor(sk(36), sk(36), sk(0), ALU.mult))
                link(v.tensor_reduce(sm[:, 32:36], sk(36), AX.X, ALU.add))
                link(v.tensor_tensor(sk(36), sk(0), bc(sm[:, 32:36], 4), ALU.subtract))
                link(v.tensor_scalar(sm[:, 36:52], sm[:, 36:52], 0.0, None, ALU.max))
                v.tensor_reduce(sm[:, 20:24], sk(36), AX.X, ALU.add).then_inc(s["v_ready"], 1)
                apply_gate(xh)

            t_seen = [0]

            def t_count(k):
                t_seen[0] += k
                return t_seen[0]

            def tr_out(dst_flat):
                for b, (j0, j1) in enumerate(TB):
                    v.wait_ge(s["t_ps"], turn(s["t_ps"]))
                    v.tensor_copy(dst_flat[:, j0 * P:j1 * P], PB[b][:, 0:(j1 - j0) * P]).then_inc(s["t_done"], 1)

            def conv3(xh, h):
                flat = tmp[:, :, :].rearrange("p t c -> p (t c)")
                if h == 0:
                    link(v.memset(pad, 0.0))
                tr_out(flat)
                v.wait_ge(s["t_done"], t_count(len(TB)))
                link(v.tensor_copy(pad[:, :, 1:1 + HW, 1:1 + HW].rearrange("p s a b -> p s a b"),
                                   flat.rearrange("p (s a b) -> p s a b", s=QS, a=HW)))
                img = flat.rearrange("p (s a b) -> p s a b", s=QS, a=HW)
                for smp in range(QS):
                    for tap in range(9):
                        dy, dx = divmod(tap, 3)
                        win = pad[:, smp, dy:dy + HW, dx:dx + HW]
                        w = sc("c3w")[:, tap:tap + 1]
                        if tap == 0:
                            ins = v.tensor_scalar(img[:, smp], win, w, sc("c3b"), ALU.mult, ALU.add)
                        else:
                            ins = v.scalar_tensor_tensor(img[:, smp], win, w, img[:, smp], ALU.mult, ALU.add)
                        if smp < QS - 1 or tap < 8:
                            link(ins)
                ins.then_inc(s["conv_done"], 1)
                for b, (j0, j1) in enumerate(TB):
                    v.wait_ge(s["res_ps"], turn(s["res_ps"]))
                    xv = xh[:, 2 * j0:2 * j1, :].rearrange("p t c -> p (t c)")
                    pv = PB[b][:, 0:(j1 - j0) * P]
                    ins = v.tensor_tensor(xv, xv, pv, ALU.add)
                ins.then_inc(s["applied"], 1)
                v.wait_ge(s["applied"], turn(s["applied"]))

            def top(src, mask, m):
                link(v.tensor_tensor(eq[:, :, :], src, bc(m, E), ALU.is_equal))
                link(v.tensor_tensor(eq[:, :, :], eq[:, :, :], bt(kc("e8"), NT), ALU.mult))
                link(v.tensor_reduce(st[:, 7, :], eq[:, :, :], AX.X, ALU.max))
                link(v.tensor_tensor(mask[:, :, :], eq[:, :, :], bc(st[:, 7, :], E), ALU.is_equal))

            def route(l, h):
                flat = tmp[:, :, :].rearrange("p t c -> p (t c)")
                tr_out(flat)
                t_count(len(TB))
                v.wait_ge(s["split_hi"], turn(s["split_hi"]))
                v.tensor_tensor(rowsb[h][:, :, C:2 * C], xn[:, :, :], rowsb[h][:, :, 0:C], ALU.subtract)
                v.wait_ge(s["logits_ps"], turn(s["logits_ps"]))
                src = PB[5][:, 0:QT * 16].rearrange("p (t e) -> p t e", e=E)
                if l < 2:
                    link(v.tensor_tensor(lg[:, :, :], src, bt(sc(f"rb{l}"), NT), ALU.add))
                else:
                    link(v.tensor_copy(lg[:, :, :], src))
                m1, m2 = st[:, 0, :], st[:, 1, :]
                link(v.tensor_reduce(m1, lg[:, :, :], AX.X, ALU.max))
                top(lg[:, :, :], k1, m1)
                exv = ex[:, 0:NT * E].rearrange("p (t e) -> p t e", e=E)
                link(v.tensor_tensor(exv, lg[:, :, :], bc(m1, E), ALU.subtract))
                link(v.scalar_tensor_tensor(lg[:, :, :], k1[:, :, :], -BIG, lg[:, :, :], ALU.mult, ALU.add))
                link(v.tensor_reduce(m2, lg[:, :, :], AX.X, ALU.max))
                v.tensor_tensor(ex[:, NT * E:], m2, m1, ALU.subtract).then_inc(s["logit_shift"], 1)
                top(lg[:, :, :], k2, m2)
                v.tensor_tensor(mt[:, :].rearrange("p (e t) -> p t e", e=E), k1[:, :, :], k2[:, :, :], ALU.add
                                ).then_inc(s["onehot_ready"], 1)
                v.wait_ge(s["exp_ready"], turn(s["exp_ready"]))
                link(v.tensor_reduce(st[:, 2, :], exv, AX.X, ALU.add))
                link(v.reciprocal(gts[h][:, 0, :], st[:, 2, :]))
                link(v.tensor_tensor(gts[h][:, 1, :], gts[h][:, 0, :], ex[:, NT * E:], ALU.mult))
                if l > 0:
                    link(v.tensor_tensor(st[:, 2, :], gts[h][:, 0, :], gts[h][:, 1, :], ALU.add))
                    if l > 1:
                        link(v.tensor_scalar(st[:, 2, :], st[:, 2, :], 1e-9, None, ALU.add))
                    link(v.reciprocal(st[:, 3, :], st[:, 2, :]))
                    link(v.tensor_tensor(gts[h][:, :, :], gts[h][:, :, :], bt(st[:, 3, :], TOPK), ALU.mult))
                link(v.tensor_copy(gate_column(h), gts[h][:, 0, :]))
                v.wait_ge(s["rank_ps"], turn(s["rank_ps"]))
                rank = PB[6][:, 0:E * NT].rearrange("p (e t) -> p e t", e=E)
                cnt = PB[7][:, 0:E * NT].rearrange("p (e t) -> p e t", e=E)
                one = onef[:, 0:1]
                inf = incl[:, :, :].rearrange("p e t -> p (e t)")
                link(v.tensor_tensor_scan(inf, one.broadcast_to([P, E * NT]), PB[7][:, 0:E * NT], 0.0, ALU.mult, ALU.add))
                link(v.tensor_tensor(incl[:, :, :], incl[:, :, :], cnt, ALU.subtract))
                link(v.tensor_tensor(incl[:, :, :], incl[:, :, :], rank, ALU.add))
                link(v.tensor_reduce(r8[:, 0, :], cnt, AX.X, ALU.add))
                cv = cmp_.rearrange("p (e k) -> p e k", e=E)
                link(v.tensor_tensor(cv, bc(r8[:, 0, :], MAXE), bt(kc("thr"), E), ALU.is_gt))
                link(v.tensor_reduce(r8[:, 1, :], cv, AX.X, ALU.add))
                link(v.tensor_tensor_scan(r8[:, 2, :], one.broadcast_to([P, E]), r8[:, 1, :], 0.0, ALU.mult, ALU.add))
                link(v.tensor_tensor_scan(r8[:, 3, :], one.broadcast_to([P, E]), r8[:, 0, :], 0.0, ALU.mult, ALU.add))
                link(v.tensor_tensor(r8[:, 4, :], r8[:, 2, :], r8[:, 1, :], ALU.subtract))
                link(v.tensor_tensor(r8[:, 5, :], r8[:, 0, :], r8[:, 3, :], ALU.subtract))
                link(v.scalar_tensor_tensor(r8[:, 5, :], r8[:, 4, :], float(ROWS), r8[:, 5, :], ALU.mult, ALU.add))
                link(v.tensor_tensor(incl[:, :, :], incl[:, :, :], bc(r8[:, 5, :], NT), ALU.add))
                pv = incl[:, :, :].rearrange("p e t -> p t e")
                for k, m in enumerate((k1, k2)):
                    link(v.tensor_tensor(eq[:, :, :], m[:, :, :], pv, ALU.mult))
                    link(v.tensor_reduce(st[:, 2, :], eq[:, :, :], AX.X, ALU.add))
                    link(v.tensor_copy(pos[h][:, k, :], st[:, 2, :]))
                ev = eidf.rearrange("p (t e) -> p t e", e=E)
                link(v.tensor_tensor(ev, bt(r8[0:1, 2, :], NEID), bc(kc("tile", 1), E), ALU.is_le))
                link(v.tensor_reduce(eidr, ev, AX.X, ALU.add))
                link(v.tensor_scalar(eidr, eidr, float(E - 1), None, ALU.min))
                link(v.tensor_copy(eidw, eidr[:, WORD - 1::UNROLL]))
                for k in reversed(range(WORD - 1)):
                    link(v.scalar_tensor_tensor(eidw, eidw, float(E), eidr[:, k:k + TILES - UNROLL + 1:UNROLL], ALU.mult, ALU.add))
                v.tensor_copy(eid[h][:, :], eidw).then_inc(s["route_ready"], 1)

            def prep(l, h):
                if l > 0:
                    v.wait_ge(s["second_added"], 16 * NT * (n_of(l - 1, h) + 1))
                ln(x[h], EPS_C)
                (conv0, conv1, conv2, conv3)[l](x[h], h)
                ln(x[h], EPS_T)
                route(l, h)

            def wprep():
                for k in range(2):
                    for b in range(12):
                        v.wait_ge(s["w_hi"], turn(s["w_hi"]))
                        hi = (gA, uA)[k][:, b * 4 * CH:(b + 1) * 4 * CH]
                        lo = (gB, uB)[k][:, b * 4 * CH:(b + 1) * 4 * CH]
                        v.scalar_tensor_tensor(lo, PB[b % 4][:, 0:4 * CH], WSCALE, hi, ALU.mult, ALU.subtract
                                               ).then_inc(s["w_lo"], 1)
                for k in range(2):
                    for b in range(2):
                        v.wait_ge(s["w_hi"], turn(s["w_hi"]))
                        at = slice((2 * k + b) * 8, (2 * k + b + 1) * 8)
                        v.scalar_tensor_tensor(dV[:, at, 1, :], PB[4 + (3 * k + b) % 2][0:CH, :].rearrange(
                            "p (k c) -> p k c", c=C), WSCALE, dV[:, at, 0, :], ALU.mult, ALU.subtract).then_inc(s["w_lo"], 1)
                    v.wait_ge(s["wt_ps"], turn(s["wt_ps"], 27 if k == 0 else 3))
                    v.tensor_scalar(dF[:, k * 512:(k + 1) * 512], PB[4 + (3 * k + 2) % 2][0:CH, :], WSCALE, None, ALU.mult
                                    ).then_inc(s["w_lo"], 1)
                v.wait_ge(s["w_lo"], turn(s["w_lo"], 30))
                last = dF[0:OVERLAP, :].rearrange("p (e k c) -> p e k c", e=E, k=NFU)[:, :, NFU - 1, :]
                v.memset(last, 0.0).then_inc(s["w_lo"], 1)
                turn(s["w_lo"])

            def moe(l, h):
                n, tb, gb = n_of(l, h), tile_base(l, h), group_base(l, h)

                def evict(i, k, e=None):
                    t = i * UNROLL + (tb + k)
                    v.wait_ge(s["y_grp"], i * (UNROLL * G[l]) + (gb + (k + 1) * G[l]))
                    wait_from(v, y_st[k], i * 16 + 16 * LOOPS * n, 0)
                    wait_from(v, s["y_done"], t - 1, 0)
                    y = yb[k % 2][:, :].rearrange("p (u c) -> p u c", u=SUB)
                    if l < 2:
                        b2 = b2R[l][:, ds(e * C, C)]
                        for u in range(SUB):
                            ins = v.tensor_tensor(y[:, u, :], PB[4 + k % 2][:, u * C:(u + 1) * C], b2, ALU.add)
                    else:
                        src = PB[4 + k % 2][:, 0:SUB * 2 * C].rearrange("p (u s c) -> p u c s", u=SUB, s=2)
                        ins = v.tensor_reduce(y, src, AX.X, ALU.add)
                    ins.then_inc(s["b_done"], 1)
                    v.wait_ge(s["b_done"], t + 4)
                    v.tensor_tensor(ysb[k][:, :].rearrange("p (u c) -> p u c", u=SUB), y, bc(gt[k][:, :], C), ALU.mult
                                    ).then_inc(s["y_done"], 1)

                def take(i, k, t):
                    r = (k + t) % UNROLL
                    v.wait_ge(s["xT_ps"], i * UNROLL + (tb + k + t + 1))
                    gv = xs[r][:, :].bitcast(FP32).rearrange("p (s c) -> p s c", s=SUB)[:, :, RW // 2 - 1]
                    if t == UNROLL - 1:
                        wait_from(v, s["y_done"], i * UNROLL + (tb + k), 0)
                    v.tensor_copy(gt[r][:, :], gv)
                    v.tensor_copy(xT[r][:, :], PB[6 + r % 2][:, :].bitcast(FP16)[:, 0:ROWS]).then_inc(s["xT_done"], 1)

                def body01(i, last=False, first=False):
                    es = experts(v, h, i, range(0 if first else -1, UNROLL if last else UNROLL - 1))
                    for k in range(UNROLL):
                        if k > 0:
                            evict(i, k - 1, es[k - 1])
                        elif not first:
                            evict(i - 1, UNROLL - 1, es[-1])
                        if not (last and k + AHEAD >= UNROLL):
                            take(i, k, AHEAD)
                    if last:
                        evict(i, UNROLL - 1, es[UNROLL - 1])

                g0, sb_ = group_base(2, 0), split_base(l, h)

                def product(i, k, g):
                    q = k * G[l] + g
                    p = hold(k, g)[0:CH, :]
                    v.wait_ge(s["s_ready"], i * (UNROLL * G[l]) + (gb + q + 1 - g0))
                    v.tensor_tensor(p, PB[2 + q % 2][0:CH, :], p, ALU.mult).then_inc(s["prod_ready"], 1)

                def low(i, k, g):
                    v.wait_ge(s["hi_ready"], i * (UNROLL * SPLIT) + (sb_ + k * SPLIT + g + 1))
                    v.tensor_tensor(hl[g][0:CH, 2 * ROWS:4 * ROWS], hold(k, g)[0:CH, :], hl[g][0:CH, 0:2 * ROWS], ALU.subtract
                                    ).then_inc(s["hp_ready"], 1)

                def body23(i, first=False):
                    for k in range(UNROLL):
                        for g in range(G[l]):
                            product(i, k, g)
                            if g > 0:
                                low(i, k, g - 1)
                            elif k >= 2:
                                evict(i, k - 2)
                            elif not first:
                                evict(i - 1, k + UNROLL - 2)
                if l < 2:
                    for k in range(AHEAD):
                        take(0, k, 0)
                    body01(0, first=True)
                    middle(v, body01)
                    body01(LOOPS - 1, last=True)
                else:
                    body23(0, first=True)
                    middle(v, body23)
                    body23(LOOPS - 1)
                    evict(LOOPS - 1, UNROLL - 2)
                    evict(LOOPS - 1, UNROLL - 1)

            v.wait_ge(s["const_ld"], 16)
            v.wait_ge(s["rows_zero"], 2)
            v.tensor_copy(id16[:, :], ident)
            v.tensor_copy(tri16[:, :], kc("tri"))
            v.memset(one16[:, :], 1.0)
            v.wait_ge(s["small_ld"], 16 * (2 * 20 + 3))
            v.tensor_scalar(wencb[:, :], kc("blk"), sc("c2we"), None, ALU.mult)
            v.tensor_scalar(i15[:, :], kc("i2"), 1.5, None, ALU.mult).then_inc(s["consts_done"], 1)
            for h in range(HALVES):
                for b, (j0, j1) in enumerate(TB):
                    v.wait_ge(s["xin_ps"], turn(s["xin_ps"]))
                    xv = x[h][:, 2 * j0:2 * j1, :].rearrange("p t c -> p (t c)")
                    v.tensor_copy(xv, PB[b][:, 0:(j1 - j0) * P]).then_inc(s["xin_done"], 1)
            v.wait_ge(s["xin_done"], turn(s["xin_done"], HALVES * len(TB)))
            v.wait_ge(s["b_ps"], 1)
            v.tensor_copy(b1T[0][:, :], PB[5][:, 0:E])
            link(v.tensor_copy(b1T[1][:, :], PB[5][:, 64:64 + 2 * E]))
            v.tensor_copy(lnT[:, :], PB[5][:, 128:128 + 2 * E]).then_inc(s["b_done"], 1)
            v.wait_ge(s["b_done"], 1)
            v.wait_ge(s["stage_ld0"], 32)
            v.tensor_scalar(lnT[:, 0:1], lnT[:, 0:1], 1.0, None, ALU.mult).then_inc(s["w01_done"], 1)
            v.wait_ge(s["w01_done"], 1)
            v.wait_ge(s["l1b_ps"], 1)
            v.tensor_tensor(b1T[1][:, :], b1T[1][:, :], PB[6][:, 0:2 * E], ALU.add).then_inc(s["b_done"], 1)
            for e in range(E):
                ins = v.tensor_scalar(stage[1][:, e * H1:(e + 1) * H1], stage[1][:, e * H1:(e + 1) * H1], lnT[:, e:e + 1],
                                      None, ALU.mult)
            ins.then_inc(s["w01_done"], 1)
            for l, w in ((0, H0), (1, H1)):
                v.wait_ge(s["w_hi"], turn(s["w_hi"]))
                v.scalar_tensor_tensor(wB[l][:, :], stage[l][:, 0:E * w], WSCALE, wA[l][:, :], ALU.mult, ALU.subtract
                                       ).then_inc(s["stage_used"], 1)
            v.wait_ge(s["b_ld"], 16 * 10)
            v.memset(yb[0][:, :], 0.0).then_inc(s["b_done"], 1)
            for l in range(NL):
                for h in range(HALVES):
                    prep(l, h)
                if l in (0, 3):
                    wprep()
                for h in range(HALVES):
                    moe(l, h)
            for h in range(HALVES):
                v.wait_ge(s["second_added"], 16 * NT * (n_of(NL - 1, h) + 1))
                flat = (xn, tmp)[h][:, :, :].rearrange("p t c -> p (t c)")
                tr_out(flat)
                v.wait_ge(s["t_done"], t_count(len(TB)))
                v.tensor_scalar(sm[:, 63:64], onef[:, 0:1], 1.0, None, ALU.mult).then_inc(s["out_ready"], 1)

        @block.tensor
        def _(pe):
            turn = Turn()

            def transposes(src, sem_ps, sem_done, wait_all):
                for b, (j0, j1) in enumerate(TB):
                    for j in range(j0, j1):
                        ins = pe.transpose(PB[b][:, (j - j0) * P:(j - j0 + 1) * P], src(j), ident)
                    ins.then_inc(sem_ps, 1)

            def conv0():
                pe.wait_ge(s["mixed_ready"], turn(s["mixed_ready"]))
                for smp in range(HB):
                    ops = pieces(*divmod(smp, QS))
                    for i, o in enumerate(ops):
                        ins = pe.matmul(PB[0][0:1, smp * C:(smp + 1) * C], onef[:, 0:1], o, start=(i == 0), stop=(i == 4))
                ins.then_inc(s["sums_ps"], 1)
                for smp in range(HB):
                    q, s4 = divmod(smp, QS)
                    ops = pieces(q, s4)
                    for i, o in enumerate(ops):
                        pe.matmul(PB[1][q * C:(q + 1) * C, s4 * C:(s4 + 1) * C], o, o, start=(i == 0 and s4 == 0),
                                  stop=False, skip_group_check=True)
                pe.wait_ge(s["rows_ready"], turn(s["rows_ready"]))
                for smp in range(HB):
                    q, s4 = divmod(smp, QS)
                    ins = pe.matmul(PB[1][q * C:(q + 1) * C, s4 * C:(s4 + 1) * C], srow[0:1, 1, smp * C:(smp + 1) * C],
                                    srow[0:1, 0, smp * C:(smp + 1) * C], start=False, stop=True, skip_group_check=True)
                ins.then_inc(s["cov_ps"], 1)
                pe.wait_ge(s["diag_ready"], turn(s["diag_ready"]))
                pe.matmul(PB[2][:, 0:QS], kc("blk"), sm[:, 0:4], start=True, stop=True).then_inc(s["tr_ps"], 1)

                def product(bank, a_, b_):
                    for s4 in range(QS):
                        for q in range(2):
                            r = slice(q * C, (q + 1) * C)
                            ins = pe.matmul(PB[bank][r, s4 * C:(s4 + 1) * C], a_[r, s4, :], b_[r, s4, :], start=True, stop=True)
                    return ins
                pe.wait_ge(s["ns_ready"], turn(s["ns_ready"]))
                product(3, nsA, nsZ).then_inc(s["ns_ps"], 1)
                for it in range(4):
                    pe.wait_ge(s["ns_ready"], turn(s["ns_ready"]))
                    product(4, nsZ, nsY).then_inc(s["ns_ps"], 1)
                    pe.wait_ge(s["ns_ready"], turn(s["ns_ready"]))
                    if it < 3:
                        product(5, nsW, nsZ)
                    product(3, nsY, nsW).then_inc(s["ns_ps"], 1)
                pe.wait_ge(s["ns_ready"], turn(s["ns_ready"]))
                for s4 in range(QS):
                    for q in range(2):
                        r = slice(q * C, (q + 1) * C)
                        ins = pe.matmul(PB[2][r, s4:s4 + 1], nsY[r, s4, :], onef[r, 0:1], start=True, stop=True)
                ins.then_inc(s["col_ps"], 1)
                gate_tail("c0", 16)

            def hidden(c, hr):
                pe.wait_ge(s["v_ready"], turn(s["v_ready"]))
                pe.matmul(PB[4][0:hr, 0:QS], sc(f"{c}w1"), sm[:, 20:24], start=True, stop=True).then_inc(s["hid_ps"], 1)
                pe.wait_ge(s["hid_ready"], turn(s["hid_ready"]))

            def spread(src, banks, kind):
                for k in range(NV):
                    m, part = divmod(k, 3)
                    if part == 1:
                        at = (kind * QS + 2 * m) * C
                        lhs = gx[:, at:at + P]
                    else:
                        c = 2 * m + part // 2
                        lhs = src[:, c:c + 1].broadcast_to([P, P])
                    i = kind * NV + k
                    ins = pe.matmul(PB[banks[i // 4]][:, (i % 4) * P:(i % 4 + 1) * P], lhs, ident, start=True, stop=True)
                return ins

            def gate_tail(c, hr):
                hidden(c, hr)
                pe.matmul(PB[5][:, 0:QS], sc(f"{c}w2", 0, hr), hid[0:hr, :], start=True, stop=True).then_inc(s["gate_ps"], 1)
                pe.wait_ge(s["gate_wide"], turn(s["gate_wide"]))
                spread(gate, (6, 7), 0).then_inc(s["gain_ps"], 1)

            def sums(cols, w):
                for j in range(QT):
                    ins = pe.matmul(PB[0][:, 0:w], pair(xn, j), kc(cols)[:, j * w:(j + 1) * w], start=(j == 0), stop=(j == QT - 1))
                return ins

            def conv1():
                sums("ind", QS).then_inc(s["pool_ps"], 1)
                hidden("c1", 16)
                for k in range(4):
                    ins = pe.matmul(PB[5][:, k * QS:(k + 1) * QS], sc("c1w2", 0, 16)[:, k * P:(k + 1) * P], hid[0:16, :],
                                    start=True, stop=True)
                ins.then_inc(s["out4_ps"], 1)
                pe.wait_ge(s["par_ready"], turn(s["par_ready"]))
                for k in range(4):
                    ins = spread(par[:, k, :], (0, 1, 2, 3, 6, 7), k)
                ins.then_inc(s["gain_ps"], 1)

            def conv2():
                sums("haar", QS * 4).then_inc(s["band_ps"], 1)
                pe.wait_ge(s["band_ready"], turn(s["band_ready"]))
                pe.matmul(PB[1][:, 0:16], wencb[:, :], sm[:, 0:16], start=True, stop=True).then_inc(s["z_ps"], 1)
                gate_tail("c2", C)

            def conv3():
                transposes(lambda j: pair(xn, j), s["t_ps"], None, None)
                pe.wait_ge(s["t_done"], turn(s["t_done"], len(TB)))
                pe.wait_ge(s["conv_done"], turn(s["conv_done"]))
                flat = tmp[:, :, :].rearrange("p t c -> p (t c)")
                transposes(lambda j: flat[:, j * P:(j + 1) * P], s["res_ps"], None, None)

            def route(l, h):
                pe.wait_ge(s["applied"], n_of(l, h) + 1)
                pe.wait_ge(s["xn_ready"], 2 * (n_of(l, h) + 1))
                transposes(lambda j: pair(xn, j), s["t_ps"], None, None)
                flat = tmp[:, :, :].rearrange("p t c -> p (t c)")
                for b, (j0, j1) in enumerate(TB):
                    pe.wait_ge(s["t_done"], turn(s["t_done"]))
                    for j in range(j0, j1):
                        ins = pe.matmul(PB[5][:, j * 16:(j + 1) * 16], flat[:, j * P:(j + 1) * P], sc(f"r{l}"),
                                        start=True, stop=True)
                ins.then_inc(s["logits_ps"], 1)
                pe.wait_ge(s["onehot_ready"], turn(s["onehot_ready"]))
                pe.matmul(PB[6][:, 0:E * NT], tri16[:, :], mt[:, :], start=True, stop=True)
                pe.matmul(PB[7][:, 0:E * NT], one16[:, :], mt[:, :], start=True, stop=True).then_inc(s["rank_ps"], 1)

            def prep(l, h):
                n = n_of(l, h)
                pe.wait_ge(s["xn_ready"], 2 * n + 1)
                if n > 0:
                    pe.wait_ge(s["route_ready"], n)
                (conv0, conv1, conv2, conv3)[l]()
                route(l, h)

            stage_n = [2, 2]

            def wprep(l):
                nonlocal_lo = turn(s["w_lo"], 0)
                for k in range(2):
                    stage_n[k] += NCH
                    pe.wait_ge(s[f"stage_ld{k}"], 16 * stage_n[k])
                    vv = stage[k][0:CH, :].rearrange("p (k e c) -> p e k c", k=NCH, e=E)
                    for b in range(12):
                        if k * 12 + b >= 4:
                            pe.wait_ge(s["w_lo"], nonlocal_lo + k * 12 + b - 3)
                        for i in range(4):
                            e, c = divmod(4 * b + i, NCH)
                            for q in range(2):
                                ins = pe.matmul(PB[b % 4][q * C:(q + 1) * C, i * CH:(i + 1) * CH], vv[:, e, c, :],
                                                ident[0:CH, 0:CH], start=True, stop=True)
                        ins.then_inc(s["wt_ps"], 1)
                    pe.wait_ge(s["wt_ps"], turn(s["wt_ps"], 12))
                    pe.matmul(PB[7][0:1, 0:1], onef[:, 0:1], onef[:, 0:1], start=True, stop=True).then_inc(s["stage_used"], 1)
                for k in range(2):
                    stage_n[k] += 1
                    pe.wait_ge(s[f"stage_ld{k}"], 16 * stage_n[k])
                    for b in range(3):
                        n = 3 * k + b
                        if n >= 2:
                            pe.wait_ge(s["w_lo"], nonlocal_lo + 24 + n - 1)
                        for i in range(8):
                            e, c = divmod(8 * b + i, NSP) if b < 2 else (i // NFU, NSP + i % NFU)
                            src = stage[k][0:C, e * H2 + CH_AT[c]:e * H2 + CH_AT[c] + CH]
                            ins = pe.transpose(PB[4 + n % 2][0:CH, i * C:(i + 1) * C], src, ident[0:C, 0:C])
                        ins.then_inc(s["wt_ps"], 1)
                    pe.wait_ge(s["wt_ps"], turn(s["wt_ps"], 3))
                    pe.matmul(PB[7][0:1, 0:1], onef[:, 0:1], onef[:, 0:1], start=True, stop=True).then_inc(s["stage_used"], 1)
                turn(s["w_lo"], 31)
                pe.wait_ge(s["w_lo"], nonlocal_lo + 31)

            def moe(l, h):
                n, tb, gb = n_of(l, h), tile_base(l, h), group_base(l, h)
                g_ = G[l]
                g0 = group_base(2, 0)
                width = (H0, H1)[l] if l < 2 else 0

                def turn_rows(i, k, t):
                    r = (k + t) % UNROLL
                    pe.wait_ge(xs_ld[r], i * 16 + 16 * (LOOPS * n + 1 + (k + t) // UNROLL))
                    wait_from(pe, s["xT_done"], i * UNROLL + (tb + k + t - 1), 0)
                    bank = PB[6 + r % 2][:, :].bitcast(FP16)
                    for u in range(SUB):
                        ins = pe.transpose(bank[:, u * P:(u + 1) * P], xs[r][:, u * RW:u * RW + P], id16[:, :])
                    ins.then_inc(s["xT_ps"], 1)

                def up01(i, k, t, e):
                    r = (k + t) % UNROLL
                    pe.wait_ge(s["xT_done"], i * UNROLL + (tb + k + t + 1))
                    wait_from(pe, s["hp_ready"], i * UNROLL + (gb + k + t - 3), 0)
                    for c in range(l + 1):
                        o = slice(c * ROWS, (c + 1) * ROWS)
                        at = ds(e * width + c * P, P)
                        pe.matmul(PB[r][:, o], wA[l][:, at], xT[r][:, :], start=True, stop=False)
                        ins = pe.matmul(PB[r][:, o], wB[l][:, at], xT[r][:, :], start=False, stop=True)
                    ins.then_inc(s["h_ps"], 1)

                def down01(i, k, e):
                    pe.wait_ge(s["hp_ready"], i * UNROLL + (gb + k + 1))
                    wait_from(pe, s["y_done"], i * UNROLL + (tb + k - 1), 0)
                    for c in range(l + 1):
                        w = wD[l][:, ds(e * ((l + 1) * C) + c * C, C)]
                        for u in range(SUB):
                            col = c * ROWS + u * P
                            ins = pe.matmul(PB[4 + k % 2][:, u * C:(u + 1) * C], hid4[k][:, col:col + P], w,
                                            start=(c == 0 and u == 0), stop=(c == l), skip_group_check=True)
                    ins.then_inc(s["y_grp"], 1)

                def body01(i, last=False):
                    es = experts(pe, h, i, range(UNROLL if last else UNROLL + 2))
                    for k in range(UNROLL):
                        if not (last and k + AHEAD >= UNROLL):
                            turn_rows(i, k, AHEAD)
                        if not (last and k + 2 >= UNROLL):
                            up01(i, k, 2, es[k + 2])
                        down01(i, k, es[k])

                def up23(i, k, g, e):
                    q = k * g_ + g
                    if g == 0:
                        pe.wait_ge(s["xT_done"], i * UNROLL + (tb + k + 1))
                    wait_from(pe, s["prod_ready"], i * (UNROLL * g_) + (gb + q - 1 - group_base(2, 0)), 0)
                    for c in range(2):
                        for w, bank in (((gA, gB), q % 2), ((uA, uB), 2 + q % 2)):
                            o = slice(c * ROWS, (c + 1) * ROWS)
                            at = ds(e * (NCH * CH) + (2 * g + c) * CH, CH)
                            pe.matmul(PB[bank][0:CH, o], w[0][:, at], xT[k][:, :], start=True, stop=False)
                            ins = pe.matmul(PB[bank][0:CH, o], w[1][:, at], xT[k][:, :], start=False, stop=True)
                    ins.then_inc(s["h_ps"], 1)

                def down23(i, k, g, e):
                    if g < SPLIT:
                        pe.wait_ge(s["hp_ready"], i * (UNROLL * SPLIT) + (g0 + split_base(l, h) + k * SPLIT + g + 1))
                    else:
                        pe.wait_ge(s["prod_ready"], i * (UNROLL * g_) + (gb + k * g_ + g + 1 - g0))
                    if g == 0:
                        pe.wait_ge(s["y_done"], i * UNROLL + (tb + k - 1))
                    y = PB[4 + k % 2]
                    for c in range(2):
                        if g < SPLIT:
                            w = dW[:, ds(e * (NSP * 2 * C) + (2 * g + c) * 2 * C, 2 * C)]
                        else:
                            w = dF[:, ds(e * (NFU * C) + (2 * (g - SPLIT) + c) * C, C)]
                        for u in range(SUB):
                            col = c * ROWS + u * P
                            o = u * 2 * C
                            if g < SPLIT:
                                pe.matmul(y[:, o:o + 2 * C], hl[g][0:CH, col:col + P], w,
                                          start=(g == 0 and c == 0 and u == 0), stop=False, skip_group_check=True)
                                ins = pe.matmul(y[:, o:o + C], hl[g][0:CH, 2 * ROWS + col:2 * ROWS + col + P],
                                                w[:, 0:C], start=False, stop=False, skip_group_check=True)
                            else:
                                ins = pe.matmul(y[:, o:o + C], hold(k, g)[0:CH, col:col + P], w,
                                                start=False, stop=(c == 1), skip_group_check=True)
                    ins.then_inc(s["y_grp"], 1)

                def body23(i, first=False, last=False):
                    es = experts(pe, h, i, range(0 if first else -1, UNROLL))
                    for k in range(UNROLL):
                        if not (last and k + 2 >= UNROLL):
                            turn_rows(i, k, 2)
                        for g in range(g_):
                            up23(i, k, g, es[k])
                            if k > 0:
                                down23(i, k - 1, g, es[k - 1])
                            elif not first:
                                down23(i - 1, UNROLL - 1, g, es[-1])
                    if last:
                        for g in range(g_):
                            down23(i, UNROLL - 1, g, es[UNROLL - 1])

                pe.wait_ge(s["route_ready"], 2 * (l + 1))
                if l < 2:
                    for k in range(AHEAD):
                        turn_rows(0, k, 0)
                    es = experts(pe, h, 0, range(2))
                    for k in range(2):
                        up01(0, k, 0, es[k])
                    body01(0)
                    middle(pe, body01)
                    body01(LOOPS - 1, last=True)
                else:
                    turn_rows(0, 0, 0)
                    turn_rows(0, 1, 0)
                    body23(0, first=True)
                    middle(pe, body23)
                    body23(LOOPS - 1, last=True)

            pe.wait_ge(s["const_ld"], 16)
            for h in range(HALVES):
                pe.wait_ge(s["x_ld"], 32 * (h + 1))
                if h == 0:
                    pe.wait_ge(s["x_ld"], 64)
                src = (xn, tmp)[h][:, :, :].rearrange("p t c -> p (t c)")
                for b, (j0, j1) in enumerate(TB):
                    if h:
                        pe.wait_ge(s["xin_done"], b + 1)
                    for j in range(j0, j1):
                        ins = pe.transpose(PB[b][:, (j - j0) * P:(j - j0 + 1) * P], src[:, j * P:(j + 1) * P], ident)
                    ins.then_inc(s["xin_ps"], 1)
            pe.wait_ge(s["b_ld"], 16 * 10)
            pe.wait_ge(s["consts_done"], 1)
            pe.transpose(PB[5][:, 0:E], act[0][0:E, 0:P], ident[0:E, 0:E])
            pe.transpose(PB[5][:, 64:64 + 2 * E], act[1][0:2 * E, 0:P], ident[0:2 * E, 0:2 * E])
            pe.transpose(PB[5][:, 128:128 + E], act[0][0:E, P:2 * P], ident[0:E, 0:E])
            pe.transpose(PB[5][:, 128 + E:128 + 2 * E], act[1][0:E, P:2 * P], ident[0:E, 0:E]).then_inc(s["b_ps"], 1)
            pe.wait_ge(s["b_done"], 1)
            pe.wait_ge(s["stage_ld1"], 32)
            for e in range(E):
                for c in range(2):
                    at = e * H1 + c * P
                    ins = pe.matmul(PB[6][:, 2 * e + c:2 * e + c + 1], stage[1][0:C, at:at + P], lnT[0:C, E + e:E + e + 1],
                                    start=True, stop=True)
            ins.then_inc(s["l1b_ps"], 1)
            for l in range(NL):
                for h in range(HALVES):
                    prep(l, h)
                if l in (0, 3):
                    wprep(l)
                for h in range(HALVES):
                    moe(l, h)
            pe.wait_ge(s["y_done"], tile_base(NL, 0))
            for h in range(HALVES):
                pe.wait_ge(s["second_added"], 16 * NT * (n_of(NL - 1, h) + 1))
                if h:
                    pe.wait_ge(s["t_done"], turn(s["t_done"], len(TB)))
                transposes(lambda j: pair(x[h], j), s["t_ps"], None, None)


_NAMES = ["x"] + [f"L0_conv_{n}" for n in ("w1", "b1", "w2", "b2")] + \
    [f"L0_ffn_{n}" for n in ("gate_w", "gate_b", "W1", "b1", "W2", "b2")] + \
    [f"L1_conv_{n}" for n in ("w1", "b1", "w2", "b2")] + \
    [f"L1_ffn_{n}" for n in ("Wr", "br", "ln_g", "ln_b", "W1", "b1", "W2", "b2")] + \
    [f"L2_conv_{n}" for n in ("w1", "w2", "w_enc", "b_enc")] + [f"L2_ffn_{n}" for n in ("router_w", "w1", "w2", "w3")] + \
    ["L3_conv_weight", "L3_conv_bias"] + [f"L3_ffn_{n}" for n in ("router_w", "w1", "w2", "w3")]


def kernel(**inputs):
    import concourse.bacc as bacc
    from concourse.bass_utils import run_bass_kernel_spmd

    nc = bacc.Bacc("TRN2", target_bir_lowering=False, num_devices=1)
    arrays, aps = {}, {}
    for name in _NAMES:
        arr = np.ascontiguousarray(inputs[name])
        arrays[f"in_{name}"] = arr
        aps[name] = nc.dram_tensor(f"in_{name}", arr.shape, mybir.dt.from_np(arr.dtype), kind="ExternalInput").ap()
    k = constants()
    arrays["konst"] = k
    konst = nc.dram_tensor("konst", k.shape, FP32, kind="ExternalInput").ap()
    out = nc.dram_tensor("out", (B, C, HW, HW), FP32, kind="ExternalOutput").ap()
    program(nc, aps, konst, out)
    r = run_bass_kernel_spmd(nc, [arrays], core_ids=[0])
    return r.results[0]["out"]
```

```python
import numpy as np
import concourse.bass as bass
from concourse import mybir
from contextlib import ExitStack

FP32 = mybir.dt.float32
FP16 = mybir.dt.float16
I32 = mybir.dt.int32
ALU = mybir.AluOpType
ACT = mybir.ActivationFunctionType
AX = mybir.AxisListType
ds = bass.ds

B, C, HW = 16, 64, 24
PIX = HW * HW
P = 128
HALVES = 2
HB = B // HALVES
QS = HB // 2
NTOK = HB * PIX
NT = NTOK // P
QT = NT // 2
E, TOPK = 8, 2
ROWS = 256
SUB = ROWS // P
UNROLL = 4
JOIN = 3
TILES = -(-((TOPK * NTOK + E * (ROWS - 1)) // ROWS) // UNROLL) * UNROLL
WORD = 7
MAXE = -(-NTOK // ROWS)
AHEAD = 3
WSCALE = 16.0
RW = 2 * C + 2
H0, H1, H2 = 128, 256, 682
CH = 114
NCH = 6
CH_AT = [c * CH for c in range(NCH - 1)] + [H2 - CH]
OVERLAP = NCH * CH - H2
SPLIT = 2
TBANK = 4
TB = [(b * TBANK, min(QT, (b + 1) * TBANK)) for b in range(-(-QT // TBANK))]
EPS_C, EPS_T = 1e-6, 1e-5
BIG = 1e30

_K = {}
_at = 0
for _n, _w in (("ident", P), ("tri", P), ("blk", P), ("i2", C), ("haar", QT * QS * 4), ("ind", QT * QS),
               ("mask", 2), ("e8", E), ("k4", 4), ("tile", TILES + WORD - UNROLL), ("thr", MAXE)):
    _K[_n] = (_at, _w)
    _at += _w
KCOLS = _at


def constants():
    k = np.zeros((P, KCOLS), np.float32)
    p = np.arange(P)

    def put(name, a):
        k[:, _K[name][0]:_K[name][0] + _K[name][1]] = np.asarray(a, np.float32).reshape(-1, _K[name][1])
    put("ident", np.eye(P))
    put("tri", p[:, None] < p[None, :])
    put("blk", (p[:, None] // C) == (p[None, :] // C))
    put("i2", (p[:, None] % C) == np.arange(C)[None, :])
    tok = np.arange(QT)[None, :] * P + p[:, None]
    s, pix = tok // PIX, tok % PIX
    r, c = (pix // HW) % 2, pix % 2
    sr, sc = 2 * r - 1, 2 * c - 1
    sign = np.stack([np.ones_like(r), sc, sr, sr * sc], -1)
    own = s[:, :, None] == np.arange(QS)
    put("haar", own[:, :, :, None] * sign[:, :, None, :])
    put("ind", own)
    put("mask", np.stack([p < P // 2, p >= P // 2], -1))
    put("e8", (E - np.arange(E))[None])
    put("k4", (4 - np.arange(4))[None])
    put("tile", np.arange(TILES + WORD - UNROLL)[None] - 1)
    put("thr", (np.arange(MAXE) * ROWS)[None])
    return k


_S = {}
_at = 0
for _n, _w in (("c0w1", 16), ("c0w2", P), ("c0b1", 1), ("c0b2", 1), ("c1w1", 16), ("c1w2", 4 * P), ("c1b1", 1),
               ("c1b2", 4), ("c2w1", C), ("c2w2", P), ("c2we", 1), ("c2be", 1), ("c3w", 9), ("c3b", 1),
               ("r0", 16), ("r1", 16), ("r2", 16), ("r3", 16), ("rb0", E), ("rb1", E)):
    _S[_n] = (_at, _w)
    _at += _w
SCOLS = _at


class Turn:

    def __init__(self):
        self.n = {}

    def __call__(self, sem, by=1):
        self.n[id(sem)] = self.n.get(id(sem), 0) + by
        return self.n[id(sem)]


def program(nc, I, konst, out):
    ctx = ExitStack()
    with ctx:
        def sb(name, shape, dt=FP32):
            return ctx.enter_context(nc.sbuf_tensor(name, shape, dt))

        def sem(name):
            return ctx.enter_context(nc.semaphore(name))

        rows_d = [nc.dram_tensor(f"rows_{h}", [TILES * ROWS, RW // 2], I32).ap() for h in range(HALVES)]
        y_d = [nc.dram_tensor(f"y_{h}", [TILES * ROWS, C], FP32).ap() for h in range(HALVES)]

        K = sb("K", [P, KCOLS])
        S = sb("S", [P, SCOLS])
        x = [sb(f"x{h}", [P, NT, C]) for h in range(HALVES)]
        xn = sb("xn", [P, NT, C])
        tmp = sb("tmp", [P, NT, C])
        rowsb = [sb(f"rowsb{h}", [P, NT, RW], FP16) for h in range(HALVES)]
        w01 = sb("w01", [P, 2 * E * (H0 + H1)], FP16)
        wA = {0: w01[:, 0:E * H0], 1: w01[:, 2 * E * H0:2 * E * H0 + E * H1]}
        wB = {0: w01[:, E * H0:2 * E * H0], 1: w01[:, 2 * E * H0 + E * H1:]}
        wD = {0: sb("w0d", [P, E * 2 * C], FP16), 1: sb("w1d", [P, E * 4 * C], FP16)}
        b1T = {0: sb("b1T0", [P, E]), 1: sb("b1T1", [P, 2 * E])}
        b2R = {0: sb("b2R0", [P, E * C]), 1: sb("b2R1", [P, E * C])}
        gA, gB = sb("gA", [P, E * NCH * CH], FP16), sb("gB", [P, E * NCH * CH], FP16)
        uA, uB = sb("uA", [P, E * NCH * CH], FP16), sb("uB", [P, E * NCH * CH], FP16)
        NSP, NFU = 2 * SPLIT, NCH - 2 * SPLIT
        dW = sb("dW", [CH, E * NSP * 2 * C], FP16)
        dV = dW[:, :].rearrange("p (k s c) -> p k s c", s=2, c=C)
        dF = sb("dF", [CH, E * NFU * C])
        stage = [sb(f"stage{i}", [P, E * NCH * C]) for i in range(2)]
        lnT = sb("lnT", [P, 2 * E])
        id16, tri16, one16 = (sb(n, [P, P], FP16) for n in ("id16", "tri16", "one16"))
        onef = sb("onef", [P, 2])
        i15 = sb("i15", [P, C])
        wencb = sb("wencb", [P, P])
        st = sb("st", [P, 8, NT])
        lg, eq, k1, k2 = (sb(n, [P, NT, E]) for n in ("lg", "eq", "k1", "k2"))
        ex = sb("ex", [P, NT * E + NT])
        mt = sb("mt", [P, E * NT], FP16)
        incl = sb("incl", [P, E, NT])
        r8 = sb("r8", [P, 6, E])
        spare = tmp[:, :, :].rearrange("p t c -> p (t c)")
        cmp_ = spare[:, 0:E * MAXE]
        NEID = TILES + WORD - UNROLL
        eidf = spare[0:1, E * MAXE:(MAXE + NEID) * E]
        eidr = spare[0:1, (MAXE + NEID) * E:(MAXE + NEID) * E + NEID]
        eidw = spare[0:1, (MAXE + NEID) * E + NEID:(MAXE + NEID) * E + NEID + TILES // UNROLL]
        eid = [sb(f"eid{h}", [1, TILES // UNROLL], I32) for h in range(HALVES)]
        pos = [sb(f"pos{h}", [P, TOPK, NT], I32) for h in range(HALVES)]
        gts = [sb(f"gts{h}", [P, TOPK, NT]) for h in range(HALVES)]
        mx = sb("mx", [P, 2, 4, C])
        srow = sb("srow", [1, 2, HB * C])
        nsW = sb("nsW", [P, QS, C])
        sm = sb("sm", [P, 64])
        mid = sb("mid", [P, QS])
        gate = sb("gate", [P, QS])
        par = sb("par", [P, 4, QS])
        gx = sb("gx", [P, 4 * QS * C])
        nsA, nsY, nsZ = (gx[:, k * QS * C:(k + 1) * QS * C].rearrange("p (s c) -> p s c", c=C) for k in (1, 2, 3))
        xs = [sb(f"xs{i}", [P, SUB * RW], FP16) for i in range(UNROLL)]
        xT = [sb(f"xT{i}", [P, ROWS], FP16) for i in range(UNROLL)]
        gt = [sb(f"gt{i}", [P, SUB]) for i in range(UNROLL)]
        act = [sb(f"act{i}", [P, 2 * ROWS]) for i in range(2)]
        hb = [sb(f"hb{i}", [P, 2 * ROWS]) for i in range(2)]
        prod = act + hb
        hl = [sb(f"hl{i}", [P, 4 * ROWS], FP16) for i in range(SPLIT)]
        hid = hb
        w2_in = {0: stage[0][:, E * H0:E * (H0 + C)], 1: stage[0][:, E * (H0 + C):E * (H0 + 3 * C)]}
        hid_hl = [t[:, :] for t in hl] + [t[:, :].bitcast(FP16) for t in act]
        yb = [sb(f"yb{i}", [P, SUB * C]) for i in range(2)]
        ysb = [sb(f"ysb{i}", [P, SUB * C]) for i in range(UNROLL)]
        PW = HW + 2
        pad = w01[:, 0:2 * QS * PW * PW].bitcast(FP32).rearrange("p (s a b) -> p s a b", s=QS, a=PW)
        PB = [ctx.enter_context(nc.psum_tensor(f"bank{i}", [P, 512], FP32)) for i in range(8)]

        def kc(name, rows=P):
            return K[0:rows, _K[name][0]:_K[name][0] + _K[name][1]]

        def sc(name, p0=0, p1=P):
            return S[p0:p1, _S[name][0]:_S[name][0] + _S[name][1]]

        ident = kc("ident")

        PARTS = [(0, 4 * TBANK), (4 * TBANK, NT)]
        NP = len(PARTS)

        names = ("const_ld small_ld zeroed rows_zero x_ld0 x_ld1 dve_chain consts_done xin_ps xin_done centred squared "
                 "var_ready std_ready xn_ready mixed_ready sums_ps rows_ready cov_ps diag_ready tr_ps normv_ready "
                 "norm_root ns_ready ns_ps col_ps v_ready hid_ps hid_ready gate_ps gate_ready gain_ps applied "
                 "pool_ps out4_ps out4_ready gate_wide par_ready band_ps band_ready z_ps z_ready t_ps t_done "
                 "split_hi logits_ps logit_shift exp_ready onehot_ready rank_ps pos_ready route_ready first_sent second_gate second_sent "
                 "first_added xT_ps xT_done h_ps s_ready hp_ready y_grp y_done "
                 "stage_ld0 stage_ld1 stage_used wt_ps w_hi w_lo gelu_ready prod_ready hi_ready conv_done res_ps stored "
                 "b_ld b_ps b_done l1b_ps w01_done table_zero").split()
        s = {n: sem(n) for n in names}
        xs_ld = [sem(f"xs_ld{i}") for i in range(UNROLL)]
        second_added = [sem(f"second_added{p}") for p in range(NP)]
        y_st = [sem(f"y_st{i}") for i in range(UNROLL)]

        block = ctx.enter_context(nc.Block())

        NL = 4
        WT_BANKS = 30

        def wt_after(k):
            return 6 * (k + 1) if 0 <= k < 4 else 24 + 3 * (k - 3) if k >= 4 else 3 * (k + 1)

        SMALL = 16 * (2 * 20 + 3)
        NZERO = HALVES * -(-(TILES * ROWS // P * RW) // (NT * RW))
        G = [1, 1, 3, 3]
        order = [(l, h) for l in range(NL) for h in range(HALVES)]

        def n_of(l, h):
            return l * HALVES + h

        def group_base(l, h):
            return sum(G[a] * TILES for a, b in order[:n_of(l, h)])

        def tile_base(l, h):
            return n_of(l, h) * TILES

        LOOPS = TILES // UNROLL
        assert (LOOPS - 2) % JOIN == 0

        def experts(eng, h, i, tiles=range(-1, WORD - 1)):
            w = eng.value_load(eid[h][0:1, ds(i, 1)], min_val=0, max_val=E ** WORD - 1)
            return {k: eng.snap((w >> (3 * (k + 1))) & (E - 1), min_val=0, max_val=E - 1) for k in tiles}

        def middle(eng, body):
            with eng.Fori(0, (LOOPS - 2) // JOIN) as i:
                for j in range(JOIN):
                    body(i * JOIN + (j + 1))

        def split_base(l, h):
            return (n_of(l, h) - n_of(2, 0)) * TILES * SPLIT

        def hold(k, g):
            return prod[g if g < SPLIT else SPLIT + k % 2]

        def wait_from(eng, semaphore, value):
            if not isinstance(value, int) or value > 0:
                eng.wait_ge(semaphore, value)

        def pieces(q, s4):
            m = s4 // 2
            if s4 % 2 == 0:
                return [xn[:, 2 * (9 * m + t) + q, :] for t in range(4)] + [mx[:, 0, 2 * m + q, :]]
            return [mx[:, 1, 2 * m + q, :]] + [xn[:, 2 * (9 * m + 5 + t) + q, :] for t in range(4)]

        def pair(t, j):
            return t[:, 2 * j:2 * j + 2, :].rearrange("p q c -> p (q c)")

        def words(h):
            return rowsb[h][:, :, :].rearrange("p t c -> p (t c)").bitcast(I32)

        def gate_column(h):
            return words(h).bitcast(FP32).rearrange("p (t c) -> p t c", c=RW // 2)[:, :, RW // 2 - 1]

        def gain_view(v):
            m, k = divmod(v, 3)
            t0 = 9 * m + (0, 4, 5)[k]
            return t0, t0 + (4, 1, 4)[k]

        NV = 6
        GAIN_BANKS = [(6, 7), (0, 1), (2, 3), (4, 5)]

        def small_weights():
            small, later = [], []
            for q in range(2):
                cq, hq = slice(q * C, (q + 1) * C), slice(q * 8, (q + 1) * 8)
                small += [
                    (sc("c0w1")[cq, hq], I["L0_conv_w1"].rearrange("o c -> c o")),
                    (sc("c0w2")[hq, cq], I["L0_conv_w2"].rearrange("c o -> o c")),
                    (sc("c0b1")[hq, :], I["L0_conv_b1"].rearrange("(c o) -> c o", o=1)),
                    (sc("c0b2")[cq, :], I["L0_conv_b2"].rearrange("(c o) -> c o", o=1)),
                    (sc("r0")[cq, hq], I["L0_ffn_gate_w"]),
                ]
                later += [
                    (sc("c1w1")[cq, hq], I["L1_conv_w1"].rearrange("o c -> c o")),
                    (sc("c1b1")[hq, :], I["L1_conv_b1"].rearrange("(c o) -> c o", o=1)),
                    (sc("c1b2")[cq, :].rearrange("p (k t) -> p k t", k=2), I["L1_conv_b2"].rearrange("k (c t) -> c k t", t=2)),
                    (sc("c2w1")[cq, q * 32:(q + 1) * 32], I["L2_conv_w1"].rearrange("o c -> c o")),
                    (sc("c2w2")[q * 32:(q + 1) * 32, cq], I["L2_conv_w2"].rearrange("c o -> o c")),
                    (sc("c2we")[cq, :], I["L2_conv_w_enc"].rearrange("o c -> c o")),
                    (sc("c3w")[cq, :], I["L3_conv_weight"].rearrange("c o a b -> c (o a b)")),
                    (sc("c3b")[cq, :], I["L3_conv_bias"].rearrange("(c o) -> c o", o=1)),
                    (sc("r1")[cq, hq], I["L1_ffn_Wr"]),
                    (sc("r2")[cq, hq], I["L2_ffn_router_w"].rearrange("e c -> c e")),
                    (sc("r3")[cq, hq], I["L3_ffn_router_w"].rearrange("e c -> c e")),
                ]
                for k in range(2):
                    for t in range(2):
                        v = sc("c1w2")[hq, (2 * k + t) * P + q * C:(2 * k + t) * P + (q + 1) * C]
                        later.append((v, I["L1_conv_w2"][k].rearrange("(c t) h -> t h c", t=2)[t]))
            small.append((sc("rb0"), I["L0_ffn_gate_b"].partition_broadcast(P)))
            later.append((sc("c2be"), I["L2_conv_b_enc"].partition_broadcast(P)))
            later.append((sc("rb1"), I["L1_ffn_br"].partition_broadcast(P)))
            return small, later

        @block.sync
        def _(sp):
            turn = Turn()
            sp.dma_start(K[:, :], konst).then_inc(s["const_ld"], 16)
            for h in range(HALVES):
                for q in range(2):
                    b0 = h * HB + q * QS
                    dst = (xn, tmp)[h][q * C:(q + 1) * C, :, :].rearrange("p t c -> p (t c)").rearrange(
                        "p (s n) -> p s n", s=QS)
                    sp.dma_start(dst, I["x"][b0:b0 + QS].rearrange("s c a b -> c s (a b)")).then_inc(s[f"x_ld{h}"], 16)
            for l in (0, 1):
                sp.dma_start(w2_in[l].rearrange("p (e k c) -> p e k c", e=E, c=C),
                             I[f"L{l}_ffn_W2"].rearrange("e (k p) c -> p e k c", p=P)).then_inc(s["b_ld"], 16)
                sp.dma_start(b2R[l][:, :], I[f"L{l}_ffn_b2"].rearrange("e c -> (e c)").partition_broadcast(P)
                             ).then_inc(s["b_ld"], 16)
            sp.dma_start(act[0][0:E, 0:P], I["L0_ffn_b1"]).then_inc(s["b_ld"], 16)
            sp.dma_start(act[1][0:2 * E, 0:P], I["L1_ffn_b1"].rearrange("e (k p) -> (e k) p", p=P)).then_inc(s["b_ld"], 16)
            for d in range(2):
                sp.dma_start(act[0][0:E, P + d * C:P + (d + 1) * C], I["L1_ffn_ln_g"]).then_inc(s["b_ld"], 16)
                sp.dma_start(act[1][0:E, P + d * C:P + (d + 1) * C], I["L1_ffn_ln_b"]).then_inc(s["b_ld"], 16)
            for l, w in ((0, H0), (1, H1)):
                for d in range(2):
                    sp.dma_start(stage[l][d * C:(d + 1) * C, 0:E * w].rearrange("p (e n) -> p e n", e=E),
                                 I[f"L{l}_ffn_W1"].rearrange("e d n -> d e n")).then_inc(s[f"stage_ld{l}"], 16)

            def load_stage(l, pieces):
                for k in pieces:
                    if l == 2 and k < 2:
                        sp.wait_ge(s["stage_used"], 2)
                    else:
                        sp.wait_ge(s["wt_ps"], (l - 2) * WT_BANKS + wt_after(k - 2))
                    if k < 4:
                        w = I[f"L{l}_ffn_{('w1', 'w3')[k // 2]}"][4 * (k % 2):4 * (k % 2 + 1)]
                        v = stage[k % 2][0:CH, :].rearrange("p (k e d c) -> p k e d c", k=NCH, e=4, d=2)
                        for c in range(NCH):
                            for d in range(2):
                                sp.dma_start(v[:, c, :, d, :], w[:, CH_AT[c]:CH_AT[c] + CH, :].rearrange("e p c -> p e c")
                                             ).then_inc(s[f"stage_ld{k % 2}"], 16)
                    else:
                        w = I[f"L{l}_ffn_w2"][4 * (k - 4):4 * (k - 3)]
                        sp.dma_start(stage[k % 2][0:C, 0:4 * H2].rearrange("p (e n) -> p e n", e=4),
                                     w.rearrange("e c n -> c e n")).then_inc(s[f"stage_ld{k % 2}"], 16)
            sp.wait_ge(s["zeroed"], 1)
            for dst, src in small_weights()[1]:
                sp.dma_start(dst, src, allow_slow_non_contiguous=True).then_inc(s["small_ld"], 16)
            load_stage(2, range(2))

            def moe(l, h):
                n, tb = n_of(l, h), tile_base(l, h)
                ahead = AHEAD if l < 2 else 2

                def load(t, i, k):
                    r = (k + t) % UNROLL
                    wait_from(sp, s["xT_done"], i * UNROLL + (tb + k + t - UNROLL + 1))
                    sp.dma_start(xs[r][:, :].bitcast(I32), rows_d[h][ds((i * UNROLL + (k + t)) * ROWS, ROWS), :].rearrange(
                        "(p s) c -> p (s c)", s=SUB)).then_inc(xs_ld[r], 16)

                def store(i, k):
                    sp.wait_ge(s["y_done"], i * UNROLL + (tb + k + 1))
                    sp.dma_start(y_d[h][ds((i * UNROLL + k) * ROWS, ROWS), :].rearrange(
                        "(p s) c -> p (s c)", s=SUB), ysb[k][:, :]).then_inc(y_st[k], 16)
                sp.wait_ge(s["first_sent"], 16 * NT * (n + 1))
                sp.wait_ge(s["second_sent"], 16 * NT * (n + 1))
                for k in range(UNROLL):
                    load(0, 0, k)
                for k in range(ahead):
                    load(UNROLL, 0, k)

                def body(i, first=False, last=False):
                    for k in range(UNROLL):
                        if not (last and k + ahead >= UNROLL):
                            load(UNROLL + ahead, i, k)
                        if k > 0:
                            store(i, k - 1)
                        elif not first:
                            store(i - 1, UNROLL - 1)
                body(0, first=True)
                with sp.Fori(1, LOOPS - 2) as i:
                    body(i)
                body(LOOPS - 2, last=True)
                for k in range(UNROLL + 1):
                    store(*divmod((LOOPS - 1) * UNROLL - 1 + k, UNROLL))

            for l in range(NL):
                if l == 3:
                    load_stage(3, range(2, 6))
                for h in range(HALVES):
                    moe(l, h)
                if l == 0:
                    load_stage(2, range(2, 6))
                    load_stage(3, range(2))
            for h in range(HALVES):
                for q in range(2):
                    b0 = h * HB + q * QS
                    sp.wait_ge(s["t_done"], (NL * HALVES + HALVES + h + 1) * len(TB))
                    src = (xn, tmp)[h][q * C:(q + 1) * C, :, :].rearrange("p t c -> p (t c)").rearrange(
                        "p (s n) -> p s n", s=QS)
                    sp.dma_start(out[b0:b0 + QS].rearrange("s c a b -> c s (a b)"), src).then_inc(s["stored"], 16)
            sp.wait_ge(s["stored"], 16 * 2 * HALVES)

        @block.gpsimd
        def _(pool):
            pool.memset(S[:, :], 0.0).then_inc(s["zeroed"], 1)
            pool.memset(rowsb[0][:, :, :], 0.0).then_inc(s["rows_zero"], 1)
            pool.memset(onef[:, :], 1.0).then_inc(s["rows_zero"], 1)
            pool.wait_ge(s["rows_zero"], 2)
            for h in range(HALVES):
                pool.wait_ge(s[f"x_ld{h}"], 32)
            for h in range(HALVES):
                flat = rows_d[h].rearrange("(p r) c -> p (r c)", p=P)
                per = TILES * ROWS // P * (RW // 2)
                for a in range(0, per, NT * RW // 2):
                    w = min(NT * RW // 2, per - a)
                    pool.dma_start(flat[:, a:a + w], words(0)[:, 0:w]).then_inc(s["table_zero"], 16)
            pool.wait_ge(s["table_zero"], 16 * NZERO)

            def scatter(l, h):
                n = n_of(l, h)
                pool.wait_ge(s["pos_ready"], n + 1)
                for j in range(NT):
                    pool.indirect_dma_start(rows_d[h], bass.IndirectOffsetOnAxis(pos[h][:, 0, j:j + 1], 0),
                                            words(h)[:, j * RW // 2:(j + 1) * RW // 2], None).then_inc(s["first_sent"], 16)
                pool.wait_ge(s["first_sent"], 16 * NT * (n + 1))
                pool.tensor_copy(gate_column(h), gts[h][:, 1, :]).then_inc(s["second_gate"], 1)
                pool.wait_ge(s["second_gate"], n + 1)
                for j in range(NT):
                    pool.indirect_dma_start(rows_d[h], bass.IndirectOffsetOnAxis(pos[h][:, 1, j:j + 1], 0),
                                            words(h)[:, j * RW // 2:(j + 1) * RW // 2], None).then_inc(s["second_sent"], 16)

            def gather(l, h):
                n = n_of(l, h)
                for k in range(UNROLL):
                    pool.wait_ge(y_st[k], 16 * LOOPS * (n + 1))
                for j in range(NT):
                    pool.indirect_dma_start(x[h][:, j, :], None, y_d[h], bass.IndirectOffsetOnAxis(pos[h][:, 0, j:j + 1], 0),
                                            compute_op=ALU.add).then_inc(s["first_added"], 16)
                pool.wait_ge(s["first_added"], 16 * NT * (n + 1))
                for p, (t0, t1) in enumerate(PARTS):
                    for j in range(t0, t1):
                        pool.indirect_dma_start(x[h][:, j, :], None, y_d[h], bass.IndirectOffsetOnAxis(pos[h][:, 1, j:j + 1], 0),
                                                compute_op=ALU.add).then_inc(second_added[p], 16)
            for l in range(NL):
                for h in range(HALVES):
                    scatter(l, h)
                for h in range(HALVES):
                    gather(l, h)

        @block.scalar
        def _(a):
            turn = Turn()

            def ln():
                for t0, t1 in PARTS:
                    a.wait_ge(s["centred"], turn(s["centred"]))
                    a.activation(tmp[:, t0:t1, :], xn[:, t0:t1, :], ACT.Square).then_inc(s["squared"], 1)
                a.wait_ge(s["var_ready"], turn(s["var_ready"]))
                a.activation(st[:, 3, :], st[:, 2, :], ACT.Sqrt).then_inc(s["std_ready"], 1)

            def gate_tail(hr, b1, b2, w):
                a.wait_ge(s["hid_ps"], turn(s["hid_ps"]))
                if b1 is None:
                    a.activation(mid[0:hr, :], PB[4][0:hr, 0:QS], ACT.Relu).then_inc(s["hid_ready"], 1)
                else:
                    a.activation(mid[0:hr, :], PB[4][0:hr, 0:QS], ACT.Relu, bias=b1[0:hr, :]).then_inc(s["hid_ready"], 1)
                a.wait_ge(s["gate_ps"], turn(s["gate_ps"]))
                if b2 is None:
                    a.activation(gate[:, :], PB[5][:, 0:QS], ACT.Sigmoid).then_inc(s["gate_ready"], 1)
                else:
                    a.activation(gate[:, :], PB[5][:, 0:QS], ACT.Sigmoid, bias=b2).then_inc(s["gate_ready"], 1)

            def conv(l):
                if l == 0:
                    a.wait_ge(s["normv_ready"], turn(s["normv_ready"]))
                    a.activation(sm[:, 12:16], sm[:, 8:12], ACT.Sqrt).then_inc(s["norm_root"], 1)
                    gate_tail(16, sc("c0b1"), sc("c0b2"), None)
                elif l == 1:
                    a.wait_ge(s["hid_ps"], turn(s["hid_ps"]))
                    a.activation(mid[0:16, :], PB[4][0:16, 0:QS], ACT.Relu, bias=sc("c1b1")[0:16, :]).then_inc(s["hid_ready"], 1)
                    a.wait_ge(s["out4_ps"], turn(s["out4_ps"]))
                    for k in range(4):
                        ins = a.activation(par[:, k, :], PB[5][:, k * QS:(k + 1) * QS], ACT.Sigmoid,
                                           bias=sc("c1b2")[:, k:k + 1])
                    ins.then_inc(s["out4_ready"], 1)
                elif l == 2:
                    a.wait_ge(s["z_ps"], turn(s["z_ps"]))
                    a.activation(sm[:, 16:32], PB[1][:, 0:16], ACT.Sigmoid, bias=sc("c2be")).then_inc(s["z_ready"], 1)
                    gate_tail(C, None, None, None)

            def prep(l, h):
                ln()
                if n_of(l, h) == 0:
                    a.wait_ge(s["small_ld"], SMALL)
                conv(l)
                ln()
                for p, (t0, t1) in enumerate(PARTS):
                    a.wait_ge(s["xn_ready"], 2 * NP * n_of(l, h) + NP + p + 1)
                    a.activation(rowsb[h][:, t0:t1, 0:C], xn[:, t0:t1, :], ACT.Copy).then_inc(s["split_hi"], 1)
                a.wait_ge(s["logit_shift"], turn(s["logit_shift"]))
                a.activation(ex[:, :], ex[:, :], ACT.Exp).then_inc(s["exp_ready"], 1)

            def wprep():
                for k in range(2):
                    for b in range(12):
                        a.wait_ge(s["wt_ps"], turn(s["wt_ps"]))
                        dst = (gA, uA)[k][:, b * 4 * CH:(b + 1) * 4 * CH]
                        a.activation(dst, PB[b % 4][:, 0:4 * CH], ACT.Copy, scale=WSCALE).then_inc(s["w_hi"], 1)
                for k in range(2):
                    for b in range(2):
                        a.wait_ge(s["wt_ps"], turn(s["wt_ps"]))
                        a.activation(dV[:, (2 * k + b) * 8:(2 * k + b + 1) * 8, 0, :], PB[4 + (3 * k + b) % 2][0:CH, :].rearrange(
                            "p (k c) -> p k c", c=C), ACT.Copy, scale=WSCALE).then_inc(s["w_hi"], 1)
                    turn(s["wt_ps"])

            def moe01(l, h):
                gb = group_base(l, h)
                chunks = l + 1

                def body(i):
                    es = experts(a, h, i, range(UNROLL))
                    for k in range(UNROLL):
                        v = i * UNROLL + (gb + k)
                        a.wait_ge(s["h_ps"], v + 1)
                        wait_from(a, s["hp_ready"], v - 1)
                        wait_from(a, s["y_grp"], v - 3)
                        for c in range(chunks):
                            o = slice(c * ROWS, (c + 1) * ROWS)
                            b1 = b1T[l][:, ds(es[k] * chunks + c, 1)]
                            for dst in (hid[k % 2], hid_hl[k]):
                                ins = a.activation(dst[:, o], PB[k][:, o], ACT.Gelu, scale=1.0 / WSCALE, bias=b1)
                        ins.then_inc(s["gelu_ready"], 1)
                body(0)
                middle(a, body)
                body(LOOPS - 1)

            def moe23(l, h):
                gb, tb = group_base(l, h), tile_base(l, h)
                g0, sb_ = group_base(2, 0), split_base(l, h)

                def silu(i, k, g):
                    q = k * G[l] + g
                    w = i * (UNROLL * G[l]) + (gb + q)
                    a.wait_ge(s["h_ps"], w + 1)
                    if g < SPLIT:
                        a.wait_ge(s["hp_ready"], i * (UNROLL * SPLIT) + (g0 + sb_ + (k - 1) * SPLIT + g + 1))
                    else:
                        a.wait_ge(s["y_grp"], w + 1 - 2 * G[l])
                    a.activation(hold(k, g)[0:CH, :], PB[q % 2][0:CH, :], ACT.Silu, scale=1.0 / WSCALE
                                 ).then_inc(s["s_ready"], 1)

                def high(i, k, g):
                    w = i * (UNROLL * G[l]) + (gb + k * G[l] + g)
                    a.wait_ge(s["prod_ready"], w + 1 - g0)
                    a.wait_ge(s["y_grp"], w + 1 - G[l])
                    a.activation(hl[g][0:CH, 0:2 * ROWS], hold(k, g)[0:CH, :], ACT.Copy).then_inc(s["hi_ready"], 1)

                def take(i, k, t):
                    r = (k + t) % UNROLL
                    a.wait_ge(s["xT_ps"], i * UNROLL + (tb + k + t + 1))
                    a.wait_ge(s["y_done"], i * UNROLL + (tb + k + t - UNROLL + 1))
                    gv = xs[r][:, :].bitcast(FP32).rearrange("p (s c) -> p s c", s=SUB)[:, :, RW // 2 - 1]
                    a.activation(gt[r][:, :], gv, ACT.Copy, scale=1.0 / WSCALE ** 2)
                    a.activation(xT[r][:, :], PB[6 + r % 2][:, :].bitcast(FP16)[:, 0:ROWS], ACT.Copy
                                 ).then_inc(s["xT_done"], 1)

                def body(i, last=False):
                    for k in range(UNROLL):
                        for g in range(G[l]):
                            silu(i, k, g)
                            if g > 0:
                                high(i, k, g - 1)
                            if g == 1 and not (last and k + 2 >= UNROLL):
                                take(i, k, 2)
                take(0, 0, 0)
                take(0, 1, 0)
                body(0)
                middle(a, body)
                body(LOOPS - 1, last=True)

            def first_weights():
                for l, w in ((0, H0), (1, H1)):
                    if l == 0:
                        a.wait_ge(s["stage_ld0"], 32)
                    else:
                        a.wait_ge(s["w01_done"], 1)
                    a.activation(wA[l][:, :], stage[l][:, 0:E * w], ACT.Copy, scale=WSCALE).then_inc(s["w_hi"], 1)
                a.wait_ge(s["b_ld"], 16 * 10)
                for l in (0, 1):
                    a.activation(wD[l][:, :].rearrange("p (k s c) -> p k s c", s=2, c=C)[:, :, 0, :],
                                 w2_in[l].rearrange("p (k c) -> p k c", c=C), ACT.Copy, scale=WSCALE).then_inc(s["w_hi"], 1)

            a.wait_ge(s["zeroed"], 1)
            for dst, src in small_weights()[0]:
                a.dma_start(dst, src, allow_slow_non_contiguous=True).then_inc(s["small_ld"], 16)
            for l in range(NL):
                for h in range(HALVES):
                    prep(l, h)
                    if l == 0 and h == 0:
                        first_weights()
                if l == 3:
                    wprep()
                for h in range(HALVES):
                    (moe01 if l < 2 else moe23)(l, h)
                if l == 0:
                    wprep()

        @block.vector
        def _(v):
            turn = Turn()

            def link(ins):
                ins.then_inc(s["dve_chain"], 1)
                v.wait_ge(s["dve_chain"], turn(s["dve_chain"]))

            def bc(ap, m):
                return ap.unsqueeze(2).broadcast_to([ap.shape[0], ap.shape[1], m])

            def bt(ap, m):
                return ap.unsqueeze(1).broadcast_to([ap.shape[0], m, ap.shape[1]])

            def ln(xh, eps, added=None):
                for p, (t0, t1) in enumerate(PARTS):
                    if added is not None:
                        v.wait_ge(second_added[p], 16 * (t1 - t0) * (added + 1))
                    link(v.tensor_reduce(st[:, 0, t0:t1], xh[:, t0:t1, :], AX.X, ALU.add))
                    link(v.tensor_scalar(st[:, 1, t0:t1], st[:, 0, t0:t1], 1.0 / C, None, ALU.mult))
                    v.tensor_tensor(xn[:, t0:t1, :], xh[:, t0:t1, :], bc(st[:, 1, t0:t1], C), ALU.subtract
                                    ).then_inc(s["centred"], 1)
                for t0, t1 in PARTS:
                    v.wait_ge(s["squared"], turn(s["squared"]))
                    ins = v.tensor_reduce(st[:, 0, t0:t1], tmp[:, t0:t1, :], AX.X, ALU.add)
                link(ins)
                v.tensor_scalar(st[:, 2, :], st[:, 0, :], 1.0 / C, eps, ALU.mult, ALU.add).then_inc(s["var_ready"], 1)
                v.wait_ge(s["std_ready"], turn(s["std_ready"]))
                link(v.reciprocal(st[:, 4, :], st[:, 3, :]))
                link(v.tensor_tensor(st[:, 5, :], st[:, 4, :], st[:, 4, :], ALU.mult))
                link(v.tensor_tensor(st[:, 5, :], st[:, 5, :], st[:, 2, :], ALU.mult))
                link(v.tensor_scalar(st[:, 5, :], st[:, 5, :], -0.5, 1.5, ALU.mult, ALU.add))
                link(v.tensor_tensor(st[:, 4, :], st[:, 4, :], st[:, 5, :], ALU.mult))
                for t0, t1 in PARTS:
                    v.tensor_tensor(xn[:, t0:t1, :], xn[:, t0:t1, :], bc(st[:, 4, t0:t1], C), ALU.mult
                                    ).then_inc(s["xn_ready"], 1)
                v.wait_ge(s["xn_ready"], turn(s["xn_ready"], NP))

            def gained(dst, src, kind, op):
                for k in range(NV):
                    if k % 3 == 0:
                        v.wait_ge(s["gain_ps"], turn(s["gain_ps"]))
                    t0, t1 = gain_view(k)
                    g = PB[GAIN_BANKS[kind][k // 3]][:, (k % 3) * P:(k % 3 + 1) * P]
                    g = g.unsqueeze(1).broadcast_to([P, t1 - t0, P])
                    d = dst[:, 2 * t0:2 * t1, :].rearrange("p (t q) c -> p t (q c)", q=2)
                    r = src[:, 2 * t0:2 * t1, :].rearrange("p (t q) c -> p t (q c)", q=2)
                    ins = v.tensor_tensor(d, r, g, op)
                link(ins)

            def apply_gate(xh):
                v.wait_ge(s["gate_ready"], turn(s["gate_ready"]))
                v.tensor_copy(gx[:, 0:QS * C].rearrange("p (k c) -> p k c", c=C), bc(gate[:, :], C)).then_inc(s["gate_wide"], 1)
                gained(tmp, xn, 0, ALU.mult)
                v.tensor_tensor(xh[:, :, :], xh[:, :, :], tmp[:, :, :], ALU.add).then_inc(s["applied"], 1)
                v.wait_ge(s["applied"], turn(s["applied"]))

            def conv0(xh, h):
                shared = xn[:, :, :].rearrange("p (m t) c -> p m t c", m=2)[:, :, 8:10, :]
                for m in range(2):
                    ins = v.tensor_scalar(mx[:, m, :, :].rearrange("p (m t) c -> p m t c", m=2), shared,
                                          kc("mask")[:, m:m + 1], None, ALU.mult)
                ins.then_inc(s["mixed_ready"], 1)
                v.wait_ge(s["sums_ps"], turn(s["sums_ps"]))
                link(v.tensor_copy(srow[:, 0, :], PB[0][0:1, 0:HB * C]))
                v.tensor_scalar(srow[:, 1, :], srow[:, 0, :], -1.0 / PIX, None, ALU.mult).then_inc(s["rows_ready"], 1)
                v.wait_ge(s["cov_ps"], turn(s["cov_ps"]))
                cov = PB[1][:, 0:QS * C].rearrange("p (s c) -> p s c", s=QS)
                link(v.tensor_tensor(nsW[:, :, :], cov, bt(kc("i2"), QS), ALU.mult))
                v.tensor_reduce(sm[:, 0:4], nsW[:, :, :], AX.X, ALU.add).then_inc(s["diag_ready"], 1)
                v.wait_ge(s["tr_ps"], turn(s["tr_ps"]))
                link(v.tensor_copy(sm[:, 0:4], PB[2][:, 0:QS]))
                link(v.reciprocal(sm[:, 4:8], sm[:, 0:4]))
                v.tensor_scalar(sm[:, 8:12], sm[:, 0:4], 1.0 / PIX, None, ALU.mult).then_inc(s["normv_ready"], 1)
                link(v.tensor_tensor(nsA[:, :, :], cov, bc(sm[:, 4:8], C), ALU.mult))
                v.scalar_tensor_tensor(nsZ[:, :, :], nsA[:, :, :], -0.5, bt(i15[:, :], QS), ALU.mult, ALU.add
                                       ).then_inc(s["ns_ready"], 1)
                yp, wp, zp = (PB[b][:, 0:QS * C].rearrange("p (s c) -> p s c", s=QS) for b in (3, 4, 5))
                v.wait_ge(s["ns_ps"], turn(s["ns_ps"]))
                v.tensor_copy(nsY[:, :, :], yp).then_inc(s["ns_ready"], 1)
                for it in range(4):
                    v.wait_ge(s["ns_ps"], turn(s["ns_ps"]))
                    v.scalar_tensor_tensor(nsW[:, :, :], wp, -0.5, bt(i15[:, :], QS), ALU.mult, ALU.add
                                           ).then_inc(s["ns_ready"], 1)
                    v.wait_ge(s["ns_ps"], turn(s["ns_ps"]))
                    if it < 3:
                        v.tensor_copy(nsZ[:, :, :], zp)
                    v.tensor_copy(nsY[:, :, :], yp).then_inc(s["ns_ready"], 1)
                v.wait_ge(s["norm_root"], turn(s["norm_root"]))
                link(v.reciprocal(sm[:, 16:20], sm[:, 12:16]))
                link(v.tensor_tensor(sm[:, 16:20], sm[:, 16:20], sm[:, 8:12], ALU.mult))
                link(v.tensor_tensor(sm[:, 16:20], sm[:, 16:20], sm[:, 12:16], ALU.add))
                v.wait_ge(s["col_ps"], turn(s["col_ps"]))
                v.scalar_tensor_tensor(sm[:, 20:24], PB[2][:, 0:QS], 0.5 / C, sm[:, 16:20], ALU.mult, ALU.mult
                                       ).then_inc(s["v_ready"], 1)
                apply_gate(xh)

            def conv1(xh, h):
                v.wait_ge(s["pool_ps"], turn(s["pool_ps"]))
                v.tensor_scalar(sm[:, 20:24], PB[0][:, 0:QS], 1.0 / PIX, None, ALU.mult).then_inc(s["v_ready"], 1)
                v.wait_ge(s["out4_ready"], turn(s["out4_ready"]))
                link(v.tensor_scalar(par[:, :, :], par[:, :, :], 2.0, -1.0, ALU.mult, ALU.add))
                link(v.tensor_scalar(par[:, 1:4:2, :], par[:, 1:4:2, :], 0.5, None, ALU.mult))
                link(v.tensor_scalar(par[:, 0:2, :], par[:, 0:2, :], 1.0, None, ALU.add))
                v.tensor_copy(gx[:, :].rearrange("p (k c) -> p k c", c=C),
                              bc(par[:, :, :].rearrange("p k s -> p (k s)"), C)).then_inc(s["par_ready"], 1)
                gained(tmp, xn, 0, ALU.mult)
                gained(tmp, tmp, 1, ALU.add)
                gained(xn, xn, 2, ALU.mult)
                gained(xn, xn, 3, ALU.add)
                link(v.tensor_tensor(tmp[:, :, :], tmp[:, :, :], xn[:, :, :], ALU.max))
                v.tensor_tensor(xh[:, :, :], xh[:, :, :], tmp[:, :, :], ALU.add).then_inc(s["applied"], 1)
                v.wait_ge(s["applied"], turn(s["applied"]))

            def conv2(xh, h):
                v.wait_ge(s["band_ps"], turn(s["band_ps"]))
                ori = sm[:, 0:16]
                v.tensor_scalar(ori, PB[0][:, 0:16], 2.0 / PIX, None, ALU.mult).then_inc(s["band_ready"], 1)
                v.wait_ge(s["z_ready"], turn(s["z_ready"]))

                def sk(c):
                    return sm[:, c:c + 16].rearrange("p (s k) -> p s k", k=4)
                link(v.tensor_reduce(sm[:, 32:36], sk(16), AX.X, ALU.max))
                link(v.tensor_tensor(sk(36), sk(16), bc(sm[:, 32:36], 4), ALU.is_equal))
                link(v.tensor_tensor(sk(36), sk(36), bt(kc("k4"), QS), ALU.mult))
                link(v.tensor_reduce(sm[:, 32:36], sk(36), AX.X, ALU.max))
                link(v.tensor_tensor(sk(36), sk(36), bc(sm[:, 32:36], 4), ALU.is_equal))
                link(v.tensor_tensor(sk(36), sk(36), sk(0), ALU.mult))
                link(v.tensor_reduce(sm[:, 32:36], sk(36), AX.X, ALU.add))
                link(v.tensor_tensor(sk(36), sk(0), bc(sm[:, 32:36], 4), ALU.subtract))
                link(v.tensor_scalar(sm[:, 36:52], sm[:, 36:52], 0.0, None, ALU.max))
                v.tensor_reduce(sm[:, 20:24], sk(36), AX.X, ALU.add).then_inc(s["v_ready"], 1)
                apply_gate(xh)

            t_seen = [0]

            def t_count(k):
                t_seen[0] += k
                return t_seen[0]

            def tr_out(dst_flat):
                for b, (j0, j1) in enumerate(TB):
                    v.wait_ge(s["t_ps"], turn(s["t_ps"]))
                    v.tensor_copy(dst_flat[:, j0 * P:j1 * P], PB[b][:, 0:(j1 - j0) * P]).then_inc(s["t_done"], 1)

            def conv3(xh, h):
                flat = tmp[:, :, :].rearrange("p t c -> p (t c)")
                if h == 0:
                    link(v.memset(pad, 0.0))
                tr_out(flat)
                v.wait_ge(s["t_done"], t_count(len(TB)))
                link(v.tensor_copy(pad[:, :, 1:1 + HW, 1:1 + HW],
                                   flat.rearrange("p (s a b) -> p s a b", s=QS, a=HW)))
                img = flat.rearrange("p (s a b) -> p s a b", s=QS, a=HW)
                for smp in range(QS):
                    for tap in range(9):
                        dy, dx = divmod(tap, 3)
                        win = pad[:, smp, dy:dy + HW, dx:dx + HW]
                        w = sc("c3w")[:, tap:tap + 1]
                        if tap == 0:
                            ins = v.tensor_scalar(img[:, smp], win, w, sc("c3b"), ALU.mult, ALU.add)
                        else:
                            ins = v.scalar_tensor_tensor(img[:, smp], win, w, img[:, smp], ALU.mult, ALU.add)
                        if smp < QS - 1 or tap < 8:
                            link(ins)
                ins.then_inc(s["conv_done"], 1)
                for b, (j0, j1) in enumerate(TB):
                    v.wait_ge(s["res_ps"], turn(s["res_ps"]))
                    xv = xh[:, 2 * j0:2 * j1, :].rearrange("p t c -> p (t c)")
                    pv = PB[b][:, 0:(j1 - j0) * P]
                    ins = v.tensor_tensor(xv, xv, pv, ALU.add)
                ins.then_inc(s["applied"], 1)
                v.wait_ge(s["applied"], turn(s["applied"]))

            def top(src, mask, m):
                link(v.tensor_tensor(eq[:, :, :], src, bc(m, E), ALU.is_equal))
                link(v.tensor_tensor(eq[:, :, :], eq[:, :, :], bt(kc("e8"), NT), ALU.mult))
                link(v.tensor_reduce(st[:, 7, :], eq[:, :, :], AX.X, ALU.max))
                link(v.tensor_tensor(mask[:, :, :], eq[:, :, :], bc(st[:, 7, :], E), ALU.is_equal))

            def route(l, h):
                flat = tmp[:, :, :].rearrange("p t c -> p (t c)")
                tr_out(flat)
                t_count(len(TB))
                v.wait_ge(s["split_hi"], turn(s["split_hi"], NP))
                v.tensor_tensor(rowsb[h][:, :, C:2 * C], xn[:, :, :], rowsb[h][:, :, 0:C], ALU.subtract)
                v.wait_ge(s["logits_ps"], turn(s["logits_ps"]))
                src = PB[5][:, 0:QT * 16].rearrange("p (t e) -> p t e", e=E)
                if l < 2:
                    link(v.tensor_tensor(lg[:, :, :], src, bt(sc(f"rb{l}"), NT), ALU.add))
                else:
                    link(v.tensor_copy(lg[:, :, :], src))
                m1, m2 = st[:, 0, :], st[:, 1, :]
                link(v.tensor_reduce(m1, lg[:, :, :], AX.X, ALU.max))
                top(lg[:, :, :], k1, m1)
                exv = ex[:, 0:NT * E].rearrange("p (t e) -> p t e", e=E)
                link(v.tensor_tensor(exv, lg[:, :, :], bc(m1, E), ALU.subtract))
                link(v.scalar_tensor_tensor(lg[:, :, :], k1[:, :, :], -BIG, lg[:, :, :], ALU.mult, ALU.add))
                link(v.tensor_reduce(m2, lg[:, :, :], AX.X, ALU.max))
                v.tensor_tensor(ex[:, NT * E:], m2, m1, ALU.subtract).then_inc(s["logit_shift"], 1)
                top(lg[:, :, :], k2, m2)
                v.tensor_tensor(mt[:, :].rearrange("p (e t) -> p t e", e=E), k1[:, :, :], k2[:, :, :], ALU.add
                                ).then_inc(s["onehot_ready"], 1)
                v.wait_ge(s["exp_ready"], turn(s["exp_ready"]))
                link(v.tensor_reduce(st[:, 2, :], exv, AX.X, ALU.add))
                link(v.reciprocal(gts[h][:, 0, :], st[:, 2, :]))
                link(v.tensor_tensor(gts[h][:, 1, :], gts[h][:, 0, :], ex[:, NT * E:], ALU.mult))
                if l > 0:
                    link(v.tensor_tensor(st[:, 2, :], gts[h][:, 0, :], gts[h][:, 1, :], ALU.add))
                    if l > 1:
                        link(v.tensor_scalar(st[:, 2, :], st[:, 2, :], 1e-9, None, ALU.add))
                    link(v.reciprocal(st[:, 3, :], st[:, 2, :]))
                    link(v.tensor_tensor(gts[h][:, :, :], gts[h][:, :, :], bt(st[:, 3, :], TOPK), ALU.mult))
                link(v.tensor_copy(gate_column(h), gts[h][:, 0, :]))
                v.wait_ge(s["rank_ps"], turn(s["rank_ps"]))
                rank = PB[6][:, 0:E * NT].rearrange("p (e t) -> p e t", e=E)
                cnt = PB[7][:, 0:E * NT].rearrange("p (e t) -> p e t", e=E)
                one = onef[:, 0:1]
                inf = incl[:, :, :].rearrange("p e t -> p (e t)")
                link(v.tensor_tensor_scan(inf, one.broadcast_to([P, E * NT]), PB[7][:, 0:E * NT], 0.0, ALU.mult, ALU.add))
                link(v.tensor_tensor(incl[:, :, :], incl[:, :, :], cnt, ALU.subtract))
                link(v.tensor_tensor(incl[:, :, :], incl[:, :, :], rank, ALU.add))
                link(v.tensor_reduce(r8[:, 0, :], cnt, AX.X, ALU.add))
                cv = cmp_.rearrange("p (e k) -> p e k", e=E)
                link(v.tensor_tensor(cv, bc(r8[:, 0, :], MAXE), bt(kc("thr"), E), ALU.is_gt))
                link(v.tensor_reduce(r8[:, 1, :], cv, AX.X, ALU.add))
                link(v.tensor_tensor_scan(r8[:, 2, :], one.broadcast_to([P, E]), r8[:, 1, :], 0.0, ALU.mult, ALU.add))
                link(v.tensor_tensor_scan(r8[:, 3, :], one.broadcast_to([P, E]), r8[:, 0, :], 0.0, ALU.mult, ALU.add))
                link(v.tensor_tensor(r8[:, 4, :], r8[:, 2, :], r8[:, 1, :], ALU.subtract))
                link(v.tensor_tensor(r8[:, 5, :], r8[:, 0, :], r8[:, 3, :], ALU.subtract))
                link(v.scalar_tensor_tensor(r8[:, 5, :], r8[:, 4, :], float(ROWS), r8[:, 5, :], ALU.mult, ALU.add))
                link(v.tensor_tensor(incl[:, :, :], incl[:, :, :], bc(r8[:, 5, :], NT), ALU.add))
                pv = incl[:, :, :].rearrange("p e t -> p t e")
                for k, m in enumerate((k1, k2)):
                    link(v.tensor_tensor(eq[:, :, :], m[:, :, :], pv, ALU.mult))
                    link(v.tensor_reduce(st[:, 2, :], eq[:, :, :], AX.X, ALU.add))
                    ins = v.tensor_copy(pos[h][:, k, :], st[:, 2, :])
                    if k == 0:
                        link(ins)
                ins.then_inc(s["pos_ready"], 1)
                v.wait_ge(s["pos_ready"], n_of(l, h) + 1)
                ev = eidf.rearrange("p (t e) -> p t e", e=E)
                link(v.tensor_tensor(ev, bt(r8[0:1, 2, :], NEID), bc(kc("tile", 1), E), ALU.is_le))
                link(v.tensor_reduce(eidr, ev, AX.X, ALU.add))
                link(v.tensor_scalar(eidr, eidr, float(E - 1), None, ALU.min))
                link(v.tensor_copy(eidw, eidr[:, WORD - 1::UNROLL]))
                for k in reversed(range(WORD - 1)):
                    link(v.scalar_tensor_tensor(eidw, eidw, float(E), eidr[:, k:k + TILES - UNROLL + 1:UNROLL], ALU.mult, ALU.add))
                v.tensor_copy(eid[h][:, :], eidw).then_inc(s["route_ready"], 1)

            def prep(l, h):
                ln(x[h], EPS_C, n_of(l - 1, h) if l > 0 else None)
                (conv0, conv1, conv2, conv3)[l](x[h], h)
                if n_of(l, h) == 0:
                    v.wait_ge(s["table_zero"], 16 * NZERO)
                ln(x[h], EPS_T)
                route(l, h)

            def wprep():
                for k in range(2):
                    for b in range(12):
                        v.wait_ge(s["w_hi"], turn(s["w_hi"]))
                        hi = (gA, uA)[k][:, b * 4 * CH:(b + 1) * 4 * CH]
                        lo = (gB, uB)[k][:, b * 4 * CH:(b + 1) * 4 * CH]
                        v.scalar_tensor_tensor(lo, PB[b % 4][:, 0:4 * CH], WSCALE, hi, ALU.mult, ALU.subtract
                                               ).then_inc(s["w_lo"], 1)
                for k in range(2):
                    for b in range(2):
                        v.wait_ge(s["w_hi"], turn(s["w_hi"]))
                        at = slice((2 * k + b) * 8, (2 * k + b + 1) * 8)
                        v.scalar_tensor_tensor(dV[:, at, 1, :], PB[4 + (3 * k + b) % 2][0:CH, :].rearrange(
                            "p (k c) -> p k c", c=C), WSCALE, dV[:, at, 0, :], ALU.mult, ALU.subtract).then_inc(s["w_lo"], 1)
                    v.wait_ge(s["wt_ps"], turn(s["wt_ps"], 27 if k == 0 else 3))
                    v.tensor_scalar(dF[:, k * 512:(k + 1) * 512], PB[4 + (3 * k + 2) % 2][0:CH, :], WSCALE, None, ALU.mult
                                    ).then_inc(s["w_lo"], 1)
                v.wait_ge(s["w_lo"], turn(s["w_lo"], 30))
                last = dF[0:OVERLAP, :].rearrange("p (e k c) -> p e k c", e=E, k=NFU)[:, :, NFU - 1, :]
                v.memset(last, 0.0).then_inc(s["w_lo"], 1)
                turn(s["w_lo"])

            def moe(l, h):
                n, tb, gb = n_of(l, h), tile_base(l, h), group_base(l, h)

                def evict(i, k, e=None):
                    t = i * UNROLL + (tb + k)
                    v.wait_ge(s["y_grp"], i * (UNROLL * G[l]) + (gb + (k + 1) * G[l]))
                    wait_from(v, y_st[k], i * 16 + 16 * LOOPS * n)
                    wait_from(v, s["y_done"], t - 1)
                    y = yb[k % 2][:, :].rearrange("p (u c) -> p u c", u=SUB)
                    if l < 2:
                        src = PB[4 + k % 2][:, 0:SUB * C].rearrange("p (u c) -> p u c", u=SUB)
                        ins = v.tensor_tensor(y, src, bt(b2R[l][:, ds(e * C, C)], SUB), ALU.add)
                    else:
                        src = PB[4 + k % 2][:, 0:SUB * 2 * C].rearrange("p (u s c) -> p u c s", u=SUB, s=2)
                        ins = v.tensor_reduce(y, src, AX.X, ALU.add)
                    ins.then_inc(s["b_done"], 1)
                    v.wait_ge(s["b_done"], t + 4)
                    v.tensor_tensor(ysb[k][:, :].rearrange("p (u c) -> p u c", u=SUB), y, bc(gt[k][:, :], C), ALU.mult
                                    ).then_inc(s["y_done"], 1)

                def take(i, k, t):
                    r = (k + t) % UNROLL
                    v.wait_ge(s["xT_ps"], i * UNROLL + (tb + k + t + 1))
                    gv = xs[r][:, :].bitcast(FP32).rearrange("p (s c) -> p s c", s=SUB)[:, :, RW // 2 - 1]
                    if t == UNROLL - 1:
                        wait_from(v, s["y_done"], i * UNROLL + (tb + k))
                    v.tensor_scalar(gt[r][:, :], gv, 1.0 / WSCALE, None, ALU.mult)
                    v.tensor_copy(xT[r][:, :], PB[6 + r % 2][:, :].bitcast(FP16)[:, 0:ROWS]).then_inc(s["xT_done"], 1)

                def split(i, k):
                    v.wait_ge(s["gelu_ready"], i * UNROLL + (gb + k + 1))
                    w = (l + 1) * ROWS
                    p = hid_hl[k]
                    v.tensor_tensor(p[:, 2 * ROWS:2 * ROWS + w], hid[k % 2][:, 0:w], p[:, 0:w], ALU.subtract
                                    ).then_inc(s["hp_ready"], 1)

                def body01(i, last=False, first=False):
                    es = experts(v, h, i, range(0 if first else -1, UNROLL if last else UNROLL - 1))
                    for k in range(UNROLL):
                        split(i, k)
                        if k > 0:
                            evict(i, k - 1, es[k - 1])
                        elif not first:
                            evict(i - 1, UNROLL - 1, es[-1])
                        if not (last and k + AHEAD >= UNROLL):
                            take(i, k, AHEAD)
                    if last:
                        evict(i, UNROLL - 1, es[UNROLL - 1])

                g0, sb_ = group_base(2, 0), split_base(l, h)

                def product(i, k, g):
                    q = k * G[l] + g
                    p = hold(k, g)[0:CH, :]
                    v.wait_ge(s["s_ready"], i * (UNROLL * G[l]) + (gb + q + 1 - g0))
                    v.tensor_tensor(p, PB[2 + q % 2][0:CH, :], p, ALU.mult).then_inc(s["prod_ready"], 1)

                def low(i, k, g):
                    v.wait_ge(s["hi_ready"], i * (UNROLL * SPLIT) + (sb_ + k * SPLIT + g + 1))
                    v.tensor_tensor(hl[g][0:CH, 2 * ROWS:4 * ROWS], hold(k, g)[0:CH, :], hl[g][0:CH, 0:2 * ROWS], ALU.subtract
                                    ).then_inc(s["hp_ready"], 1)

                def body23(i, first=False):
                    for k in range(UNROLL):
                        for g in range(G[l]):
                            product(i, k, g)
                            if g > 0:
                                low(i, k, g - 1)
                            elif k >= 2:
                                evict(i, k - 2)
                            elif not first:
                                evict(i - 1, k + UNROLL - 2)
                if l < 2:
                    for k in range(AHEAD):
                        take(0, k, 0)
                    body01(0, first=True)
                    middle(v, body01)
                    body01(LOOPS - 1, last=True)
                else:
                    body23(0, first=True)
                    middle(v, body23)
                    body23(LOOPS - 1)
                    evict(LOOPS - 1, UNROLL - 2)
                    evict(LOOPS - 1, UNROLL - 1)

            def first_weights():
                v.wait_ge(s["b_ps"], 1)
                v.tensor_copy(b1T[0][:, :], PB[5][:, 0:E])
                link(v.tensor_copy(b1T[1][:, :], PB[5][:, 64:64 + 2 * E]))
                v.tensor_copy(lnT[:, :], PB[5][:, 128:128 + 2 * E]).then_inc(s["b_done"], 1)
                v.wait_ge(s["b_done"], 1)
                v.wait_ge(s["l1b_ps"], 1)
                v.tensor_tensor(b1T[1][:, :], b1T[1][:, :], PB[6][:, 0:2 * E], ALU.add).then_inc(s["b_done"], 1)
                for e in range(E):
                    ins = v.tensor_scalar(stage[1][:, e * H1:(e + 1) * H1], stage[1][:, e * H1:(e + 1) * H1], lnT[:, e:e + 1],
                                          None, ALU.mult)
                ins.then_inc(s["w01_done"], 1)
                for l, w in ((0, H0), (1, H1)):
                    v.wait_ge(s["w_hi"], turn(s["w_hi"]))
                    link(v.scalar_tensor_tensor(wB[l][:, :], stage[l][:, 0:E * w], WSCALE, wA[l][:, :], ALU.mult, ALU.subtract))
                v.wait_ge(s["b_ld"], 16 * 10)
                for l in (0, 1):
                    v.wait_ge(s["w_hi"], turn(s["w_hi"]))
                    wv = wD[l][:, :].rearrange("p (k s c) -> p k s c", s=2, c=C)
                    v.scalar_tensor_tensor(wv[:, :, 1, :], w2_in[l].rearrange("p (k c) -> p k c", c=C), WSCALE, wv[:, :, 0, :],
                                           ALU.mult, ALU.subtract).then_inc(s["stage_used"], 1)
                    v.tensor_scalar(b2R[l][:, :], b2R[l][:, :], WSCALE, None, ALU.mult)
                v.wait_ge(s["small_ld"], SMALL)
                v.tensor_scalar(wencb[:, :], kc("blk"), sc("c2we"), None, ALU.mult).then_inc(s["b_done"], 1)

            v.wait_ge(s["const_ld"], 16)
            v.tensor_copy(id16[:, :], ident)
            v.tensor_copy(tri16[:, :], kc("tri"))
            v.memset(one16[:, :], 1.0)
            v.tensor_scalar(i15[:, :], kc("i2"), 1.5, None, ALU.mult).then_inc(s["consts_done"], 1)
            for h in range(HALVES):
                for b, (j0, j1) in enumerate(TB):
                    v.wait_ge(s["xin_ps"], turn(s["xin_ps"]))
                    xv = x[h][:, 2 * j0:2 * j1, :].rearrange("p t c -> p (t c)")
                    v.tensor_copy(xv, PB[b][:, 0:(j1 - j0) * P]).then_inc(s["xin_done"], 1)
            v.wait_ge(s["xin_done"], turn(s["xin_done"], HALVES * len(TB)))
            v.wait_ge(s["rows_zero"], 2)
            v.wait_ge(s["consts_done"], 1)
            for l in range(NL):
                for h in range(HALVES):
                    prep(l, h)
                    if l == 0 and h == 0:
                        first_weights()
                if l == 3:
                    wprep()
                for h in range(HALVES):
                    moe(l, h)
                if l == 0:
                    wprep()
            for h in range(HALVES):
                flat = (xn, tmp)[h][:, :, :].rearrange("p t c -> p (t c)")
                tr_out(flat)

        @block.tensor
        def _(pe):
            turn = Turn()

            def wait_part(n, norm, j):
                for p, (t0, _) in enumerate(PARTS):
                    if 2 * j == t0:
                        pe.wait_ge(s["xn_ready"], NP * (2 * n + norm) + p + 1)

            def transposes(src, sem_ps, n=None, norm=0, last=None):
                for b, (j0, j1) in enumerate(TB):
                    if n is not None:
                        wait_part(n, norm, j0)
                    for p, (t0, t1) in enumerate(PARTS):
                        if last is not None and 2 * j0 == t0:
                            pe.wait_ge(second_added[p], 16 * (t1 - t0) * (last + 1))
                    for j in range(j0, j1):
                        ins = pe.transpose(PB[b][:, (j - j0) * P:(j - j0 + 1) * P], src(j), ident)
                    ins.then_inc(sem_ps, 1)

            def conv0(n):
                pe.wait_ge(s["mixed_ready"], turn(s["mixed_ready"]))
                for smp in range(HB):
                    ops = pieces(*divmod(smp, QS))
                    for i, o in enumerate(ops):
                        ins = pe.matmul(PB[0][0:1, smp * C:(smp + 1) * C], onef[:, 0:1], o, start=(i == 0), stop=(i == 4))
                ins.then_inc(s["sums_ps"], 1)
                for smp in range(HB):
                    q, s4 = divmod(smp, QS)
                    ops = pieces(q, s4)
                    for i, o in enumerate(ops):
                        pe.matmul(PB[1][q * C:(q + 1) * C, s4 * C:(s4 + 1) * C], o, o, start=(i == 0 and s4 == 0),
                                  stop=False, skip_group_check=True)
                pe.wait_ge(s["rows_ready"], turn(s["rows_ready"]))
                for smp in range(HB):
                    q, s4 = divmod(smp, QS)
                    ins = pe.matmul(PB[1][q * C:(q + 1) * C, s4 * C:(s4 + 1) * C], srow[0:1, 1, smp * C:(smp + 1) * C],
                                    srow[0:1, 0, smp * C:(smp + 1) * C], start=False, stop=True, skip_group_check=True)
                ins.then_inc(s["cov_ps"], 1)
                pe.wait_ge(s["diag_ready"], turn(s["diag_ready"]))
                pe.matmul(PB[2][:, 0:QS], kc("blk"), sm[:, 0:4], start=True, stop=True).then_inc(s["tr_ps"], 1)

                def product(bank, a_, b_):
                    for s4 in range(QS):
                        for q in range(2):
                            r = slice(q * C, (q + 1) * C)
                            ins = pe.matmul(PB[bank][r, s4 * C:(s4 + 1) * C], a_[r, s4, :], b_[r, s4, :], start=True, stop=True)
                    return ins
                pe.wait_ge(s["ns_ready"], turn(s["ns_ready"]))
                product(3, nsA, nsZ).then_inc(s["ns_ps"], 1)
                for it in range(4):
                    pe.wait_ge(s["ns_ready"], turn(s["ns_ready"]))
                    product(4, nsZ, nsY).then_inc(s["ns_ps"], 1)
                    pe.wait_ge(s["ns_ready"], turn(s["ns_ready"]))
                    if it < 3:
                        product(5, nsW, nsZ)
                    product(3, nsY, nsW).then_inc(s["ns_ps"], 1)
                pe.wait_ge(s["ns_ready"], turn(s["ns_ready"]))
                for s4 in range(QS):
                    for q in range(2):
                        r = slice(q * C, (q + 1) * C)
                        ins = pe.matmul(PB[2][r, s4:s4 + 1], nsY[r, s4, :], onef[r, 0:1], start=True, stop=True)
                ins.then_inc(s["col_ps"], 1)
                if n == 0:
                    pe.wait_ge(s["small_ld"], SMALL)
                gate_tail("c0", 16)

            def hidden(c, hr):
                pe.wait_ge(s["v_ready"], turn(s["v_ready"]))
                pe.matmul(PB[4][0:hr, 0:QS], sc(f"{c}w1"), sm[:, 20:24], start=True, stop=True).then_inc(s["hid_ps"], 1)
                pe.wait_ge(s["hid_ready"], turn(s["hid_ready"]))

            def spread(src, kind):
                for k in range(NV):
                    m, part = divmod(k, 3)
                    if part == 1:
                        at = (kind * QS + 2 * m) * C
                        lhs = gx[:, at:at + P]
                    else:
                        c = 2 * m + part // 2
                        lhs = src[:, c:c + 1].broadcast_to([P, P])
                    ins = pe.matmul(PB[GAIN_BANKS[kind][m]][:, part * P:(part + 1) * P], lhs, ident, start=True, stop=True)
                    if part == 2:
                        ins.then_inc(s["gain_ps"], 1)

            def gate_tail(c, hr):
                hidden(c, hr)
                pe.matmul(PB[5][:, 0:QS], sc(f"{c}w2", 0, hr), mid[0:hr, :], start=True, stop=True).then_inc(s["gate_ps"], 1)
                pe.wait_ge(s["gate_wide"], turn(s["gate_wide"]))
                spread(gate, 0)

            def sums(n, cols, w):
                for j in range(QT):
                    wait_part(n, 0, j)
                    ins = pe.matmul(PB[0][:, 0:w], pair(xn, j), kc(cols)[:, j * w:(j + 1) * w], start=(j == 0), stop=(j == QT - 1))
                return ins

            def conv1(n):
                sums(n, "ind", QS).then_inc(s["pool_ps"], 1)
                hidden("c1", 16)
                for k in range(4):
                    ins = pe.matmul(PB[5][:, k * QS:(k + 1) * QS], sc("c1w2", 0, 16)[:, k * P:(k + 1) * P], mid[0:16, :],
                                    start=True, stop=True)
                ins.then_inc(s["out4_ps"], 1)
                pe.wait_ge(s["par_ready"], turn(s["par_ready"]))
                for k in range(4):
                    spread(par[:, k, :], k)

            def conv2(n):
                sums(n, "haar", QS * 4).then_inc(s["band_ps"], 1)
                pe.wait_ge(s["band_ready"], turn(s["band_ready"]))
                pe.matmul(PB[1][:, 0:16], wencb[:, :], sm[:, 0:16], start=True, stop=True).then_inc(s["z_ps"], 1)
                gate_tail("c2", C)

            def conv3(n):
                transposes(lambda j: pair(xn, j), s["t_ps"], n, 0)
                pe.wait_ge(s["t_done"], turn(s["t_done"], len(TB)))
                pe.wait_ge(s["conv_done"], turn(s["conv_done"]))
                flat = tmp[:, :, :].rearrange("p t c -> p (t c)")
                transposes(lambda j: flat[:, j * P:(j + 1) * P], s["res_ps"])

            def route(l, h):
                pe.wait_ge(s["applied"], n_of(l, h) + 1)
                transposes(lambda j: pair(xn, j), s["t_ps"], n_of(l, h), 1)
                flat = tmp[:, :, :].rearrange("p t c -> p (t c)")
                for b, (j0, j1) in enumerate(TB):
                    pe.wait_ge(s["t_done"], turn(s["t_done"]))
                    for j in range(j0, j1):
                        ins = pe.matmul(PB[5][:, j * 16:(j + 1) * 16], flat[:, j * P:(j + 1) * P], sc(f"r{l}"),
                                        start=True, stop=True)
                ins.then_inc(s["logits_ps"], 1)
                pe.wait_ge(s["onehot_ready"], turn(s["onehot_ready"]))
                pe.matmul(PB[6][:, 0:E * NT], tri16[:, :], mt[:, :], start=True, stop=True)
                pe.matmul(PB[7][:, 0:E * NT], one16[:, :], mt[:, :], start=True, stop=True).then_inc(s["rank_ps"], 1)

            def prep(l, h):
                n = n_of(l, h)
                if n > 0:
                    pe.wait_ge(s["route_ready"], n)
                if l == 0:
                    pe.wait_ge(s["xn_ready"], NP * (2 * n + 1))
                (conv0, conv1, conv2, conv3)[l](n)
                route(l, h)

            stage_n = [2, 2]

            def wprep(l):
                lo = turn(s["w_lo"], 0)
                pe.wait_ge(s["y_done"], tile_base(1, 0) if l == 0 else tile_base(l, 0))
                for k in range(4):
                    stage_n[k % 2] += 2 * NCH
                    pe.wait_ge(s[f"stage_ld{k % 2}"], 16 * stage_n[k % 2])
                    vv = stage[k % 2][0:CH, :].rearrange("p (k e m) -> p e k m", k=NCH, e=4)
                    for b in range(6):
                        n = 6 * k + b
                        if n >= 4:
                            pe.wait_ge(s["w_lo"], lo + n - 3)
                        for i in range(4):
                            e, c = divmod(4 * b + i, NCH)
                            ins = pe.matmul(PB[n % 4][:, i * CH:(i + 1) * CH], vv[:, e, c, :], ident[0:CH, 0:CH],
                                            start=True, stop=True)
                        ins.then_inc(s["wt_ps"], 1)
                for k in range(2):
                    stage_n[k] += 1
                    pe.wait_ge(s[f"stage_ld{k}"], 16 * stage_n[k])
                    for b in range(3):
                        n = 3 * k + b
                        if n >= 2:
                            pe.wait_ge(s["w_lo"], lo + 24 + n - 1)
                        for i in range(8):
                            e, c = divmod(8 * b + i, NSP) if b < 2 else (i // NFU, NSP + i % NFU)
                            src = stage[k][0:C, e * H2 + CH_AT[c]:e * H2 + CH_AT[c] + CH]
                            ins = pe.transpose(PB[4 + n % 2][0:CH, i * C:(i + 1) * C], src, ident[0:C, 0:C])
                        ins.then_inc(s["wt_ps"], 1)
                turn(s["w_lo"], 31)
                pe.wait_ge(s["w_lo"], lo + 31)

            def moe(l, h):
                n, tb, gb = n_of(l, h), tile_base(l, h), group_base(l, h)
                g_ = G[l]
                g0 = group_base(2, 0)
                width = (H0, H1)[l] if l < 2 else 0

                def turn_rows(i, k, t):
                    r = (k + t) % UNROLL
                    pe.wait_ge(xs_ld[r], i * 16 + 16 * (LOOPS * n + 1 + (k + t) // UNROLL))
                    if t == 0 or (l >= 2 and isinstance(i, int)):
                        wait_from(pe, s["xT_done"], i * UNROLL + (tb + k + t - 1))
                    bank = PB[6 + r % 2][:, :].bitcast(FP16)
                    for u in range(SUB):
                        ins = pe.transpose(bank[:, u * P:(u + 1) * P], xs[r][:, u * RW:u * RW + P], id16[:, :])
                    ins.then_inc(s["xT_ps"], 1)

                def up01(i, k, t, e):
                    r = (k + t) % UNROLL
                    pe.wait_ge(s["xT_done"], i * UNROLL + (tb + k + t + 1))
                    for c in range(l + 1):
                        o = slice(c * ROWS, (c + 1) * ROWS)
                        at = ds(e * width + c * P, P)
                        pe.matmul(PB[r][:, o], wA[l][:, at], xT[r][:, :], start=True, stop=False)
                        ins = pe.matmul(PB[r][:, o], wB[l][:, at], xT[r][:, :], start=False, stop=True)
                    ins.then_inc(s["h_ps"], 1)

                def down01(i, k, e):
                    pe.wait_ge(s["hp_ready"], i * UNROLL + (gb + k + 1))
                    y = PB[4 + k % 2]
                    for c in range(l + 1):
                        at = (e * (l + 1) + c) * (2 * C)
                        high, low = wD[l][:, ds(at, C)], wD[l][:, ds(at + C, C)]
                        for part, w in ((0, low), (0, high), (2 * ROWS, high)):
                            for u in range(SUB):
                                col = part + c * ROWS + u * P
                                ins = pe.matmul(y[:, u * C:(u + 1) * C], hid_hl[k][:, col:col + P], w,
                                                start=(c == 0 and u == 0 and w is low), stop=(c == l and part > 0),
                                                skip_group_check=True)
                    ins.then_inc(s["y_grp"], 1)

                def body01(i, last=False):
                    es = experts(pe, h, i, range(UNROLL if last else UNROLL + 2))
                    for k in range(UNROLL):
                        if not (last and k + AHEAD >= UNROLL):
                            turn_rows(i, k, AHEAD)
                        if not (last and k + 2 >= UNROLL):
                            up01(i, k, 2, es[k + 2])
                        down01(i, k, es[k])

                def up23(i, k, g, e):
                    q = k * g_ + g
                    if g == 0:
                        pe.wait_ge(s["xT_done"], i * UNROLL + (tb + k + 1))
                    wait_from(pe, s["prod_ready"], i * (UNROLL * g_) + (gb + q - 1 - group_base(2, 0)))
                    for c in range(2):
                        for w, bank in (((gA, gB), q % 2), ((uA, uB), 2 + q % 2)):
                            o = slice(c * ROWS, (c + 1) * ROWS)
                            at = ds(e * (NCH * CH) + (2 * g + c) * CH, CH)
                            pe.matmul(PB[bank][0:CH, o], w[0][:, at], xT[k][:, :], start=True, stop=False)
                            ins = pe.matmul(PB[bank][0:CH, o], w[1][:, at], xT[k][:, :], start=False, stop=True)
                    ins.then_inc(s["h_ps"], 1)

                def down23(i, k, g, e):
                    if g < SPLIT:
                        pe.wait_ge(s["hp_ready"], i * (UNROLL * SPLIT) + (g0 + split_base(l, h) + k * SPLIT + g + 1))
                    else:
                        pe.wait_ge(s["prod_ready"], i * (UNROLL * g_) + (gb + k * g_ + g + 1 - g0))
                    y = PB[4 + k % 2]
                    for c in range(2):
                        if g < SPLIT:
                            w = dW[:, ds(e * (NSP * 2 * C) + (2 * g + c) * 2 * C, 2 * C)]
                        else:
                            w = dF[:, ds(e * (NFU * C) + (2 * (g - SPLIT) + c) * C, C)]
                        for u in range(SUB):
                            col = c * ROWS + u * P
                            o = u * 2 * C
                            if g < SPLIT:
                                pe.matmul(y[:, o:o + 2 * C], hl[g][0:CH, col:col + P], w,
                                          start=(g == 0 and c == 0 and u == 0), stop=False, skip_group_check=True)
                                ins = pe.matmul(y[:, o:o + C], hl[g][0:CH, 2 * ROWS + col:2 * ROWS + col + P],
                                                w[:, 0:C], start=False, stop=False, skip_group_check=True)
                            else:
                                ins = pe.matmul(y[:, o:o + C], hold(k, g)[0:CH, col:col + P], w,
                                                start=False, stop=(c == 1), skip_group_check=True)
                    ins.then_inc(s["y_grp"], 1)

                def body23(i, first=False, last=False):
                    es = experts(pe, h, i, range(0 if first else -1, UNROLL))
                    for k in range(UNROLL):
                        if not (last and k + 2 >= UNROLL):
                            turn_rows(i, k, 2)
                        for g in range(g_):
                            up23(i, k, g, es[k])
                            if k > 0:
                                down23(i, k - 1, g, es[k - 1])
                            elif not first:
                                down23(i - 1, UNROLL - 1, g, es[-1])
                    if last:
                        for g in range(g_):
                            down23(i, UNROLL - 1, g, es[UNROLL - 1])

                pe.wait_ge(s["route_ready"], 2 * (l + 1))
                if l < 2:
                    for k in range(AHEAD):
                        turn_rows(0, k, 0)
                    es = experts(pe, h, 0, range(2))
                    for k in range(2):
                        up01(0, k, 0, es[k])
                    body01(0)
                    middle(pe, body01)
                    body01(LOOPS - 1, last=True)
                else:
                    turn_rows(0, 0, 0)
                    turn_rows(0, 1, 0)
                    body23(0, first=True)
                    middle(pe, body23)
                    body23(LOOPS - 1, last=True)

            def first_weights():
                pe.wait_ge(s["b_ld"], 16 * 10)
                pe.wait_ge(s["route_ready"], 1)
                pe.transpose(PB[5][:, 0:E], act[0][0:E, 0:P], ident[0:E, 0:E])
                pe.transpose(PB[5][:, 64:64 + 2 * E], act[1][0:2 * E, 0:P], ident[0:2 * E, 0:2 * E])
                pe.transpose(PB[5][:, 128:128 + E], act[0][0:E, P:2 * P], ident[0:E, 0:E])
                pe.transpose(PB[5][:, 128 + E:128 + 2 * E], act[1][0:E, P:2 * P], ident[0:E, 0:E]).then_inc(s["b_ps"], 1)
                pe.wait_ge(s["b_done"], 1)
                pe.wait_ge(s["stage_ld1"], 32)
                for e in range(E):
                    for c in range(2):
                        at = e * H1 + c * P
                        ins = pe.matmul(PB[6][:, 2 * e + c:2 * e + c + 1], stage[1][0:C, at:at + P], lnT[0:C, E + e:E + e + 1],
                                        start=True, stop=True)
                ins.then_inc(s["l1b_ps"], 1)

            pe.wait_ge(s["const_ld"], 16)
            for h in range(HALVES):
                pe.wait_ge(s[f"x_ld{h}"], 32)
                src = (xn, tmp)[h][:, :, :].rearrange("p t c -> p (t c)")
                for b, (j0, j1) in enumerate(TB):
                    if h:
                        pe.wait_ge(s["xin_done"], b + 1)
                    for j in range(j0, j1):
                        ins = pe.transpose(PB[b][:, (j - j0) * P:(j - j0 + 1) * P], src[:, j * P:(j + 1) * P], ident)
                    ins.then_inc(s["xin_ps"], 1)
            for l in range(NL):
                for h in range(HALVES):
                    prep(l, h)
                    if l == 0 and h == 0:
                        first_weights()
                if l == 3:
                    wprep(l)
                for h in range(HALVES):
                    moe(l, h)
                if l == 0:
                    wprep(l)
            pe.wait_ge(s["y_done"], tile_base(NL, 0))
            for h in range(HALVES):
                if h:
                    pe.wait_ge(s["t_done"], turn(s["t_done"], len(TB)))
                transposes(lambda j: pair(x[h], j), s["t_ps"], last=n_of(NL - 1, h))


_NAMES = ["x"] + [f"L0_conv_{n}" for n in ("w1", "b1", "w2", "b2")] + \
    [f"L0_ffn_{n}" for n in ("gate_w", "gate_b", "W1", "b1", "W2", "b2")] + \
    [f"L1_conv_{n}" for n in ("w1", "b1", "w2", "b2")] + \
    [f"L1_ffn_{n}" for n in ("Wr", "br", "ln_g", "ln_b", "W1", "b1", "W2", "b2")] + \
    [f"L2_conv_{n}" for n in ("w1", "w2", "w_enc", "b_enc")] + [f"L2_ffn_{n}" for n in ("router_w", "w1", "w2", "w3")] + \
    ["L3_conv_weight", "L3_conv_bias"] + [f"L3_ffn_{n}" for n in ("router_w", "w1", "w2", "w3")]


def kernel(**inputs):
    import concourse.bacc as bacc
    from concourse.bass_utils import run_bass_kernel_spmd

    nc = bacc.Bacc("TRN2", target_bir_lowering=False, num_devices=1)
    arrays, aps = {}, {}
    for name in _NAMES:
        arr = np.ascontiguousarray(inputs[name])
        arrays[f"in_{name}"] = arr
        aps[name] = nc.dram_tensor(f"in_{name}", arr.shape, mybir.dt.from_np(arr.dtype), kind="ExternalInput").ap()
    k = constants()
    arrays["konst"] = k
    konst = nc.dram_tensor("konst", k.shape, FP32, kind="ExternalInput").ap()
    out = nc.dram_tensor("out", (B, C, HW, HW), FP32, kind="ExternalOutput").ap()
    program(nc, aps, konst, out)
    r = run_bass_kernel_spmd(nc, [arrays], core_ids=[0])
    return r.results[0]["out"]
```
